# Optimizing a Trainium2 kernel written in Bass

```python
import numpy as np
import jax
import jax.numpy as jnp

def _softmax(x, axis=-1):
    return jax.nn.softmax(x, axis=axis)

def _gelu(x):
    return jax.nn.gelu(x, approximate=True)

def _silu(x):
    return jax.nn.silu(x)

def _sigmoid(x):
    return jax.nn.sigmoid(x)

def _layernorm(x, axis=-1, eps=1e-05):
    m = jnp.mean(x, axis=axis, keepdims=True)
    v = jnp.var(x, axis=axis, keepdims=True)
    return (x - m) / jnp.sqrt(v + eps)

def _scatter_add(tgt, idx, src, axis=0):
    return tgt.at[idx].add(src)

def _segment_sum(src, seg, n):
    return jax.ops.segment_sum(src, seg, n)
kernel_name = 'mk_vit_tower_d1_tok_img256_r4_ec7b78'

def setup_inputs(seed: int=0):
    np.random.seed(seed)
    _w = jnp.asarray

    def _rec_inputs():
        import jax
        import jax.numpy as jnp
        _rk = jax.random.key(seed)
        x = -0.000392918 + 0.999932 * jax.random.normal(jax.random.fold_in(_rk, 1), (16, 1, 128, 512), jnp.float32)
        return x
    x = _rec_inputs()

    def _L0_tok_setup():
        import jax, jax.numpy as jnp
        import numpy as np
        PATCH = 8
        EMBED = 64
        N_MELS = 128
        N_FRAMES = 512
        BATCH = 64
        NUM_PATCHES = N_MELS // PATCH * (N_FRAMES // PATCH)
        key = jax.random.key(seed)
        k1, k2, k3, k4 = jax.random.split(key, 4)
        x = jax.random.normal(k1, (BATCH, 1, N_MELS, N_FRAMES), dtype=jnp.float32)
        W = jax.random.normal(k2, (EMBED, PATCH * PATCH), dtype=jnp.float32) * (1.0 / np.sqrt(PATCH * PATCH))
        b = jax.random.normal(k3, (EMBED,), dtype=jnp.float32) * 0.01
        pos_embed = jax.random.normal(k4, (1, NUM_PATCHES, EMBED), dtype=jnp.float32) * 0.02
        return {'x': x, 'W': W, 'b': b, 'pos_embed': pos_embed}
    _L0_tok_all = _L0_tok_setup()
    _L0_tok_in = {k: v for k, v in _L0_tok_all.items() if k in ('W', 'b', 'pos_embed')}
    del _L0_tok_all

    def _L0_attn_setup():
        import jax, jax.numpy as jnp
        import numpy as np
        H = 8
        key = jax.random.key(seed)
        ks = jax.random.split(key, 10)
        B, N, D, E = (1, 1024, 64, 16384)
        s = 0.02
        return {'x': jax.random.normal(ks[0], (B, N, D), jnp.float32), 'edge_index': jax.random.randint(ks[1], (2, E), 0, N, jnp.int32), 'edge_attr': jax.random.normal(ks[2], (E, 3), jnp.float32), 'Wq': jax.random.normal(ks[3], (D, D), jnp.float32) * s, 'bq': jnp.zeros((D,), jnp.float32), 'Wk': jax.random.normal(ks[4], (D, D), jnp.float32) * s, 'bk': jnp.zeros((D,), jnp.float32), 'Wv': jax.random.normal(ks[5], (D, D), jnp.float32) * s, 'bv': jnp.zeros((D,), jnp.float32), 'Wo': jax.random.normal(ks[6], (D, D), jnp.float32) * s, 'bo': jnp.zeros((D,), jnp.float32), 'We': jax.random.normal(ks[7], (3, H), jnp.float32) * s, 'be': jnp.zeros((H,), jnp.float32)}
    _L0_attn_all = _L0_attn_setup()
    _L0_attn_in = {k: v for k, v in _L0_attn_all.items() if k in ('edge_index', 'edge_attr', 'Wq', 'bq', 'Wk', 'bk', 'Wv', 'bv', 'Wo', 'bo', 'We', 'be')}
    del _L0_attn_all

    def _L0_ffn_setup():
        import jax, jax.numpy as jnp
        import numpy as np
        NUM_EXPERTS = 8
        TOP_K = 2
        B, S, D = (8, 2048, 64)

        def _moe(tokens, router_w, w1, b1, w2, b2):
            N = tokens.shape[0]
            E = router_w.shape[0]
            logits = tokens.astype(jnp.float32) @ router_w.astype(jnp.float32).T
            probs = jax.nn.softmax(logits, axis=-1)
            rw, re = jax.lax.top_k(probs, TOP_K)
            if TOP_K > 1:
                rw = rw / jnp.maximum(rw.sum(-1, keepdims=True), 1e-12)
            rw = rw.astype(tokens.dtype)
            combine = jnp.zeros((N, E), tokens.dtype).at[jnp.arange(N)[:, None], re].set(rw)
            out = tokens
            for e in range(E):
                h = jax.nn.gelu(tokens @ w1[e] + b1[e], approximate=False)
                y = h @ w2[e] + b2[e]
                out = out + combine[:, e:e + 1] * y
            return out
        key = jax.random.key(seed)
        ks = jax.random.split(key, 4)
        scale = 1.0 / np.sqrt(D).astype(np.float32)
        return {'input_embeddings': jax.random.normal(ks[0], (B, S, D), jnp.float32), 'router_w': jax.random.normal(ks[1], (NUM_EXPERTS, D), jnp.float32) * scale, 'w1': jax.random.normal(ks[2], (NUM_EXPERTS, D, D), jnp.float32) * scale, 'b1': jnp.zeros((NUM_EXPERTS, D), jnp.float32), 'w2': jax.random.normal(ks[3], (NUM_EXPERTS, D, D), jnp.float32) * scale, 'b2': jnp.zeros((NUM_EXPERTS, D), jnp.float32)}
    _L0_ffn_all = _L0_ffn_setup()
    _L0_ffn_in = {k: v for k, v in _L0_ffn_all.items() if k in ('router_w', 'w1', 'b1', 'w2', 'b2')}
    del _L0_ffn_all
    return {'x': x, 'L0_tok_W': _L0_tok_in['W'], 'L0_tok_b': _L0_tok_in['b'], 'L0_tok_pos_embed': _L0_tok_in['pos_embed'], 'L0_attn_edge_index': _L0_attn_in['edge_index'], 'L0_attn_edge_attr': _L0_attn_in['edge_attr'], 'L0_attn_Wq': _L0_attn_in['Wq'], 'L0_attn_bq': _L0_attn_in['bq'], 'L0_attn_Wk': _L0_attn_in['Wk'], 'L0_attn_bk': _L0_attn_in['bk'], 'L0_attn_Wv': _L0_attn_in['Wv'], 'L0_attn_bv': _L0_attn_in['bv'], 'L0_attn_Wo': _L0_attn_in['Wo'], 'L0_attn_bo': _L0_attn_in['bo'], 'L0_attn_We': _L0_attn_in['We'], 'L0_attn_be': _L0_attn_in['be'], 'L0_ffn_router_w': _L0_ffn_in['router_w'], 'L0_ffn_w1': _L0_ffn_in['w1'], 'L0_ffn_b1': _L0_ffn_in['b1'], 'L0_ffn_w2': _L0_ffn_in['w2'], 'L0_ffn_b2': _L0_ffn_in['b2']}

def reference(x, L0_tok_W, L0_tok_b, L0_tok_pos_embed, L0_attn_edge_index, L0_attn_edge_attr, L0_attn_Wq, L0_attn_bq, L0_attn_Wk, L0_attn_bk, L0_attn_Wv, L0_attn_bv, L0_attn_Wo, L0_attn_bo, L0_attn_We, L0_attn_be, L0_ffn_router_w, L0_ffn_w1, L0_ffn_b1, L0_ffn_w2, L0_ffn_b2):
    import jax
    import jax.numpy as jnp

    def _L0_tok_ref(x, W, b, pos_embed):
        import jax, jax.numpy as jnp
        import numpy as np
        PATCH = 8
        EMBED = 64
        N_MELS = 128
        N_FRAMES = 512
        BATCH = 64
        NUM_PATCHES = N_MELS // PATCH * (N_FRAMES // PATCH)
        B = x.shape[0]
        mp, fp = (N_MELS // PATCH, N_FRAMES // PATCH)
        xs = x[:, 0]
        patches = xs.reshape(B, mp, PATCH, fp, PATCH).transpose(0, 1, 3, 2, 4).reshape(B, mp * fp, PATCH * PATCH)
        emb = jnp.einsum('bnk,ek->bne', patches, W) + b
        return emb + pos_embed

    def _L0_attn_ref(x, edge_index, edge_attr, Wq, bq, Wk, bk, Wv, bv, Wo, bo, We, be):
        import jax, jax.numpy as jnp
        import numpy as np
        H = 8
        B, N, D = x.shape
        hd = D // H
        q = (x @ Wq + bq).reshape(B, N, H, hd)
        k = (x @ Wk + bk).reshape(B, N, H, hd)
        v = (x @ Wv + bv).reshape(B, N, H, hd)
        scores = jnp.einsum('bihd,bjhd->bhij', q, k) / jnp.sqrt(jnp.asarray(hd, x.dtype))
        eb = edge_attr @ We + be
        edge_tgt = edge_index[1]
        col_bias = jnp.zeros((H, N), x.dtype).at[:, edge_tgt].set(eb.T)
        scores = scores + col_bias[None, :, None, :]
        attn = jax.nn.softmax(scores, axis=-1)
        out = jnp.einsum('bhij,bjhd->bihd', attn, v).reshape(B, N, D)
        return out @ Wo + bo

    def _L0_ffn_ref(input_embeddings, router_w, w1, b1, w2, b2):
        import jax, jax.numpy as jnp
        import numpy as np
        NUM_EXPERTS = 8
        TOP_K = 2
        B, S, D = (8, 2048, 64)

        def _moe(tokens, router_w, w1, b1, w2, b2):
            N = tokens.shape[0]
            E = router_w.shape[0]
            logits = tokens.astype(jnp.float32) @ router_w.astype(jnp.float32).T
            probs = jax.nn.softmax(logits, axis=-1)
            rw, re = jax.lax.top_k(probs, TOP_K)
            if TOP_K > 1:
                rw = rw / jnp.maximum(rw.sum(-1, keepdims=True), 1e-12)
            rw = rw.astype(tokens.dtype)
            combine = jnp.zeros((N, E), tokens.dtype).at[jnp.arange(N)[:, None], re].set(rw)
            out = tokens
            for e in range(E):
                h = jax.nn.gelu(tokens @ w1[e] + b1[e], approximate=False)
                y = h @ w2[e] + b2[e]
                out = out + combine[:, e:e + 1] * y
            return out
        b, s, d = input_embeddings.shape
        tokens = input_embeddings.reshape(b * s, d)
        return _moe(tokens, router_w, w1, b1, w2, b2).reshape(b, s, d)
    h = _L0_tok_ref(x, L0_tok_W, L0_tok_b, L0_tok_pos_embed)
    h = h + _L0_attn_ref(_layernorm(h, axis=-1), L0_attn_edge_index, L0_attn_edge_attr, L0_attn_Wq, L0_attn_bq, L0_attn_Wk, L0_attn_bk, L0_attn_Wv, L0_attn_bv, L0_attn_Wo, L0_attn_bo, L0_attn_We, L0_attn_be)
    h = h + _L0_ffn_ref(_layernorm(h, axis=-1), L0_ffn_router_w, L0_ffn_w1, L0_ffn_b1, L0_ffn_w2, L0_ffn_b2)
    return h

_drawn_inputs = setup_inputs


def setup_inputs(seed=0):
    import zlib

    import numpy as np

    out = dict(_drawn_inputs(seed))
    spreads = {'L0_attn_bq': (0.0, 0.8),
     'L0_attn_bk': (0.0, 0.8),
     'L0_attn_bv': (0.0, 0.286),
     'L0_attn_bo': (0.0, 0.1),
     'L0_attn_be': (0.0, 0.8),
     'L0_ffn_b1': (0.0, 0.327),
     'L0_ffn_b2': (0.0, 0.1)}
    factors = {'L0_attn_edge_attr': 8.0,
     'L0_attn_Wq': 8.0,
     'L0_attn_Wk': 8.0,
     'L0_attn_Wv': 8.0,
     'L0_attn_We': 8.0}
    for name, (base, spread) in spreads.items():
        noise = np.random.default_rng([zlib.crc32(name.encode()), seed]).standard_normal(out[name].shape)
        drawn = base * np.exp(spread * noise) if base else spread * noise
        out[name] = jnp.asarray(drawn.astype(out[name].dtype))
    for name, factor in factors.items():
        out[name] = (out[name] * factor).astype(out[name].dtype)
    return out
```

```python
import concourse.bass as bass
from concourse import mybir
from contextlib import ExitStack

F32 = mybir.dt.float32
BF16 = mybir.dt.bfloat16
I32 = mybir.dt.int32
ALU = mybir.AluOpType
ACT = mybir.ActivationFunctionType
AX = mybir.AxisListType

P = 128
NB = 16
T = 1024
D = 64
H = 8
HD = D // H
NCH = T // P
E = 16384
EC = E // P
NX = 8

EPS = 1e-5
BANK = 512

PARTS = 3
PART_ROWS = PARTS * PARTS * HD
BIAS_ROW = PART_ROWS
SHIFT_ROW = PART_ROWS + PARTS
SCORE_ROWS = SHIFT_ROW + PARTS

QUADS = 2 * 2 * NCH
BLOCKS = 2 * QUADS
GROUPS = 4
LAG = 2
SCORE_BUFS = 3
PROB_BUFS = 8
EVAC_SLOTS = {8 * g + 7 + LAG: g for g in range(3)}
LAST_EVAC_SLOT = LAG - 1
AUX_SLOTS = {2: ["embed"], 4: ["out_proj"], 7: ["norm_t0"], 8: ["norm_t1"], 9: ["qk0"], 10: ["qk1"],
             11: ["v"], 15: ["sq0"], 16: ["sq1"], 19: ["flag"],
             20: ["post_t0"], 21: ["post_t1"], 22: ["router"], 29: ["combine_t"]}
PREP = ["embed", "norm_t0", "norm_t1", "qk0", "qk1", "v", "sq0", "sq1", "flag"]
POST = ["out_proj", "post_t0", "post_t1", "router", "combine_t"]
ROUTER_EXP_BLOCK = 47
RQ_LIMIT = 31.0
TINY = 1e-30


ds = bass.ds

FB_UNITS = 4 * NCH


def steps_of(slot, prep, post):
    return [s for s in AUX_SLOTS.get(slot, []) if (prep and s in PREP) or (post and s in POST)]


def aux_order(prep, post):
    return [s for slot in range(QUADS) for s in steps_of(slot, prep, post)]


def aux_base(b):
    if isinstance(b, int) and b == 0:
        return len(PREP)
    return (len(PREP) + len(POST)) * b + (2 * len(PREP) - len(PREP) - len(POST))


def edge_bias(nc, pool, io, psum, scratch):
    KA, QA, bmax = pool["KA"], pool["QA"], pool["bmax"]
    ctx = ExitStack()
    with ctx:
        def sb(name, shape, dt):
            return ctx.enter_context(nc.sbuf_tensor(name, shape, dt))

        def sem(name):
            return ctx.enter_context(nc.semaphore(name))

        tgt = sb("tgt", [P, EC], I32)
        node_a = sb("node_a", [P, EC], I32)
        node_b = sb("node_b", [P, EC], I32)
        node_af = sb("node_af", [P, EC], F32)
        node_bf = sb("node_bf", [P, EC], F32)
        iota32 = sb("iota32", [P, 32], F32)
        exp_bits = sb("exp_bits", [P, 1], I32)
        hot_a = sb("hot_a", [P, EC, 2, 32], BF16)
        hot_b = sb("hot_b", [P, EC, 32], BF16)
        exps = sb("exps", [64, EC * 32], I32)
        base = sb("base", [64, EC * 32], F32)
        key = sb("key", [64, EC * 32], F32)
        win2 = sb("win2", [64, 32], F32)
        win_hi = sb("win_hi", [32, 32], F32)
        win = sb("win", [32, 32], F32)
        winp = sb("winp", [P, NCH], F32)
        valid = sb("valid", [P, NCH], F32)
        first = sb("first", [P, NCH], F32)
        idx = sb("idx", [P, NCH], I32)
        attr = sb("attr", [P, NCH, 3], F32)
        we = sb("we", [P, 3, H], F32)
        be = sb("be", [P, H], F32)
        term = sb("term", [P, NCH, H], F32)
        bias = sb("bias", [P, NCH, H], F32)
        bias_hj = sb("bias_hj", [P, H, NCH], F32)
        biasT = sb("biasT", [D, P], F32)
        rows = sb("rows", [H, T], F32)
        rest = sb("rest", [H, T], F32)
        rest2 = sb("rest2", [H, T], F32)
        bparts = sb("bparts", [H, PARTS, T], BF16)

        s_load = sem("e_load")
        s_iota = sem("e_iota")
        s_ident = sem("e_ident")
        s_hot = sem("e_hot")
        s_sum = sem("e_sum")
        s_win = sem("e_win")
        s_winp = sem("e_winp")
        s_idx = sem("e_idx")
        s_gather = sem("e_gather")
        s_bias = sem("e_bias")
        s_biasT = sem("e_biasT")
        s_rows_out = sem("e_rows_out")
        s_rows = sem("e_rows")
        s_parts = sem("e_parts")
        s_done = sem("e_done")
        s_chain = sem("e_chain")
        win_d, bias_d, bparts_d = scratch["win"], scratch["bias"], scratch["bparts"]

        with nc.Block() as block:
            @block.sync
            def _(sp):
                sp.dma_start(tgt[:, :], io["tgt"]).then_inc(s_load, 16)
                sp.dma_start(we[:, :, :], io["We"].rearrange("c h -> (c h)").partition_broadcast(P)).then_inc(s_load, 16)
                sp.dma_start(be[:, :], io["be"].partition_broadcast(P)).then_inc(s_load, 16)
                sp.wait_ge(s_win, 1)
                sp.dma_start(win_d.rearrange("(a b) -> a b", b=32), win[:, :]).then_inc(s_winp, 16)
                sp.wait_ge(s_winp, 16)
                with nc.allow_non_contiguous_dma(reason="1024 words, once"):
                    sp.dma_start(winp[:, :], win_d.rearrange("(c p) -> p c", p=P)).then_inc(s_winp, 16)
                sp.wait_ge(s_biasT, 1)
                sp.dma_start(bias_d.rearrange("h (c p) -> (h c) p", p=P), biasT[:, :]).then_inc(s_rows_out, 16)
                sp.wait_ge(s_rows_out, 16)
                sp.dma_start(rows[:, :], bias_d).then_inc(s_rows, 16)
                sp.wait_ge(s_parts, 1)
                sp.dma_start(bparts_d.rearrange("c h j -> h c j"), bparts[:, :, :]).then_inc(s_done, 16)
                sp.wait_ge(s_done, 16)
                sp.dma_start(KA[BIAS_ROW:BIAS_ROW + PARTS, :, :], bparts_d).then_inc(s_done, 16)
                sp.wait_ge(s_done, 32)

            @block.gpsimd
            def _(g):
                g.iota(iota32[:, :], pattern=[[1, 32]], base=0, channel_multiplier=0,
                       allow_small_or_imprecise_dtypes=True).then_inc(s_iota, 1)
                for half in range(2):
                    g.wait_ge(s_iota, 1 + half)
                    g.iota(exp_bits[64 * half:64 * half + 64, :], pattern=[[0, 1]], base=127,
                           channel_multiplier=2).then_inc(s_iota, 1)
                for half in range(2):
                    g.wait_ge(s_iota, 3 + half)
                    g.iota(base[32 * half:32 * half + 32, :], pattern=[[P, EC], [0, 32]], base=64 * half,
                           channel_multiplier=0, allow_small_or_imprecise_dtypes=True).then_inc(s_iota, 1)
                ident, ident_bf = pool["ident"], pool["ident_bf"]
                g.wait_ge(s_iota, 5)
                g.memset(ident[:, :], 0.0).then_inc(s_ident, 1)
                g.wait_ge(s_ident, 1)
                g.affine_select(out=ident[:, :], in_=ident[:, :], compare_op=ALU.not_equal, fill=1.0, base=0,
                                pattern=[[-1, P]], channel_multiplier=1).then_inc(s_ident, 1)
                g.wait_ge(s_ident, 2)
                g.tensor_copy(ident_bf[:, :], ident[:, :]).then_inc(s_ident, 1)
                g.wait_ge(s_idx, 1)
                for c in range(NCH):
                    g.indirect_dma_start(out=attr[:, c, :], out_offset=None, in_=io["edge_attr"],
                                         in_offset=bass.IndirectOffsetOnAxis(ap=idx[:, c:c + 1], axis=0)
                                         ).then_inc(s_gather, 16)

            @block.vector
            def _(v):
                count = [0]

                def link(ins):
                    count[0] += 1
                    ins.then_inc(s_chain, 1)
                    v.wait_ge(s_chain, count[0])

                v.memset(hot_a[:, :, :, :], 0.0)
                v.memset(KA[64:P, :, :], 1.0)
                v.memset(QA[64:P, :, :], 1.0)
                v.wait_ge(s_load, 48)
                v.wait_ge(s_iota, 5)
                v.tensor_scalar(node_a[:, :], tgt[:, :], 5, None, ALU.logical_shift_right)
                link(v.tensor_scalar(node_b[:, :], tgt[:, :], 31, None, ALU.bitwise_and))
                v.tensor_copy(node_af[:, :], node_a[:, :])
                v.tensor_copy(node_bf[:, :], node_b[:, :])
                link(v.tensor_scalar(exp_bits[:, :], exp_bits[:, :], 23, None, ALU.logical_shift_left))
                for g in range(2):
                    q = slice(64 * g, 64 * g + 64)
                    v.tensor_tensor(hot_a[q, :, g, :], node_af[q, :].unsqueeze(2).broadcast_to([64, EC, 32]),
                                    iota32[q, :].unsqueeze(1).broadcast_to([64, EC, 32]), ALU.is_equal)
                link(v.tensor_tensor(hot_b[:, :, :], node_bf[:, :].unsqueeze(2).broadcast_to([P, EC, 32]),
                                     iota32[:, :].unsqueeze(1).broadcast_to([P, EC, 32]), ALU.is_equal))
                v.tensor_scalar(hot_b[:, :, :], hot_b[:, :, :], exp_bits[:, 0:1].bitcast(F32), None,
                                ALU.mult).then_inc(s_hot, 1)
                v.wait_ge(s_sum, 8)
                sums = psum[0:64, :].bitcast(I32)
                link(v.tensor_scalar(exps[:, :], sums, 23, None, ALU.logical_shift_right))
                link(v.scalar_tensor_tensor(key[:, :], exps[:, :], 0.5, base[:, :], ALU.mult, ALU.add))
                link(v.tensor_scalar(key[:, :], key[:, :], -62.5, None, ALU.add))
                link(v.scalar_tensor_tensor(base[:, :], exps[:, :], 0.0, key[:, :], ALU.is_gt, ALU.mult))
                link(v.tensor_reduce(win2[:, :], base[:, :].rearrange("p (m b) -> p b m", b=32), AX.X, ALU.max))
                link(v.tensor_copy(win_hi[:, :], win2[32:64, :]))
                v.tensor_tensor(win[:, :], win2[0:32, :], win_hi[:, :], ALU.max).then_inc(s_win, 1)
                v.wait_ge(s_winp, 32)
                v.tensor_scalar(valid[:, :], winp[:, :], 0.0, None, ALU.is_gt)
                link(v.tensor_scalar(first[:, :], winp[:, :], -1.0, 0.0, ALU.add, ALU.max))
                v.tensor_copy(idx[:, :], first[:, :]).then_inc(s_idx, 1)
                v.wait_ge(s_gather, 16 * NCH)
                for c in range(3):
                    dst = bias if c == 0 else term
                    link(v.tensor_tensor(dst[:, :, :], attr[:, :, c:c + 1].broadcast_to([P, NCH, H]),
                                         we[:, c, :].unsqueeze(1).broadcast_to([P, NCH, H]), ALU.mult))
                    if c:
                        link(v.tensor_tensor(bias[:, :, :], bias[:, :, :], term[:, :, :], ALU.add))
                link(v.tensor_tensor(bias[:, :, :], bias[:, :, :],
                                     be[:, :].unsqueeze(1).broadcast_to([P, NCH, H]), ALU.add))
                v.tensor_tensor(bias_hj[:, :, :].rearrange("p h c -> p c h"), bias[:, :, :],
                                valid[:, :].unsqueeze(2).broadcast_to([P, NCH, H]), ALU.mult).then_inc(s_bias, 1)
                v.wait_ge(s_sum, 9)
                v.tensor_copy(biasT[:, :], psum[0:D, 0:P]).then_inc(s_biasT, 1)
                v.wait_ge(s_rows, 16)
                v.reduce_max(bmax[:, :], rows[:, :], AX.X)
                link(v.tensor_copy(bparts[:, 0, :], rows[:, :]))
                link(v.tensor_tensor(rest[:, :], rows[:, :], bparts[:, 0, :], ALU.subtract))
                link(v.tensor_copy(bparts[:, 1, :], rest[:, :]))
                v.tensor_tensor(bparts[:, 2, :], rest[:, :], bparts[:, 1, :], ALU.subtract).then_inc(s_parts, 1)

            @block.tensor
            def _(pe):
                pe.wait_ge(s_hot, 1)
                for m in range(EC):
                    last = pe.matmul(psum[0:64, 32 * m:32 * m + 32], hot_a[:, m, :, :].rearrange("p g a -> p (g a)"),
                                     hot_b[:, m, :], start=True, stop=True)
                    if m % 16 == 15:
                        last.then_inc(s_sum, 1)
                pe.wait_ge(s_ident, 2)
                pe.wait_ge(s_bias, 1)
                pe.transpose(psum[0:D, 0:P], bias_hj[:, :, :].rearrange("p h c -> p (h c)"),
                             pool["ident"][:, :]).then_inc(s_sum, 1)


def attention(nc, pool, io, psum, scratch):
    KA, QA, H_all, bmax, ident, ident_bf = (pool[k] for k in ("KA", "QA", "H_all", "bmax", "ident", "ident_bf"))
    parts_d, shift_d, fb_d = scratch["parts"], scratch["shift"], scratch["fb"]
    x2T_d, cT_d = scratch["x2T"], scratch["cT"]
    ctx = ExitStack()
    with ctx:
        def sb(name, shape, dt):
            return ctx.enter_context(nc.sbuf_tensor(name, shape, dt))

        def sem(name):
            return ctx.enter_context(nc.semaphore(name))

        w_tok = sb("w_tok", [D, D], F32)
        w_qk = sb("w_qk", [D, 2 * D], F32)
        w_v = sb("w_v", [D, D], F32)
        w_o = sb("w_o", [P, 2, D], F32)
        w_r = sb("w_r", [D, NX], F32)
        posb = sb("posb", [P, NCH, D], F32)
        tok_b = sb("tok_b", [P, D], F32)
        b_v = sb("b_v", [P, D], F32)
        b_o = sb("b_o", [P, D], F32)
        b_qk = sb("b_qk", [P, 1], F32)
        scale_qk = sb("scale_qk", [P, 1], F32)
        sel_sq = sb("sel_sq", [P, H], BF16)
        ones8 = sb("ones8", [H, 1], F32)
        lower = sb("lower", [P, NX, NX], F32)
        neg_half = sb("neg_half", [P, NCH], F32)
        half = sb("half", [H, 1], F32)
        xT = sb("xT", [D, T], F32)
        stats = sb("stats", [P, NCH, 6], F32)
        mv = sb("mv", [P, NCH, 2], F32)
        ve = sb("ve", [P, NCH], F32)
        rstd = sb("rstd", [P, NCH], F32)
        centred = sb("centred", [P, NCH, D], F32)
        xn = sb("xn", [P, NCH, D], F32)
        xnT = sb("xnT", [D, T], F32)
        qk = sb("qk", [P, T], F32)
        qk_rest = sb("qk_rest", [P, T], F32)
        qk_parts = sb("qk_parts", [P, PARTS, T], BF16)
        squares = sb("squares", [P, T], BF16)
        v_new = sb("v_new", [P, NCH, D], F32)
        q_sq = sb("q_sq", [H, T], F32)
        q_sq_max = sb("q_sq_max", [H, 1], F32)
        k_sq_max = sb("k_sq_max", [H, 3], F32)
        rq2 = sb("rq2", [H, 1], F32)
        rq = sb("rq", [H, 1], F32)
        coef = sb("coef", [H, 4], F32)
        excess = sb("excess", [H, 1], F32)
        shift = sb("shift", [H, T], F32)
        shift_rest = sb("shift_rest", [H, T], F32)
        shift_parts = sb("shift_parts", [H, PARTS, T], BF16)
        flags = sb("flags", [1, NB], I32)
        VA = sb("VA", [P, NCH, H, 32], F32)
        probs = sb("probs", [P, PROB_BUFS, 2 * BANK], F32)
        o_raw = sb("o_raw", [P, BANK], F32)
        denom = sb("denom", [P, BANK], F32)
        o_inv = sb("o_inv", [P, BANK], F32)
        ON = sb("ON", [P, 2, T], F32)
        h1 = sb("h1", [P, NCH, D], F32)
        p_stats = sb("p_stats", [P, NCH, 6], F32)
        p_mv = sb("p_mv", [P, NCH, 2], F32)
        p_ve = sb("p_ve", [P, NCH], F32)
        p_rstd = sb("p_rstd", [P, NCH], F32)
        p_centred = sb("p_centred", [P, NCH, D], F32)
        x2 = sb("x2", [P, NCH, D], F32)
        x2T = sb("x2T", [D, T], F32)
        logit_max = sb("logit_max", [P, NCH], F32)
        logits = sb("logits", [P, NCH, NX], F32)
        router_e = sb("router_e", [P, NCH, NX], F32)
        r_sum = sb("r_sum", [P, NCH], F32)
        r_inv = sb("r_inv", [P, NCH], F32)
        rprob = sb("rprob", [P, NCH, NX], F32)
        above = sb("above", [P, NCH, NX * NX], F32)
        equal = sb("equal", [P, NCH, NX * NX], F32)
        rank = sb("rank", [P, NCH, NX], F32)
        chosen = sb("chosen", [P, NCH, NX], F32)
        c_sum = sb("c_sum", [P, NCH], F32)
        c_inv = sb("c_inv", [P, NCH], F32)
        comb = sb("comb", [P, NCH, NX], F32)
        comb_rest = sb("comb_rest", [P, NCH, NX], F32)
        comb_parts = sb("comb_parts", [P, NCH, PARTS, NX], BF16)
        cT = sb("cT", [PARTS * NX, T], BF16)
        fb_max = sb("fb_max", [P, FB_UNITS], F32)
        fb_rows = sb("fb_rows", [FB_UNITS, P], F32)
        fb_rest = sb("fb_rest", [FB_UNITS, P], F32)
        fb_parts = sb("fb_parts", [FB_UNITS, PARTS, P], BF16)

        def score_buf(i):
            return psum[:, 2 * BANK * i:2 * BANK * (i + 1)]

        o_acc = psum[:, 6 * BANK:7 * BANK]
        aux = psum[:, 7 * BANK:8 * BANK]

        w_loaded = sem("w_loaded")
        stood_alone = sem("stood_alone")
        w_out_loaded = sem("w_out_loaded")
        const_ready = sem("const_ready")
        x_loaded = sem("x_loaded")
        aux_filled = sem("aux_filled")
        aux_drained = sem("aux_drained")
        var_ready = sem("var_ready")
        rstd_ready = sem("rstd_ready")
        xn_ready = sem("xn_ready")
        parts_ready = sem("parts_ready")
        squares_ready = sem("squares_ready")
        rq2_ready = sem("rq2_ready")
        rq_ready = sem("rq_ready")
        excess_ready = sem("excess_ready")
        shift_ready = sem("shift_ready")
        parts_stored = sem("parts_stored")
        shift_stored = sem("shift_stored")
        aug_loaded = [sem("aug_loaded_0"), sem("aug_loaded_1")]
        va_ready = sem("va_ready")
        scored = sem("scored")
        exped = sem("exped")
        pv_done = sem("pv_done")
        o_evacuated = sem("o_evacuated")
        on_ready = sem("on_ready")
        p_var_ready = sem("p_var_ready")
        p_rstd_ready = sem("p_rstd_ready")
        x2_ready = sem("x2_ready")
        x2T_stored = sem("x2T_stored")
        router_exped = sem("router_exped")
        comb_ready = sem("comb_ready")
        cT_stored = sem("cT_stored")
        prep_chain = sem("prep_chain")
        post_chain = sem("post_chain")
        evac_chain = sem("evac_chain")
        fb_scored = sem("fb_scored")
        fb_maxed = sem("fb_maxed")
        fb_chain = sem("fb_chain")
        fb_moved = sem("fb_moved")

        WEIGHTS = 11
        AUG_DMAS = 2 * PARTS * PARTS + 1
        FB_SCORED, FB_MAXED, FB_MOVED, FB_CHAIN = FB_UNITS + 1, FB_UNITS + 1, 32, 4
        PREP_CHAIN, POST_CHAIN, EVAC_CHAIN = 15, 20, 2

        def later(b):
            return not (isinstance(b, int) and b == 0)

        def alone(eng):
            eng.sem_inc(stood_alone, 1)

        def all_batches(eng, prologue, body):
            prologue()
            body(0, True, False)
            with eng.Fori(1, NB - 1) as b:
                body(b, False, False)
            body(NB - 1, False, True)

        with nc.Block() as block:
            @block.sync
            def _(sp):
                for dst, src in ((w_tok[:, :], io["tok_WT"]), (w_qk[:, 0:D], io["Wq"]), (w_qk[:, D:2 * D], io["Wk"]),
                                 (w_v[:, :], io["Wv"]), (w_r[:, :], io["router_wT"]), (posb[:, :, :], io["pos"]),
                                 (tok_b[:, :], io["tok_b"].partition_broadcast(P)),
                                 (b_v[:, :], io["bv"].partition_broadcast(P)),
                                 (b_o[:, :], io["bo"].partition_broadcast(P)),
                                 (b_qk[0:D, :], io["bq"].unsqueeze(1)), (b_qk[D:P, :], io["bk"].unsqueeze(1))):
                    sp.dma_start(dst, src).then_inc(w_loaded, 16)
                sp.wait_ge(const_ready, 1)
                for h in range(H):
                    r = 32 * (h % 4)
                    sp.dma_start(w_o[r:r + HD, h // 4, :], io["Wo"][h * HD:(h + 1) * HD, :]).then_inc(w_out_loaded, 16)

                def load_x(bp):
                    sp.dma_start(xT[:, :], io["xT"][bp, :, :]).then_inc(x_loaded, 16)

                def store_parts(bp):
                    sp.wait_ge(parts_ready, bp + 1)
                    sp.dma_start(parts_d.rearrange("a r i -> r a i"), qk_parts[:, :, :]).then_inc(parts_stored, 16)
                    sp.wait_ge(shift_ready, bp + 1)
                    sp.dma_start(shift_d.rearrange("a h i -> h a i"), shift_parts[:, :, :]).then_inc(shift_stored, 16)
                    sp.wait_ge(parts_stored, 16 * (bp + 1))
                    alone(sp)
                    sp.wait_ge(shift_stored, 16 * (bp + 1))
                    alone(sp)

                def load_aug(hg):
                    rows = slice(32 * hg, 32 * hg + 32)
                    krows = slice(D + 32 * hg, D + 32 * hg + 32)
                    hs = slice(4 * hg, 4 * hg + 4)
                    for a in range(PARTS):
                        for c in range(PARTS):
                            r = 24 * a + 8 * c
                            sp.dma_start(QA[r:r + HD, hs, :],
                                         parts_d[a, rows, :].rearrange("(h d) i -> d h i", d=HD)
                                         ).then_inc(aug_loaded[hg], 16)
                            sp.dma_start(KA[r:r + HD, hs, :],
                                         parts_d[c, krows, :].rearrange("(h d) i -> d h i", d=HD)
                                         ).then_inc(aug_loaded[hg], 16)
                    sp.dma_start(QA[SHIFT_ROW:SHIFT_ROW + PARTS, hs, :], shift_d[:, hs, :]).then_inc(aug_loaded[hg], 16)

                def prologue():
                    load_x(0)
                    store_parts(0)
                    load_aug(0)
                    load_aug(1)

                def body(b, first, last):
                    if not last:
                        sp.wait_ge(aux_filled, aux_base(b))
                        load_x(b + 1)
                        for hg in range(2):
                            sp.wait_ge(aug_loaded[hg], 16 * AUG_DMAS * (b + 1))
                            alone(sp)
                        store_parts(b + 1)
                    order = aux_order(not last, not first)
                    if not first:
                        sp.wait_ge(aux_drained, aux_base(b) + order.index("post_t1") + 1)
                        sp.dma_start(x2T_d[b - 1, :, :], x2T[:, :]).then_inc(x2T_stored, 16)
                    if not last:
                        sp.wait_ge(scored, BLOCKS * b + BLOCKS // 2)
                        load_aug(0)
                    if not first:
                        sp.wait_ge(aux_drained, aux_base(b) + order.index("combine_t") + 1)
                        sp.dma_start(cT_d[b - 1, :, :], cT[:, :]).then_inc(cT_stored, 16)
                    if not last:
                        sp.wait_ge(scored, BLOCKS * (b + 1))
                        load_aug(1)

                all_batches(sp, prologue, body)
                end = aux_base(NB - 1) + len(POST)
                sp.wait_ge(aux_drained, end + POST.index("post_t1") + 1)
                sp.dma_start(x2T_d[NB - 1, :, :], x2T[:, :]).then_inc(x2T_stored, 16)
                sp.wait_ge(aux_drained, end + POST.index("combine_t") + 1)
                sp.dma_start(cT_d[NB - 1, :, :], cT[:, :]).then_inc(cT_stored, 16)
                sp.wait_ge(x2T_stored, 16 * NB)
                sp.wait_ge(cT_stored, 16 * NB)

            @block.gpsimd
            def _(g):
                def prep_rstd(bp):
                    g.wait_ge(var_ready, bp + 1)
                    g.tensor_tensor(rstd[:, :], ve[:, :], neg_half[:, :], ALU.pow).then_inc(rstd_ready, 1)

                def prep_rq(bp):
                    g.wait_ge(rq2_ready, bp + 1)
                    g.tensor_tensor(rq[:, :], rq2[:, :], half[:, :], ALU.pow).then_inc(rq_ready, 1)

                def copy_v(hg):
                    hs = slice(4 * hg, 4 * hg + 4)
                    src = v_new[:, :, 32 * hg:32 * hg + 32].rearrange("p c (h d) -> p c h d", d=HD)
                    g.tensor_copy(VA[:, :, hs, 0:HD], src).then_inc(va_ready, 1)

                def prologue():
                    g.wait_ge(const_ready, 3)
                    prep_rstd(0)
                    g.wait_ge(aux_drained, PREP.index("v") + 1)
                    copy_v(0)
                    copy_v(1)
                    prep_rq(0)

                def post_pow(bq):
                    g.wait_ge(p_var_ready, bq + 1)
                    g.tensor_tensor(p_rstd[:, :], p_ve[:, :], neg_half[:, :], ALU.pow).then_inc(p_rstd_ready, 1)

                def body(b, first, last):
                    if not last:
                        prep_rstd(b + 1)
                    if not first:
                        post_pow(b - 1)
                    if not last:
                        prep_rq(b + 1)
                        g.wait_ge(aux_drained, aux_base(b) + aux_order(True, not first).index("v") + 1)
                        for hg in range(2):
                            g.wait_ge(pv_done, QUADS * b + 16 * (hg + 1))
                            alone(g)
                            copy_v(hg)

                all_batches(g, prologue, body)
                post_pow(NB - 1)

            @block.scalar
            def _(act):
                def exp_block(b, k):
                    act.wait_ge(scored, BLOCKS * b + k + 1)
                    if k >= PROB_BUFS:
                        act.wait_ge(pv_done, QUADS * b + (k - PROB_BUFS) // 2 + 1)
                    elif later(b):
                        act.wait_ge(pv_done, QUADS * b + (k - PROB_BUFS) // 2 + 1)
                    nc.scalar.activation(probs[:, k % PROB_BUFS, :], score_buf(k % SCORE_BUFS),
                                         ACT.Exp).then_inc(exped, 1)

                def router_exp(drained):
                    act.wait_ge(aux_drained, drained)
                    nc.scalar.activation(router_e[:, :, :], logits[:, :, :], ACT.Exp).then_inc(router_exped, 1)

                def fallback(b, hg, flag):
                    with act.If(flag != 0):
                        act.wait_ge(fb_maxed, FB_MAXED * (2 * b + hg + 1))
                        act.dma_start(fb_d.rearrange("a u p -> u a p"), fb_parts[:, :, :]).then_inc(fb_moved, 16)
                        act.wait_ge(fb_moved, FB_MOVED * (2 * b + hg) + 16)
                        act.dma_start(QA[SHIFT_ROW:SHIFT_ROW + PARTS, 4 * hg:4 * hg + 4, :],
                                      fb_d.rearrange("a (h c) p -> a h (c p)", h=4)).then_inc(fb_moved, 16)
                    with act.Else():
                        act.sem_inc(fb_moved, FB_MOVED)

                def body(b, first, last):
                    act.wait_ge(aux_drained, aux_base(b))
                    flag = act.value_load(flags[0:1, ds(b, 1)], min_val=0, max_val=1)
                    for k in range(BLOCKS):
                        if k % (BLOCKS // 2) == 0:
                            fallback(b, k // (BLOCKS // 2), flag)
                        exp_block(b, k)
                        if k == ROUTER_EXP_BLOCK and not first:
                            router_exp(aux_base(b) + aux_order(not last, True).index("router") + 1)

                all_batches(act, lambda: None, body)
                router_exp(aux_base(NB - 1) + len(POST) + POST.index("router") + 1)

            @block.vector
            def _(v):
                def chain(sem, base, total):
                    count = [0]

                    def link(ins):
                        count[0] += 1
                        ins.then_inc(sem, 1)
                        v.wait_ge(sem, base + count[0])

                    def close():
                        assert count[0] == total, (count[0], total)
                    return link, close

                v.memset(w_o[:, :, :], 0.0).then_inc(const_ready, 1)
                v.memset(VA[:, :, :, :], 0.0)
                v.memset(scale_qk[0:D, :], HD ** -0.5)
                v.memset(scale_qk[D:P, :], 1.0)
                v.memset(ones8[:, :], 1.0)
                v.memset(half[:, :], 0.5)
                v.memset(neg_half[:, :], -0.5).then_inc(const_ready, 1)
                v.wait_ge(const_ready, 2)
                v.memset(VA[:, :, :, HD:HD + 1], 1.0).then_inc(const_ready, 1)
                v.wait_ge(w_loaded, 16 * WEIGHTS)
                v.tensor_reduce(lower[:, 0, :], ident[:, 0:D].rearrange("p (h d) -> p h d", d=HD), AX.X, ALU.add)
                v.tensor_reduce(lower[:, 1, :], ident[:, D:P].rearrange("p (h d) -> p h d", d=HD), AX.X,
                                ALU.add).then_inc(const_ready, 1)
                v.wait_ge(const_ready, 4)
                v.tensor_tensor(sel_sq[:, :], lower[:, 0, :], lower[:, 1, :], ALU.add)
                v.tensor_tensor(posb[:, :, :], posb[:, :, :], tok_b[:, :].unsqueeze(1).broadcast_to([P, NCH, D]),
                                ALU.add).then_inc(const_ready, 1)
                v.wait_ge(const_ready, 5)
                v.memset(lower[:, :, :], 0.0).then_inc(const_ready, 1)
                v.wait_ge(const_ready, 6)
                for e in range(1, NX):
                    last = v.memset(lower[:, e, 0:e], 1.0)
                last.then_inc(const_ready, 1)
                v.wait_ge(const_ready, 7)

                def layernorm(src, stats_, mv_, ve_, centred_, rstd_, dst, link, ready, rstd_done, count, out_sem):
                    for c in range(NCH):
                        last = v.bn_stats(stats_[:, c, :], src(c))
                    link(last)
                    alone(v)
                    for c in range(NCH):
                        last = v.bn_aggr(mv_[:, c, :], stats_[:, c, :])
                    link(last)
                    v.tensor_scalar(ve_[:, :], mv_[:, :, 1], EPS, None, ALU.add).then_inc(ready, 1)
                    link(v.tensor_tensor(centred_[:, :, :], src(None),
                                         mv_[:, :, 0:1].broadcast_to([P, NCH, D]), ALU.subtract))
                    v.wait_ge(rstd_done, count)
                    return v.tensor_tensor(dst[:, :, :], centred_[:, :, :],
                                           rstd_[:, :].unsqueeze(2).broadcast_to([P, NCH, D]),
                                           ALU.mult).then_inc(out_sem, 1)

                def prep_step(step, bp, filled, st):
                    if step == "embed":
                        st["link"], st["close"] = chain(prep_chain, PREP_CHAIN * bp, PREP_CHAIN)
                    link, close = st["link"], st["close"]
                    v.wait_ge(aux_filled, filled)
                    if step == "embed":
                        v.tensor_tensor(H_all[:, ds(bp * NCH, NCH), :], aux.rearrange("p (c e) -> p c e", e=D),
                                        posb[:, :, :], ALU.add).then_inc(aux_drained, 1)
                        v.wait_ge(aux_drained, filled)
                        alone(v)
                        layernorm(lambda c: H_all[:, ds(bp * NCH + c, 1), :] if c is not None
                                  else H_all[:, ds(bp * NCH, NCH), :], stats, mv, ve, centred, rstd, xn, link, var_ready, rstd_ready, bp + 1, xn_ready)
                    elif step in ("norm_t0", "norm_t1"):
                        n = int(step[-1])
                        v.tensor_copy(xnT[:, n * BANK:(n + 1) * BANK], aux[0:D, :]).then_inc(aux_drained, 1)
                    elif step in ("qk0", "qk1"):
                        n = int(step[-1])
                        v.tensor_scalar(qk[:, n * BANK:(n + 1) * BANK], aux, b_qk[:, 0:1], scale_qk[:, 0:1],
                                        ALU.add, ALU.mult).then_inc(aux_drained, 1)
                    elif step == "v":
                        if later(bp):
                            v.wait_ge(va_ready, 2 * bp)
                        v.tensor_tensor(v_new[:, :, :], aux.rearrange("p (c e) -> p c e", e=D),
                                        b_v[:, :].unsqueeze(1).broadcast_to([P, NCH, D]),
                                        ALU.add).then_inc(aux_drained, 1)
                        v.wait_ge(aux_drained, filled)
                        if later(bp):
                            v.wait_ge(parts_stored, 16 * bp)
                        link(v.tensor_copy(qk_parts[:, 0, :], qk[:, :]))
                        link(v.tensor_tensor(qk_rest[:, :], qk[:, :], qk_parts[:, 0, :], ALU.subtract))
                        v.tensor_tensor(squares[:, :], qk_parts[:, 0, :], qk_parts[:, 0, :],
                                        ALU.mult).then_inc(squares_ready, 1)
                        link(v.tensor_copy(qk_parts[:, 1, :], qk_rest[:, :]))
                        v.tensor_tensor(qk_parts[:, 2, :], qk_rest[:, :], qk_parts[:, 1, :],
                                        ALU.subtract).then_inc(parts_ready, 1)
                    elif step in ("sq0", "sq1"):
                        n = int(step[-1])
                        v.tensor_copy(q_sq[:, n * BANK:(n + 1) * BANK], aux[0:H, :])
                        v.reduce_max(k_sq_max[:, n:n + 1], aux[32:32 + H, :], AX.X).then_inc(aux_drained, 1)
                        if n == 1:
                            v.wait_ge(aux_drained, filled)
                            v.reduce_max(q_sq_max[:, :], q_sq[:, :], AX.X)
                            link(v.reduce_max(k_sq_max[:, 2:3], k_sq_max[:, 0:2], AX.X))
                            v.tensor_tensor(rq2[:, :], q_sq_max[:, :], k_sq_max[:, 2:3],
                                            ALU.mult).then_inc(rq2_ready, 1)
                            link(v.tensor_scalar(coef[:, 0:1], q_sq_max[:, :], TINY, None, ALU.max))
                            link(v.reciprocal(coef[:, 1:2], coef[:, 0:1]))
                            v.wait_ge(rq_ready, bp + 1)
                            v.tensor_scalar(excess[:, :], rq[:, :], RQ_LIMIT, None, ALU.is_gt
                                            ).then_inc(excess_ready, 1)
                            link(v.tensor_scalar(coef[:, 2:3], rq[:, :], 0.5, bmax[:, 0:1], ALU.mult, ALU.add))
                            link(v.scalar_tensor_tensor(coef[:, 3:4], coef[:, 1:2], -0.5, rq[:, :],
                                                        ALU.mult, ALU.mult))
                            link(v.tensor_scalar(shift[:, :], q_sq[:, :], coef[:, 3:4], coef[:, 2:3],
                                                 ALU.mult, ALU.subtract))
                            if later(bp):
                                v.wait_ge(shift_stored, 16 * bp)
                            link(v.tensor_copy(shift_parts[:, 0, :], shift[:, :]))
                            link(v.tensor_tensor(shift_rest[:, :], shift[:, :], shift_parts[:, 0, :], ALU.subtract))
                            link(v.tensor_copy(shift_parts[:, 1, :], shift_rest[:, :]))
                            close()
                            v.tensor_tensor(shift_parts[:, 2, :], shift_rest[:, :], shift_parts[:, 1, :],
                                            ALU.subtract).then_inc(shift_ready, 1)
                    else:
                        v.tensor_scalar(flags[0:1, ds(bp, 1)], aux[0:1, 0:1], 1.0, None,
                                        ALU.min).then_inc(aux_drained, 1)

                def post_step(step, bq, filled, st):
                    if step == "out_proj":
                        st["plink"], st["pclose"] = chain(post_chain, POST_CHAIN * bq, POST_CHAIN)
                    link, close = st["plink"], st["pclose"]
                    v.wait_ge(aux_filled, filled)
                    hq = H_all[:, ds(bq * NCH, NCH), :]
                    if step == "out_proj":
                        v.tensor_tensor(h1[:, :, :], aux.rearrange("p (c e) -> p c e", e=D), hq,
                                        ALU.add).then_inc(aux_drained, 1)
                        v.wait_ge(aux_drained, filled)
                        link(v.tensor_tensor(h1[:, :, :], h1[:, :, :], b_o[:, :].unsqueeze(1).broadcast_to([P, NCH, D]),
                                             ALU.add))
                        layernorm(lambda c: h1[:, c, :] if c is not None else h1[:, :, :], p_stats, p_mv, p_ve,
                                  p_centred, p_rstd, x2, link, p_var_ready, p_rstd_ready, bq + 1, x2_ready)
                        v.wait_ge(x2_ready, bq + 1)
                        v.tensor_tensor(hq, h1[:, :, :], x2[:, :, :], ALU.add)
                    elif step in ("post_t0", "post_t1"):
                        n = int(step[-1])
                        if n == 0 and later(bq):
                            v.wait_ge(x2T_stored, 16 * bq)
                        v.tensor_copy(x2T[:, n * BANK:(n + 1) * BANK], aux[0:D, :]).then_inc(aux_drained, 1)
                    elif step == "router":
                        raw = aux[:, 0:NCH * NX].rearrange("p (c e) -> p c e", e=NX)
                        link(v.tensor_reduce(logit_max[:, :], raw, AX.X, ALU.max))
                        v.tensor_tensor(logits[:, :, :], raw, logit_max[:, :].unsqueeze(2).broadcast_to([P, NCH, NX]),
                                        ALU.subtract).then_inc(aux_drained, 1)
                    else:
                        if later(bq):
                            v.wait_ge(cT_stored, 16 * bq)
                        v.tensor_copy(cT[:, :], aux[0:PARTS * NX, :].bitcast(BF16)).then_inc(aux_drained, 1)

                def combine(bq, st):
                    link, close = st["plink"], st["pclose"]
                    v.wait_ge(router_exped, bq + 1)
                    link(v.tensor_reduce(r_sum[:, :], router_e[:, :, :], AX.X, ALU.add))
                    link(v.reciprocal(r_inv[:, :], r_sum[:, :]))
                    link(v.tensor_tensor(rprob[:, :, :], router_e[:, :, :],
                                         r_inv[:, :].unsqueeze(2).broadcast_to([P, NCH, NX]), ALU.mult))
                    other = rprob[:, :, :].unsqueeze(2).broadcast_to([P, NCH, NX, NX])
                    own = rprob[:, :, :].unsqueeze(3).broadcast_to([P, NCH, NX, NX])
                    v.tensor_tensor(above[:, :, :].rearrange("p c (e f) -> p c e f", f=NX), other, own, ALU.is_gt)
                    last = v.tensor_tensor(equal[:, :, :].rearrange("p c (e f) -> p c e f", f=NX), other, own,
                                           ALU.is_equal)
                    link(last)
                    link(v.tensor_tensor(equal[:, :, :], equal[:, :, :],
                                         lower[:, :, :].rearrange("p e f -> p (e f)").unsqueeze(1).broadcast_to(
                                             [P, NCH, NX * NX]), ALU.mult))
                    link(v.tensor_tensor(above[:, :, :], above[:, :, :], equal[:, :, :], ALU.add))
                    link(v.tensor_reduce(rank[:, :, :], above[:, :, :].rearrange("p c (e f) -> p c e f", f=NX),
                                         AX.X, ALU.add))
                    link(v.scalar_tensor_tensor(chosen[:, :, :], rank[:, :, :], 2.0, rprob[:, :, :],
                                                ALU.is_lt, ALU.mult))
                    link(v.tensor_reduce(c_sum[:, :], chosen[:, :, :], AX.X, ALU.add))
                    link(v.tensor_scalar(c_inv[:, :], c_sum[:, :], 1e-12, None, ALU.max))
                    link(v.reciprocal(c_sum[:, :], c_inv[:, :]))
                    link(v.tensor_tensor(comb[:, :, :], chosen[:, :, :],
                                         c_sum[:, :].unsqueeze(2).broadcast_to([P, NCH, NX]), ALU.mult))
                    link(v.tensor_copy(comb_parts[:, :, 0, :], comb[:, :, :]))
                    link(v.tensor_tensor(comb_rest[:, :, :], comb[:, :, :], comb_parts[:, :, 0, :], ALU.subtract))
                    link(v.tensor_copy(comb_parts[:, :, 1, :], comb_rest[:, :, :]))
                    close()
                    v.tensor_tensor(comb_parts[:, :, 2, :], comb_rest[:, :, :], comb_parts[:, :, 1, :],
                                    ALU.subtract).then_inc(comb_ready, 1)

                def evacuate(b, g):
                    link, _ = chain(evac_chain, EVAC_CHAIN * (GROUPS * b + g), EVAC_CHAIN)
                    if later(b) or g:
                        v.wait_ge(on_ready, GROUPS * b + g)
                    v.wait_ge(pv_done, QUADS * b + 8 * g + 8)
                    v.tensor_copy(o_raw[:, :], o_acc).then_inc(o_evacuated, 1)
                    v.wait_ge(o_evacuated, GROUPS * b + g + 1)
                    alone(v)
                    link(v.stream_shuffle(denom[:, :], o_raw[:, :], [HD] * 32))
                    link(v.reciprocal(o_inv[:, :], denom[:, :]))
                    hg, ih = g // 2, g % 2
                    v.tensor_tensor(ON[:, hg, ih * BANK:(ih + 1) * BANK], o_raw[:, :], o_inv[:, :],
                                    ALU.mult).then_inc(on_ready, 1)

                def fallback(b, hg, flag):
                    base = 2 * b + hg
                    with v.If(flag != 0):
                        for u in range(FB_UNITS):
                            v.wait_ge(fb_scored, FB_SCORED * base + u + 1)
                            v.tensor_reduce(fb_max[:, u:u + 1], score_buf(u % 2), AX.X, ALU.max,
                                            negate=True).then_inc(fb_maxed, 1)
                        v.wait_ge(fb_scored, FB_SCORED * base + FB_UNITS + 1)
                        v.tensor_copy(fb_rows[:, :], psum[0:FB_UNITS, 4 * BANK:4 * BANK + P]).then_inc(fb_chain, 1)
                        v.wait_ge(fb_chain, FB_CHAIN * base + 1)
                        v.tensor_copy(fb_parts[:, 0, :], fb_rows[:, :]).then_inc(fb_chain, 1)
                        v.wait_ge(fb_chain, FB_CHAIN * base + 2)
                        v.tensor_tensor(fb_rest[:, :], fb_rows[:, :], fb_parts[:, 0, :],
                                        ALU.subtract).then_inc(fb_chain, 1)
                        v.wait_ge(fb_chain, FB_CHAIN * base + 3)
                        v.tensor_copy(fb_parts[:, 1, :], fb_rest[:, :]).then_inc(fb_chain, 1)
                        v.wait_ge(fb_chain, FB_CHAIN * base + 4)
                        v.tensor_tensor(fb_parts[:, 2, :], fb_rest[:, :], fb_parts[:, 1, :],
                                        ALU.subtract).then_inc(fb_maxed, 1)
                    with v.Else():
                        v.sem_inc(fb_maxed, FB_MAXED)
                        v.sem_inc(fb_chain, FB_CHAIN)

                def prologue():
                    st = {}
                    for i, step in enumerate(PREP):
                        prep_step(step, 0, i + 1, st)

                def body(b, first, last):
                    v.wait_ge(aux_drained, aux_base(b))
                    flag = v.value_load(flags[0:1, ds(b, 1)], min_val=0, max_val=1)
                    order = aux_order(not last, not first)
                    st = {}
                    for slot in range(QUADS):
                        if slot == 0:
                            fallback(b, 0, flag)
                        if slot == 16:
                            fallback(b, 1, flag)
                        for step in steps_of(slot, not last, not first):
                            filled = aux_base(b) + order.index(step) + 1
                            if step in PREP:
                                prep_step(step, b + 1, filled, st)
                            else:
                                post_step(step, b - 1, filled, st)
                        if slot == LAST_EVAC_SLOT and not first:
                            evacuate(b - 1, 3)
                        if slot in EVAC_SLOTS:
                            evacuate(b, EVAC_SLOTS[slot])
                            if EVAC_SLOTS[slot] == 2 and not first:
                                combine(b - 1, st)

                all_batches(v, prologue, body)
                evacuate(NB - 1, 3)
                st = {}
                for i, step in enumerate(POST):
                    if step == "combine_t":
                        combine(NB - 1, st)
                    post_step(step, NB - 1, aux_base(NB) - len(PREP) + i + 1, st)

            @block.tensor
            def _(pe):
                def aux_step(step, n, done, drained):
                    pe.wait_ge(aux_drained, drained) if not (isinstance(drained, int) and drained == 0) else None
                    if step == "embed":
                        pe.wait_ge(x_loaded, 16 * (n + 1))
                        for c in range(NCH):
                            last = pe.matmul(aux[:, c * D:(c + 1) * D], xT[:, c * P:(c + 1) * P], w_tok[:, :],
                                             start=True, stop=True)
                    elif step in ("norm_t0", "norm_t1", "post_t0", "post_t1"):
                        src, ready = (xn, xn_ready) if step[0] == "n" else (x2, x2_ready)
                        pe.wait_ge(ready, n + 1)
                        alone(pe)
                        for c in range(4):
                            last = pe.transpose(aux[0:D, c * P:(c + 1) * P], src[:, 4 * int(step[-1]) + c, :],
                                                ident[:, :])
                    elif step in ("qk0", "qk1"):
                        i = int(step[-1])
                        last = pe.matmul(aux, w_qk[:, :], xnT[:, i * BANK:(i + 1) * BANK], start=True, stop=True)
                    elif step == "v":
                        for c in range(NCH):
                            last = pe.matmul(aux[:, c * D:(c + 1) * D], xnT[:, c * P:(c + 1) * P], w_v[:, :],
                                             start=True, stop=True)
                    elif step in ("sq0", "sq1"):
                        i = int(step[-1])
                        pe.wait_ge(squares_ready, n + 1)
                        alone(pe)
                        cols = slice(i * BANK, (i + 1) * BANK)
                        pe.matmul(aux[0:H, :], sel_sq[0:D, :], squares[0:D, cols], start=True, stop=True)
                        last = pe.matmul(aux[32:32 + H, :], sel_sq[D:P, :], squares[D:P, cols], start=True, stop=True)
                    elif step == "flag":
                        pe.wait_ge(excess_ready, n + 1)
                        alone(pe)
                        last = pe.matmul(aux[0:1, 0:1], excess[:, :], ones8[:, :], start=True, stop=True)
                    elif step == "out_proj":
                        pe.wait_ge(on_ready, GROUPS * (n + 1))
                        for c in range(NCH):
                            for hg in range(2):
                                last = pe.matmul(aux[:, c * D:(c + 1) * D], ON[:, hg, c * P:(c + 1) * P], w_o[:, hg, :],
                                                 start=(hg == 0), stop=(hg == 1))
                    elif step == "router":
                        for c in range(NCH):
                            last = pe.matmul(aux[:, c * NX:(c + 1) * NX], x2T[:, c * P:(c + 1) * P], w_r[:, :],
                                             start=True, stop=True)
                    else:
                        pe.wait_ge(comb_ready, n + 1)
                        for c in range(NCH):
                            last = pe.transpose(aux[0:PARTS * NX, :].bitcast(BF16)[:, c * P:(c + 1) * P],
                                                comb_parts[:, c, :, :].rearrange("p a e -> p (a e)"), ident_bf[:, :])
                    last.then_inc(aux_filled, 1)

                def head_of(q, g):
                    return 4 * (q // 16) + g, (q // 8) % 2, q % 8

                def scores(b, q):
                    for g in range(4):
                        k = 2 * q + g // 2
                        if g % 2 == 0:
                            if k >= SCORE_BUFS:
                                pe.wait_ge(exped, BLOCKS * b + k - SCORE_BUFS + 1)
                            elif later(b):
                                prev = max(j for j in range(BLOCKS) if j % SCORE_BUFS == k)
                                pe.wait_ge(exped, BLOCKS * b - BLOCKS + prev + 1)
                        h, ih, jt = head_of(q, g)
                        last = pe.matmul(score_buf(k % SCORE_BUFS)[:, (g % 2) * BANK:(g % 2 + 1) * BANK],
                                         KA[0:SCORE_ROWS, h, jt * P:(jt + 1) * P],
                                         QA[0:SCORE_ROWS, h, ih * BANK:(ih + 1) * BANK], start=True, stop=True)
                        if g % 2:
                            last.then_inc(scored, 1)

                def values(b, q):
                    pe.wait_ge(exped, BLOCKS * b + 2 * q + 2)
                    if q % 8 == 0 and (later(b) or q):
                        pe.wait_ge(o_evacuated, GROUPS * b + q // 8)
                    if q % 16 == 0:
                        pe.wait_ge(va_ready, 2 * b + q // 16 + 1)
                    for g in range(4):
                        k = 2 * q + g // 2
                        h, ih, jt = head_of(q, g)
                        last = pe.matmul(o_acc[32 * g:32 * g + 32, :], VA[:, jt, h, :],
                                         probs[:, k % PROB_BUFS, (g % 2) * BANK:(g % 2 + 1) * BANK],
                                         start=(jt == 0), stop=(jt == NCH - 1))
                    last.then_inc(pv_done, 1)

                def fallback(b, hg, flag):
                    base = 2 * b + hg
                    with pe.If(flag != 0):
                        if later(b) or hg:
                            pe.wait_ge(exped, BLOCKS * b + BLOCKS // 2 * hg)
                        for u in range(FB_UNITS):
                            if u >= 2:
                                pe.wait_ge(fb_maxed, FB_MAXED * base + u - 1)
                            h, c = 4 * hg + u // NCH, u % NCH
                            for n in range(2):
                                last = pe.matmul(score_buf(u % 2)[:, n * BANK:(n + 1) * BANK],
                                                 QA[0:SHIFT_ROW, h, c * P:(c + 1) * P],
                                                 KA[0:SHIFT_ROW, h, n * BANK:(n + 1) * BANK], start=True, stop=True)
                            last.then_inc(fb_scored, 1)
                        pe.wait_ge(fb_maxed, FB_MAXED * base + FB_UNITS)
                        pe.transpose(psum[0:FB_UNITS, 4 * BANK:4 * BANK + P], fb_max[:, :],
                                     ident[:, :]).then_inc(fb_scored, 1)
                    with pe.Else():
                        pe.sem_inc(fb_scored, FB_SCORED)
                    pe.wait_ge(fb_moved, FB_MOVED * (base + 1))

                def prologue():
                    pe.wait_ge(w_loaded, 16 * WEIGHTS)
                    pe.wait_ge(w_out_loaded, 16 * H)
                    pe.wait_ge(const_ready, 7)
                    for i, step in enumerate(PREP):
                        aux_step(step, 0, i + 1, i)

                def body(b, first, last):
                    pe.wait_ge(aux_drained, aux_base(b))
                    flag = pe.value_load(flags[0:1, ds(b, 1)], min_val=0, max_val=1)
                    order = aux_order(not last, not first)
                    for q in range(QUADS):
                        if q % 16 == 0:
                            pe.wait_ge(aug_loaded[q // 16], 16 * AUG_DMAS * (b + 1))
                            fallback(b, q // 16, flag)
                        scores(b, q)
                        for step in steps_of(q, not last, not first):
                            i = order.index(step)
                            aux_step(step, b + 1 if step in PREP else b - 1, aux_base(b) + i + 1, aux_base(b) + i)
                        if q >= LAG:
                            values(b, q - LAG)
                        elif not first:
                            values(b - 1, QUADS + q - LAG)

                all_batches(pe, prologue, body)
                for q in range(QUADS - LAG, QUADS):
                    values(NB - 1, q)
                for i, step in enumerate(POST):
                    n = aux_base(NB) - len(PREP) + i
                    aux_step(step, NB - 1, n + 1, n)


def experts(nc, pool, io, psum, scratch, out):
    H_all = pool["H_all"]
    ctx = ExitStack()
    with ctx:
        def sb(name, shape, dt):
            return ctx.enter_context(nc.sbuf_tensor(name, shape, dt))

        def sem(name):
            return ctx.enter_context(nc.semaphore(name))

        PAIRS = NX // 2
        UNITS = 2 * PAIRS
        KC = PARTS * NX
        w1 = sb("w1", [D, NX * D], F32)
        w2 = sb("w2", [P, PAIRS, D], F32)
        b1 = sb("b1", [P, PAIRS], F32)
        b2 = sb("b2", [KC, D], F32)
        b2_rest = sb("b2_rest", [KC, D], F32)
        b2_parts = sb("b2_parts", [KC, PARTS, D], BF16)
        spread = sb("spread", [KC, PAIRS, P], BF16)
        x2T = sb("m_x2T", [D, 2, T], F32)
        cT = sb("m_cT", [KC, 2, T], BF16)
        act_h = sb("act_h", [P, 2, BANK], F32)
        gated = sb("gated", [P, 2 * PAIRS, BANK], F32)
        result = sb("result", [P, 2, NCH, D], F32)
        hid = [psum[:, i * BANK:(i + 1) * BANK] for i in range(2)]
        wgt = [psum[:, (2 + i) * BANK:(3 + i) * BANK] for i in range(2)]
        ybank = [psum[:, (4 + i) * BANK:(4 + i) * BANK + 4 * D] for i in range(2)]

        loaded = sem("m_loaded")
        consts = sem("m_consts")
        tokens = [sem(f"m_tokens_{i}") for i in range(2)]
        hidden = sem("m_hidden")
        weights = sem("m_weights")
        gelued = sem("m_gelued")
        gated_ready = sem("m_gated")
        y_ready = sem("m_y")
        y_taken = sem("m_y_taken")
        stored = [sem(f"m_stored_{i}") for i in range(2)]

        b2_ready = sem("m_b2_ready")
        LOADS = 3 + PARTS
        TAKE_AT = 3

        with nc.Block() as block:
            @block.sync
            def _(sp):
                def load_tokens(b, s):
                    sp.dma_start(x2T[:, s, :], scratch["x2T"][ds(b, 1), :, :].rearrange("o d t -> (o d) t")
                                 ).then_inc(tokens[s], 16)
                    sp.dma_start(cT[:, s, :], scratch["cT"][ds(b, 1), :, :].rearrange("o d t -> (o d) t")
                                 ).then_inc(tokens[s], 16)

                def store(pair, s):
                    sp.wait_ge(y_taken, 4 * pair + 2 * s + 2)
                    sp.dma_start(out[ds(pair * 2 + s, 1), :, :].rearrange("o (c p) e -> p (o c) e", p=P),
                                 result[:, s, :, :]).then_inc(stored[s], 16)

                def body_sp(pair, first, last):
                    for s in range(2):
                        if not last:
                            sp.wait_ge(y_ready, 4 * pair + 2 * s + 2)
                            load_tokens(pair * 2 + 2 + s, s)
                        store(pair, s)

                sp.dma_start(w1[:, :], io["w1"]).then_inc(loaded, 16)
                sp.dma_start(w2[:, :, :], io["w2"]).then_inc(loaded, 16)
                sp.dma_start(b1[:, :], io["b1"]).then_inc(loaded, 16)
                for a in range(PARTS):
                    sp.dma_start(b2[a * NX:(a + 1) * NX, :], io["b2"]).then_inc(loaded, 16)
                for s in range(2):
                    load_tokens(s, s)
                body_sp(0, True, False)
                with sp.Fori(1, NB // 2 - 1) as pair:
                    body_sp(pair, False, False)
                body_sp(NB // 2 - 1, False, True)
                for s in range(2):
                    sp.wait_ge(stored[s], 8 * NB)

            @block.gpsimd
            def _(g):
                g.memset(spread[:, :, :], 0.0).then_inc(consts, 1)
                for a in range(PARTS):
                    g.wait_ge(consts, a + 1)
                    view = spread[:, :, :].rearrange("k m (e n) -> k m e n", e=2)
                    g.affine_select(out=view, in_=view, compare_op=ALU.not_equal, fill=1.0, base=-NX * a,
                                    pattern=[[-2, PAIRS], [-1, 2], [0, D]], channel_multiplier=1).then_inc(consts, 1)

            @block.scalar
            def _(act):
                act.wait_ge(loaded, 16 * LOADS)

                def body(pair, first):
                    for i in range(2 * UNITS):
                        act.wait_ge(hidden, 2 * UNITS * pair + i + 1)
                        if i >= 2 or not first:
                            act.wait_ge(gated_ready, 2 * UNITS * pair + i - 1)
                        nc.scalar.activation(act_h[:, i % 2, :], hid[i % 2], ACT.Gelu,
                                             bias=b1[:, i % PAIRS:i % PAIRS + 1]).then_inc(gelued, 1)

                body(0, True)
                with act.Fori(1, NB // 2) as pair:
                    body(pair, False)

            @block.vector
            def _(v):
                v.wait_ge(loaded, 16 * LOADS)
                for n, ins in enumerate((
                        lambda: v.tensor_copy(b2_parts[:, 0, :], b2[:, :]),
                        lambda: v.tensor_tensor(b2_rest[:, :], b2[:, :], b2_parts[:, 0, :], ALU.subtract),
                        lambda: v.tensor_copy(b2_parts[:, 1, :], b2_rest[:, :]),
                        lambda: v.tensor_tensor(b2_parts[:, 2, :], b2_rest[:, :], b2_parts[:, 1, :], ALU.subtract))):
                    ins().then_inc(b2_ready, 1)
                    v.wait_ge(b2_ready, n + 1)

                def take(pair, half, first):
                    s, hh = (half % 4) // 2, half % 2
                    v.wait_ge(y_ready, 4 * pair + half + 1)
                    if hh == 0 and not first:
                        v.wait_ge(stored[s], 16 * pair)
                    rows = H_all[:, ds((pair * 2) * NCH + 4 * half, 4), :]
                    v.tensor_tensor(result[:, s, 4 * hh:4 * hh + 4, :], ybank[half % 2].rearrange(
                        "p (c e) -> p c e", e=D), rows, ALU.add).then_inc(y_taken, 1)

                def body(pair, first):
                    for i in range(2 * UNITS):
                        half = i // PAIRS
                        v.wait_ge(gelued, 2 * UNITS * pair + i + 1)
                        v.wait_ge(weights, 2 * UNITS * pair + i + 1)
                        if half >= 2 or not first:
                            v.wait_ge(y_ready, 4 * pair + half - 1)
                        v.tensor_tensor(gated[:, i % 8, :], act_h[:, i % 2, :], wgt[i % 2],
                                        ALU.mult).then_inc(gated_ready, 1)
                        if i % PAIRS == TAKE_AT and (half >= 1 or not first):
                            take(pair, half - 1, first)

                body(0, True)
                with v.Fori(1, NB // 2) as pair:
                    body(pair, False)
                take(NB // 2 - 1, 3, False)

            @block.tensor
            def _(pe):
                pe.wait_ge(loaded, 16 * LOADS)
                pe.wait_ge(consts, PARTS + 1)
                pe.wait_ge(b2_ready, 4)

                def sums(pair, half, first):
                    s, hh = (half % 4) // 2, half % 2
                    pe.wait_ge(gated_ready, 2 * UNITS * pair + PAIRS * (half + 1))
                    if half >= 2 or not first:
                        pe.wait_ge(y_taken, 4 * pair + half - 1)
                    for c in range(4):
                        y = ybank[half % 2][:, c * D:(c + 1) * D]
                        for m in range(PAIRS):
                            pe.matmul(y, gated[:, (PAIRS * (half % 2)) + m, c * P:(c + 1) * P], w2[:, m, :],
                                      start=(m == 0), stop=False)
                        for a in range(PARTS):
                            last = pe.matmul(y, cT[:, s, (4 * hh + c) * P:(4 * hh + c + 1) * P], b2_parts[:, a, :],
                                             start=False, stop=(a == PARTS - 1))
                    last.then_inc(y_ready, 1)

                def body(pair, first):
                    for i in range(2 * UNITS):
                        half, m = i // PAIRS, i % PAIRS
                        s, cols = half // 2, slice((half % 2) * BANK, (half % 2 + 1) * BANK)
                        if i % UNITS == 0:
                            pe.wait_ge(tokens[s], 32 * pair + 32)
                        if i >= 2 or not first:
                            pe.wait_ge(gelued, 2 * UNITS * pair + i - 1)
                        pe.matmul(hid[i % 2], w1[:, m * P:(m + 1) * P], x2T[:, s, cols],
                                  start=True, stop=True).then_inc(hidden, 1)
                        if i >= 2 or not first:
                            pe.wait_ge(gated_ready, 2 * UNITS * pair + i - 1)
                        pe.matmul(wgt[i % 2], spread[:, m, :], cT[:, s, cols],
                                  start=True, stop=True).then_inc(weights, 1)
                        if m == 1 and (half >= 1 or not first):
                            sums(pair, half - 1, first)

                body(0, True)
                with pe.Fori(1, NB // 2) as pair:
                    body(pair, False)
                sums(NB // 2 - 1, 3, False)


def vit_tower(nc, xT, tok_WT, tok_b, pos, tgt, edge_attr, Wq, bq, Wk, bk, Wv, bv, Wo, bo, We, be, router_wT,
              w1, b1, w2, b2, out):
    io = dict(xT=xT, tok_WT=tok_WT, tok_b=tok_b, pos=pos, tgt=tgt, edge_attr=edge_attr, Wq=Wq, bq=bq, Wk=Wk, bk=bk,
              Wv=Wv, bv=bv, Wo=Wo, bo=bo, We=We, be=be, router_wT=router_wT, w1=w1, b1=b1, w2=w2, b2=b2)

    def dram(name, shape, dt):
        return nc.dram_tensor(name, shape, dt, kind="Internal").ap()

    scratch = dict(win=dram("win_d", [T], F32), bias=dram("bias_d", [H, T], F32),
                   bparts=dram("bparts_d", [PARTS, H, T], BF16), parts=dram("parts_d", [PARTS, P, T], BF16),
                   shift=dram("shift_d", [PARTS, H, T], BF16), fb=dram("fb_d", [PARTS, FB_UNITS, P], BF16),
                   x2T=dram("x2T_d", [NB, D, T], F32), cT=dram("cT_d", [NB, PARTS * NX, T], BF16))
    with ExitStack() as ctx:
        def sb(name, shape, dt):
            return ctx.enter_context(nc.sbuf_tensor(name, shape, dt))

        psum = ctx.enter_context(nc.psum_tensor("psum", [P, 8 * BANK], F32))
        pool = dict(H_all=sb("H_all", [P, NB * NCH, D], F32), ident=sb("ident", [P, P], F32),
                    ident_bf=sb("ident_bf", [P, P], BF16), bmax=sb("bmax", [H, 1], F32))
        with ExitStack() as ctx2:
            pool["KA"] = ctx2.enter_context(nc.sbuf_tensor("KA", [P, H, T], BF16))
            pool["QA"] = ctx2.enter_context(nc.sbuf_tensor("QA", [P, H, T], BF16))
            edge_bias(nc, pool, io, psum, scratch)
            attention(nc, pool, io, psum, scratch)
        experts(nc, pool, io, psum, scratch, out)


def kernel(x, L0_tok_W, L0_tok_b, L0_tok_pos_embed, L0_attn_edge_index, L0_attn_edge_attr, L0_attn_Wq, L0_attn_bq,
           L0_attn_Wk, L0_attn_bk, L0_attn_Wv, L0_attn_bv, L0_attn_Wo, L0_attn_bo, L0_attn_We, L0_attn_be,
           L0_ffn_router_w, L0_ffn_w1, L0_ffn_b1, L0_ffn_w2, L0_ffn_b2):
    import numpy as np
    import concourse.bacc as bacc
    from concourse.bass_utils import run_bass_kernel_spmd

    def laid(a):
        return np.ascontiguousarray(a)

    x = np.asarray(x)
    side = HD
    mp, fp = x.shape[2] // side, x.shape[3] // side
    patches = x[:, 0].reshape(NB, mp, side, fp, side).transpose(0, 2, 4, 1, 3).reshape(NB, D, T)
    w1 = np.asarray(L0_ffn_w1)
    arrays = dict(
        xT=laid(patches), tok_WT=laid(np.asarray(L0_tok_W).T), tok_b=laid(L0_tok_b),
        pos=laid(np.asarray(L0_tok_pos_embed).reshape(NCH, P, D).transpose(1, 0, 2)),
        tgt=laid(np.asarray(L0_attn_edge_index)[1].reshape(EC, P).T), edge_attr=laid(L0_attn_edge_attr),
        Wq=laid(L0_attn_Wq), bq=laid(L0_attn_bq), Wk=laid(L0_attn_Wk), bk=laid(L0_attn_bk),
        Wv=laid(L0_attn_Wv), bv=laid(L0_attn_bv), Wo=laid(L0_attn_Wo), bo=laid(L0_attn_bo),
        We=laid(L0_attn_We), be=laid(L0_attn_be), router_wT=laid(np.asarray(L0_ffn_router_w).T),
        w1=laid(w1.transpose(1, 0, 2).reshape(D, NX * D)),
        b1=laid(np.asarray(L0_ffn_b1).reshape(NX // 2, P).T),
        w2=laid(np.asarray(L0_ffn_w2).reshape(NX // 2, P, D).transpose(1, 0, 2)), b2=laid(L0_ffn_b2))
    nc = bacc.Bacc("TRN2", target_bir_lowering=False, num_devices=1)
    args = {n: nc.dram_tensor(f"in_{n}", a.shape, mybir.dt.from_np(a.dtype), kind="ExternalInput").ap()
            for n, a in arrays.items()}
    out = nc.dram_tensor("out_h", (NB, T, D), F32, kind="ExternalOutput").ap()
    vit_tower(nc, **args, out=out)
    r = run_bass_kernel_spmd(nc, [{f"in_{n}": a for n, a in arrays.items()}], core_ids=[0])
    return r.results[0]["out_h"]
```

```python
import concourse.bass as bass
from concourse import mybir
from contextlib import ExitStack

F32 = mybir.dt.float32
BF16 = mybir.dt.bfloat16
I32 = mybir.dt.int32
ALU = mybir.AluOpType
ACT = mybir.ActivationFunctionType
AX = mybir.AxisListType

P = 128
NB = 16
T = 1024
D = 64
H = 8
HD = D // H
NCH = T // P
E = 16384
EC = E // P
NX = 8

EPS = 1e-5
BANK = 512

PARTS = 3
PART_ROWS = PARTS * PARTS * HD
BIAS_ROW = PART_ROWS
SHIFT_ROW = PART_ROWS + PARTS
SCORE_ROWS = SHIFT_ROW + PARTS

QUADS = 2 * 2 * NCH
BLOCKS = 2 * QUADS
GROUPS = 4
LAG = 2
SCORE_BUFS = 3
PROB_BUFS = 8
EVAC_SLOTS = {8 * g + 7 + LAG: g for g in range(3)}
LAST_EVAC_SLOT = LAG - 1
AUX_SLOTS = {2: ["embed"], 5: ["out_proj"], 9: ["norm_t0"], 10: ["norm_t1"], 11: ["qk0"], 12: ["qk1"],
             13: ["v"], 18: ["sq"], 22: ["post_t0"], 23: ["post_t1"], 24: ["router"], 25: ["flag"],
             30: ["combine_t"]}
PREP = ["embed", "norm_t0", "norm_t1", "qk0", "qk1", "v", "sq", "flag"]
POST = ["out_proj", "post_t0", "post_t1", "router", "combine_t"]
ROUTER_EXP_BLOCK = 53
COMBINE_SLOT = 25
RQ_LIMIT = 31.0
TINY = 1e-30
SECOND = 64
Q_ROWS = SECOND + H


ds = bass.ds

FB_UNITS = 4 * NCH


def steps_of(slot, prep, post):
    return [s for s in AUX_SLOTS.get(slot, []) if (prep and s in PREP) or (post and s in POST)]


def aux_order(prep, post):
    return [s for slot in range(QUADS) for s in steps_of(slot, prep, post)]


def aux_base(b):
    if isinstance(b, int) and b == 0:
        return len(PREP)
    return (len(PREP) + len(POST)) * b + (2 * len(PREP) - len(PREP) - len(POST))


def edge_bias(nc, pool, io, psum, scratch):
    KA, QA, bmax = pool["KA"], pool["QA"], pool["bmax"]
    ctx = ExitStack()
    with ctx:
        def sb(name, shape, dt):
            return ctx.enter_context(nc.sbuf_tensor(name, shape, dt))

        def sem(name):
            return ctx.enter_context(nc.semaphore(name))

        tgt = sb("tgt", [P, EC], I32)
        node_a = sb("node_a", [P, EC], I32)
        node_b = sb("node_b", [P, EC], I32)
        node_af = sb("node_af", [P, EC], F32)
        node_bf = sb("node_bf", [P, EC], F32)
        iota32 = sb("iota32", [P, 32], F32)
        exp_bits = sb("exp_bits", [P, 1], I32)
        hot_a = sb("hot_a", [P, EC, 2, 32], BF16)
        hot_b = sb("hot_b", [P, EC, 32], BF16)
        exps = sb("exps", [64, EC * 32], I32)
        base = sb("base", [64, EC * 32], F32)
        key = sb("key", [64, EC * 32], F32)
        win2 = sb("win2", [64, 32], F32)
        win_hi = sb("win_hi", [32, 32], F32)
        win = sb("win", [32, 32], F32)
        winp = sb("winp", [P, NCH], F32)
        valid = sb("valid", [P, NCH], F32)
        first = sb("first", [P, NCH], F32)
        idx = sb("idx", [P, NCH], I32)
        attr = sb("attr", [P, NCH, 3], F32)
        we = sb("we", [P, 3, H], F32)
        be = sb("be", [P, H], F32)
        term = sb("term", [P, NCH, H], F32)
        bias = sb("bias", [P, NCH, H], F32)
        bias_hj = sb("bias_hj", [P, H, NCH], F32)
        biasT = sb("biasT", [D, P], F32)
        rows = sb("rows", [H, T], F32)
        rest = sb("rest", [H, T], F32)
        rest2 = sb("rest2", [H, T], F32)
        bparts = sb("bparts", [H, PARTS, T], BF16)

        s_load = sem("e_load")
        s_iota = sem("e_iota")
        s_ident = sem("e_ident")
        s_hot = sem("e_hot")
        s_sum = sem("e_sum")
        s_win = sem("e_win")
        s_winp = sem("e_winp")
        s_idx = sem("e_idx")
        s_gather = sem("e_gather")
        s_bias = sem("e_bias")
        s_biasT = sem("e_biasT")
        s_rows_out = sem("e_rows_out")
        s_rows = sem("e_rows")
        s_parts = sem("e_parts")
        s_done = sem("e_done")
        s_chain = sem("e_chain")
        win_d, bias_d, bparts_d = scratch["win"], scratch["bias"], scratch["bparts"]

        with nc.Block() as block:
            @block.sync
            def _(sp):
                sp.dma_start(tgt[:, :], io["tgt"]).then_inc(s_load, 16)
                sp.dma_start(we[:, :, :], io["We"].rearrange("c h -> (c h)").partition_broadcast(P)).then_inc(s_load, 16)
                sp.dma_start(be[:, :], io["be"].partition_broadcast(P)).then_inc(s_load, 16)
                sp.wait_ge(s_win, 1)
                sp.dma_start(win_d.rearrange("(a b) -> a b", b=32), win[:, :]).then_inc(s_winp, 16)
                sp.wait_ge(s_winp, 16)
                with nc.allow_non_contiguous_dma(reason="1024 words, once"):
                    sp.dma_start(winp[:, :], win_d.rearrange("(c p) -> p c", p=P)).then_inc(s_winp, 16)
                sp.wait_ge(s_biasT, 1)
                sp.dma_start(bias_d.rearrange("h (c p) -> (h c) p", p=P), biasT[:, :]).then_inc(s_rows_out, 16)
                sp.wait_ge(s_rows_out, 16)
                sp.dma_start(rows[:, :], bias_d).then_inc(s_rows, 16)
                sp.wait_ge(s_parts, 1)
                sp.dma_start(bparts_d.rearrange("c h j -> h c j"), bparts[:, :, :]).then_inc(s_done, 16)
                sp.wait_ge(s_done, 16)
                sp.dma_start(KA[BIAS_ROW:BIAS_ROW + PARTS, :, :], bparts_d).then_inc(s_done, 16)
                sp.wait_ge(s_done, 32)

            @block.gpsimd
            def _(g):
                g.iota(iota32[:, :], pattern=[[1, 32]], base=0, channel_multiplier=0,
                       allow_small_or_imprecise_dtypes=True).then_inc(s_iota, 1)
                for half in range(2):
                    g.wait_ge(s_iota, 1 + half)
                    g.iota(exp_bits[64 * half:64 * half + 64, :], pattern=[[0, 1]], base=127,
                           channel_multiplier=2).then_inc(s_iota, 1)
                for half in range(2):
                    g.wait_ge(s_iota, 3 + half)
                    g.iota(base[32 * half:32 * half + 32, :], pattern=[[P, EC], [0, 32]], base=64 * half,
                           channel_multiplier=0, allow_small_or_imprecise_dtypes=True).then_inc(s_iota, 1)
                ident, ident_bf = pool["ident"], pool["ident_bf"]
                g.wait_ge(s_iota, 5)
                g.memset(ident[:, :], 0.0).then_inc(s_ident, 1)
                g.wait_ge(s_ident, 1)
                g.affine_select(out=ident[:, :], in_=ident[:, :], compare_op=ALU.not_equal, fill=1.0, base=0,
                                pattern=[[-1, P]], channel_multiplier=1).then_inc(s_ident, 1)
                g.wait_ge(s_ident, 2)
                g.tensor_copy(ident_bf[:, :], ident[:, :]).then_inc(s_ident, 1)
                g.wait_ge(s_idx, 1)
                for c in range(NCH):
                    g.indirect_dma_start(out=attr[:, c, :], out_offset=None, in_=io["edge_attr"],
                                         in_offset=bass.IndirectOffsetOnAxis(ap=idx[:, c:c + 1], axis=0)
                                         ).then_inc(s_gather, 16)

            @block.vector
            def _(v):
                count = [0]

                def link(ins):
                    count[0] += 1
                    ins.then_inc(s_chain, 1)
                    v.wait_ge(s_chain, count[0])

                v.memset(hot_a[:, :, :, :], 0.0)
                v.memset(KA[64:P, :, :], 1.0)
                v.memset(QA[64:P, :, :], 1.0)
                v.wait_ge(s_load, 48)
                v.wait_ge(s_iota, 5)
                v.tensor_scalar(node_a[:, :], tgt[:, :], 5, None, ALU.logical_shift_right)
                link(v.tensor_scalar(node_b[:, :], tgt[:, :], 31, None, ALU.bitwise_and))
                v.tensor_copy(node_af[:, :], node_a[:, :])
                v.tensor_copy(node_bf[:, :], node_b[:, :])
                link(v.tensor_scalar(exp_bits[:, :], exp_bits[:, :], 23, None, ALU.logical_shift_left))
                for g in range(2):
                    q = slice(64 * g, 64 * g + 64)
                    v.tensor_tensor(hot_a[q, :, g, :], node_af[q, :].unsqueeze(2).broadcast_to([64, EC, 32]),
                                    iota32[q, :].unsqueeze(1).broadcast_to([64, EC, 32]), ALU.is_equal)
                link(v.tensor_tensor(hot_b[:, :, :], node_bf[:, :].unsqueeze(2).broadcast_to([P, EC, 32]),
                                     iota32[:, :].unsqueeze(1).broadcast_to([P, EC, 32]), ALU.is_equal))
                v.tensor_scalar(hot_b[:, :, :], hot_b[:, :, :], exp_bits[:, 0:1].bitcast(F32), None,
                                ALU.mult).then_inc(s_hot, 1)
                v.wait_ge(s_sum, 8)
                sums = psum[0:64, :].bitcast(I32)
                link(v.tensor_scalar(exps[:, :], sums, 23, None, ALU.logical_shift_right))
                link(v.scalar_tensor_tensor(key[:, :], exps[:, :], 0.5, base[:, :], ALU.mult, ALU.add))
                link(v.tensor_scalar(key[:, :], key[:, :], -62.5, None, ALU.add))
                link(v.scalar_tensor_tensor(base[:, :], exps[:, :], 0.0, key[:, :], ALU.is_gt, ALU.mult))
                link(v.tensor_reduce(win2[:, :], base[:, :].rearrange("p (m b) -> p b m", b=32), AX.X, ALU.max))
                link(v.tensor_copy(win_hi[:, :], win2[32:64, :]))
                v.tensor_tensor(win[:, :], win2[0:32, :], win_hi[:, :], ALU.max).then_inc(s_win, 1)
                v.wait_ge(s_winp, 32)
                v.tensor_scalar(valid[:, :], winp[:, :], 0.0, None, ALU.is_gt)
                link(v.tensor_scalar(first[:, :], winp[:, :], -1.0, 0.0, ALU.add, ALU.max))
                v.tensor_copy(idx[:, :], first[:, :]).then_inc(s_idx, 1)
                v.wait_ge(s_gather, 16 * NCH)
                for c in range(3):
                    dst = bias if c == 0 else term
                    link(v.tensor_tensor(dst[:, :, :], attr[:, :, c:c + 1].broadcast_to([P, NCH, H]),
                                         we[:, c, :].unsqueeze(1).broadcast_to([P, NCH, H]), ALU.mult))
                    if c:
                        link(v.tensor_tensor(bias[:, :, :], bias[:, :, :], term[:, :, :], ALU.add))
                link(v.tensor_tensor(bias[:, :, :], bias[:, :, :],
                                     be[:, :].unsqueeze(1).broadcast_to([P, NCH, H]), ALU.add))
                v.tensor_tensor(bias_hj[:, :, :].rearrange("p h c -> p c h"), bias[:, :, :],
                                valid[:, :].unsqueeze(2).broadcast_to([P, NCH, H]), ALU.mult).then_inc(s_bias, 1)
                v.wait_ge(s_sum, 9)
                v.tensor_copy(biasT[:, :], psum[0:D, 0:P]).then_inc(s_biasT, 1)
                v.wait_ge(s_rows, 16)
                v.reduce_max(bmax[:, :], rows[:, :], AX.X)
                link(v.tensor_copy(bparts[:, 0, :], rows[:, :]))
                link(v.tensor_tensor(rest[:, :], rows[:, :], bparts[:, 0, :], ALU.subtract))
                link(v.tensor_copy(bparts[:, 1, :], rest[:, :]))
                v.tensor_tensor(bparts[:, 2, :], rest[:, :], bparts[:, 1, :], ALU.subtract).then_inc(s_parts, 1)

            @block.tensor
            def _(pe):
                pe.wait_ge(s_hot, 1)
                for m in range(EC):
                    last = pe.matmul(psum[0:64, 32 * m:32 * m + 32], hot_a[:, m, :, :].rearrange("p g a -> p (g a)"),
                                     hot_b[:, m, :], start=True, stop=True)
                    if m % 16 == 15:
                        last.then_inc(s_sum, 1)
                pe.wait_ge(s_ident, 2)
                pe.wait_ge(s_bias, 1)
                pe.transpose(psum[0:D, 0:P], bias_hj[:, :, :].rearrange("p h c -> p (h c)"),
                             pool["ident"][:, :]).then_inc(s_sum, 1)


def attention(nc, pool, io, psum, scratch):
    KA, QA, H_all, bmax, ident, ident_bf = (pool[k] for k in ("KA", "QA", "H_all", "bmax", "ident", "ident_bf"))
    parts_d, shift_d, fb_d = scratch["parts"], scratch["shift"], scratch["fb"]
    x2T_d, cT_d = scratch["x2T"], scratch["cT"]
    ctx = ExitStack()
    with ctx:
        def sb(name, shape, dt):
            return ctx.enter_context(nc.sbuf_tensor(name, shape, dt))

        def sem(name):
            return ctx.enter_context(nc.semaphore(name))

        w_tok = sb("w_tok", [D, D], F32)
        w_qk = sb("w_qk", [D, 2 * D], F32)
        w_v = sb("w_v", [D, D], F32)
        w_o = sb("w_o", [P, D], F32)
        w_r = sb("w_r", [D, NX], F32)
        posb = sb("posb", [P, NCH, D], F32)
        tok_b = sb("tok_b", [P, D], F32)
        b_v = sb("b_v", [P, D], F32)
        b_o = sb("b_o", [P, D], F32)
        b_qk = sb("b_qk", [P, 1], F32)
        scale_qk = sb("scale_qk", [P, 1], F32)
        sel_sq = sb("sel_sq", [P, 2, 32], BF16)
        ones8 = sb("ones8", [H, 1], F32)
        lower = sb("lower", [P, NX, NX], F32)
        neg_half = sb("neg_half", [P, NCH], F32)
        half = sb("half", [H, 1], F32)
        xT = sb("xT", [D, T], F32)
        stats = sb("stats", [P, NCH, 6], F32)
        mv = sb("mv", [P, NCH, 2], F32)
        ve = sb("ve", [P, NCH], F32)
        rstd = sb("rstd", [P, NCH], F32)
        centred = sb("centred", [P, NCH, D], F32)
        xn = sb("xn", [P, NCH, D], F32)
        xnT = sb("xnT", [D, T], F32)
        qk = sb("qk", [P, T], F32)
        qk_rest = sb("qk_rest", [P, T], F32)
        qk_parts = sb("qk_parts", [P, PARTS, T], BF16)
        squares = sb("squares", [P, T], BF16)
        v_new = sb("v_new", [P, NCH, D], F32)
        sq = sb("sq", [P, BANK], F32)
        sq_max = sb("sq_max", [P, 1], F32)
        sq_moved = sb("sq_moved", [H, 3], F32)
        q_sq_max = sb("q_sq_max", [H, 1], F32)
        k_sq_max = sb("k_sq_max", [H, 1], F32)
        rq2 = sb("rq2", [H, 1], F32)
        rq = sb("rq", [H, 1], F32)
        coef = sb("coef", [P, 4], F32)
        excess = sb("excess", [H, 1], F32)
        shift = sb("shift", [Q_ROWS, BANK], F32)
        shift_rest = sb("shift_rest", [Q_ROWS, BANK], F32)
        shift_parts = sb("shift_parts", [Q_ROWS, PARTS, BANK], BF16)
        flags = sb("flags", [1, NB], I32)
        VA = sb("VA", [P, NCH, H, 32], F32)
        probs = sb("probs", [P, PROB_BUFS, 2 * BANK], F32)
        oT = sb("oT", [P, BANK // 32, 32], F32)
        o_inv = sb("o_inv", [P, BANK // 32], F32)
        oT_norm = sb("oT_norm", [P, 2, BANK // 32, 32], F32)
        ON = sb("ON", [P, T], F32)
        h1 = sb("h1", [P, NCH, D], F32)
        p_stats = sb("p_stats", [P, NCH, 6], F32)
        p_mv = sb("p_mv", [P, NCH, 2], F32)
        p_ve = sb("p_ve", [P, NCH], F32)
        p_rstd = sb("p_rstd", [P, NCH], F32)
        p_centred = sb("p_centred", [P, NCH, D], F32)
        x2 = sb("x2", [P, NCH, D], F32)
        x2T = sb("x2T", [D, T], F32)
        logit_max = sb("logit_max", [P, NCH], F32)
        logits = sb("logits", [P, NCH, NX], F32)
        router_e = sb("router_e", [P, NCH, NX], F32)
        r_sum = sb("r_sum", [P, NCH], F32)
        r_inv = sb("r_inv", [P, NCH], F32)
        rprob = sb("rprob", [P, NCH, NX], F32)
        above = sb("above", [P, NCH, NX * NX], F32)
        equal = sb("equal", [P, NCH, NX * NX], F32)
        rank = sb("rank", [P, NCH, NX], F32)
        chosen = sb("chosen", [P, NCH, NX], F32)
        c_sum = sb("c_sum", [P, NCH], F32)
        c_inv = sb("c_inv", [P, NCH], F32)
        comb = sb("comb", [P, NCH, NX], F32)
        comb_rest = sb("comb_rest", [P, NCH, NX], F32)
        comb_parts = sb("comb_parts", [P, NCH, PARTS, NX], BF16)
        cT = sb("cT", [PARTS * NX, T], BF16)
        fb_max = sb("fb_max", [P, FB_UNITS], F32)
        fb_rows = sb("fb_rows", [FB_UNITS, P], F32)
        fb_rest = sb("fb_rest", [FB_UNITS, P], F32)
        fb_parts = sb("fb_parts", [FB_UNITS, PARTS, P], BF16)

        def score_buf(i):
            return psum[:, 2 * BANK * i:2 * BANK * (i + 1)]

        def buf_of(k):
            return 1 if k == BLOCKS - 1 else k % SCORE_BUFS

        def last_use(k):
            return max(j for j in range(k - BLOCKS, k) if buf_of(j % BLOCKS) == buf_of(k))

        o_acc = psum[:, 6 * BANK:7 * BANK]
        aux = psum[:, 7 * BANK:8 * BANK]

        w_loaded = sem("w_loaded")
        stood_alone = sem("stood_alone")
        w_out_loaded = sem("w_out_loaded")
        const_ready = sem("const_ready")
        x_loaded = sem("x_loaded")
        aux_filled = sem("aux_filled")
        aux_drained = sem("aux_drained")
        var_ready = sem("var_ready")
        rstd_ready = sem("rstd_ready")
        xn_ready = sem("xn_ready")
        parts_ready = sem("parts_ready")
        squares_ready = sem("squares_ready")
        rq2_ready = sem("rq2_ready")
        rq_ready = sem("rq_ready")
        excess_ready = sem("excess_ready")
        shift_ready = sem("shift_ready")
        flag_ready = sem("flag_ready")
        parts_stored = sem("parts_stored")
        shift_stored = sem("shift_stored")
        aug_loaded = [sem("aug_loaded_0"), sem("aug_loaded_1")]
        va_ready = sem("va_ready")
        scored = sem("scored")
        exped = sem("exped")
        pv_done = sem("pv_done")
        o_evacuated = sem("o_evacuated")
        on_ready = sem("on_ready")
        p_var_ready = sem("p_var_ready")
        p_rstd_ready = sem("p_rstd_ready")
        x2_ready = sem("x2_ready")
        x2T_stored = sem("x2T_stored")
        router_exped = sem("router_exped")
        comb_ready = sem("comb_ready")
        cT_stored = sem("cT_stored")
        prep_chain = sem("prep_chain")
        post_chain = sem("post_chain")
        evac_chain = sem("evac_chain")
        fb_scored = sem("fb_scored")
        fb_maxed = sem("fb_maxed")
        fb_chain = sem("fb_chain")
        fb_moved = sem("fb_moved")

        WEIGHTS = 11
        AUG_DMAS = 2 * PARTS * PARTS + 1
        FB_SCORED, FB_MAXED, FB_MOVED, FB_CHAIN = FB_UNITS + 1, FB_UNITS + 1, 32, 4
        PREP_CHAIN, POST_CHAIN, EVAC_CHAIN = 16, 20, 6
        EVAC_BASE = (0, 1, 2, 4, EVAC_CHAIN)

        def later(b):
            return not (isinstance(b, int) and b == 0)

        def alone(eng):
            eng.sem_inc(stood_alone, 1)

        def all_batches(eng, prologue, body):
            prologue()
            body(0, True, False)
            with eng.Fori(1, NB - 1) as b:
                body(b, False, False)
            body(NB - 1, False, True)

        with nc.Block() as block:
            @block.sync
            def _(sp):
                for dst, src in ((w_tok[:, :], io["tok_WT"]), (w_qk[:, 0:D], io["Wq"]), (w_qk[:, D:2 * D], io["Wk"]),
                                 (w_v[:, :], io["Wv"]), (w_r[:, :], io["router_wT"]), (posb[:, :, :], io["pos"]),
                                 (tok_b[:, :], io["tok_b"].partition_broadcast(P)),
                                 (b_v[:, :], io["bv"].partition_broadcast(P)),
                                 (b_o[:, :], io["bo"].partition_broadcast(P)),
                                 (b_qk[0:D, :], io["bq"].unsqueeze(1)), (b_qk[D:P, :], io["bk"].unsqueeze(1))):
                    sp.dma_start(dst, src).then_inc(w_loaded, 16)
                sp.wait_ge(const_ready, 1)
                for h in range(H):
                    r = 32 * (h % 4) + HD * (h // 4)
                    sp.dma_start(w_o[r:r + HD, :], io["Wo"][h * HD:(h + 1) * HD, :]).then_inc(w_out_loaded, 16)

                def load_x(bp):
                    sp.dma_start(xT[:, :], io["xT"][bp, :, :]).then_inc(x_loaded, 16)

                def store_parts(bp):
                    sp.wait_ge(parts_ready, bp + 1)
                    sp.dma_start(parts_d.rearrange("a r i -> r a i"), qk_parts[:, :, :]).then_inc(parts_stored, 16)
                    sp.wait_ge(parts_stored, 16 * (bp + 1))
                    alone(sp)

                def store_shift(bp):
                    sp.wait_ge(shift_ready, bp + 1)
                    for n in range(2):
                        sp.dma_start(shift_d[:, :, n * BANK:(n + 1) * BANK].rearrange("a h i -> h a i"),
                                     shift_parts[n * SECOND:n * SECOND + H, :, :]).then_inc(shift_stored, 16)
                    sp.wait_ge(shift_stored, 32 * (bp + 1))
                    alone(sp)

                def load_rows(hg):
                    rows = slice(32 * hg, 32 * hg + 32)
                    krows = slice(D + 32 * hg, D + 32 * hg + 32)
                    hs = slice(4 * hg, 4 * hg + 4)
                    for a in range(PARTS):
                        r = 24 * a
                        for c in range(PARTS):
                            sp.dma_start(QA[r + 8 * c:r + 8 * c + HD, hs, :],
                                         parts_d[a, rows, :].rearrange("(h d) i -> d h i", d=HD)
                                         ).then_inc(aug_loaded[hg], 16)
                            sp.dma_start(KA[r + 8 * c:r + 8 * c + HD, hs, :],
                                         parts_d[c, krows, :].rearrange("(h d) i -> d h i", d=HD)
                                         ).then_inc(aug_loaded[hg], 16)

                def load_shift(hg):
                    hs = slice(4 * hg, 4 * hg + 4)
                    sp.dma_start(QA[SHIFT_ROW:SHIFT_ROW + PARTS, hs, :], shift_d[:, hs, :]).then_inc(aug_loaded[hg], 16)

                def prologue():
                    load_x(0)
                    store_parts(0)
                    load_rows(0)
                    store_shift(0)
                    load_shift(0)
                    load_rows(1)
                    load_shift(1)
                    sp.wait_ge(aux_filled, 1)
                    load_x(1)

                def body(b, first, last, next_x=True):
                    order = aux_order(not last, not first)
                    if not last:
                        for hg in range(2):
                            sp.wait_ge(aug_loaded[hg], 16 * AUG_DMAS * (b + 1))
                            alone(sp)
                        if next_x:
                            sp.wait_ge(aux_filled, aux_base(b) + 1)
                            load_x(b + 2)
                        store_parts(b + 1)
                        sp.wait_ge(scored, BLOCKS * b + BLOCKS // 2)
                        load_rows(0)
                        store_shift(b + 1)
                        load_shift(0)
                    if not first:
                        sp.wait_ge(aux_drained, aux_base(b) + order.index("post_t1") + 1)
                        sp.dma_start(x2T_d[b - 1, :, :], x2T[:, :]).then_inc(x2T_stored, 16)
                    if not first:
                        sp.wait_ge(aux_drained, aux_base(b) + order.index("combine_t") + 1)
                        sp.dma_start(cT_d[b - 1, :, :], cT[:, :]).then_inc(cT_stored, 16)
                    if not last:
                        sp.wait_ge(scored, BLOCKS * (b + 1))
                        load_rows(1)
                        load_shift(1)

                prologue()
                body(0, True, False)
                with sp.Fori(1, NB - 2) as b:
                    body(b, False, False)
                body(NB - 2, False, False, next_x=False)
                body(NB - 1, False, True)
                end = aux_base(NB - 1) + len(POST)
                sp.wait_ge(aux_drained, end + POST.index("post_t1") + 1)
                sp.dma_start(x2T_d[NB - 1, :, :], x2T[:, :]).then_inc(x2T_stored, 16)
                sp.wait_ge(aux_drained, end + POST.index("combine_t") + 1)
                sp.dma_start(cT_d[NB - 1, :, :], cT[:, :]).then_inc(cT_stored, 16)
                sp.wait_ge(x2T_stored, 16 * NB)
                sp.wait_ge(cT_stored, 16 * NB)

            @block.gpsimd
            def _(g):
                def prep_rstd(bp):
                    g.wait_ge(var_ready, bp + 1)
                    g.tensor_tensor(rstd[:, :], ve[:, :], neg_half[:, :], ALU.pow).then_inc(rstd_ready, 1)

                def prep_rq(bp):
                    g.wait_ge(rq2_ready, bp + 1)
                    g.tensor_tensor(rq[:, :], rq2[:, :], half[:, :], ALU.pow).then_inc(rq_ready, 1)

                def copy_v(hg):
                    hs = slice(4 * hg, 4 * hg + 4)
                    src = v_new[:, :, 32 * hg:32 * hg + 32].rearrange("p c (h d) -> p c h d", d=HD)
                    g.tensor_copy(VA[:, :, hs, 0:HD], src).then_inc(va_ready, 1)

                def prologue():
                    g.wait_ge(const_ready, 3)
                    prep_rstd(0)
                    g.wait_ge(aux_drained, PREP.index("v") + 1)
                    copy_v(0)
                    copy_v(1)
                    prep_rq(0)

                def post_pow(bq):
                    g.wait_ge(p_var_ready, bq + 1)
                    g.tensor_tensor(p_rstd[:, :], p_ve[:, :], neg_half[:, :], ALU.pow).then_inc(p_rstd_ready, 1)

                def body(b, first, last):
                    if not last:
                        prep_rstd(b + 1)
                    if not first:
                        post_pow(b - 1)
                    if not last:
                        prep_rq(b + 1)
                        g.wait_ge(aux_drained, aux_base(b) + aux_order(True, not first).index("v") + 1)
                        for hg in range(2):
                            g.wait_ge(pv_done, QUADS * b + 16 * (hg + 1))
                            alone(g)
                            copy_v(hg)

                all_batches(g, prologue, body)
                post_pow(NB - 1)

            @block.scalar
            def _(act):
                def exp_block(b, k):
                    act.wait_ge(scored, BLOCKS * b + k + 1)
                    if k >= PROB_BUFS:
                        act.wait_ge(pv_done, QUADS * b + (k - PROB_BUFS) // 2 + 1)
                    elif later(b):
                        act.wait_ge(pv_done, QUADS * b + (k - PROB_BUFS) // 2 + 1)
                    nc.scalar.activation(probs[:, k % PROB_BUFS, :], score_buf(buf_of(k)),
                                         ACT.Exp).then_inc(exped, 1)

                def router_exp(drained):
                    act.wait_ge(aux_drained, drained)
                    nc.scalar.activation(router_e[:, :, :], logits[:, :, :], ACT.Exp).then_inc(router_exped, 1)

                def fallback(b, hg, flag):
                    with act.If(flag != 0):
                        act.wait_ge(fb_maxed, FB_MAXED * (2 * b + hg + 1))
                        act.dma_start(fb_d.rearrange("a u p -> u a p"), fb_parts[:, :, :]).then_inc(fb_moved, 16)
                        act.wait_ge(fb_moved, FB_MOVED * (2 * b + hg) + 16)
                        act.dma_start(QA[SHIFT_ROW:SHIFT_ROW + PARTS, 4 * hg:4 * hg + 4, :],
                                      fb_d.rearrange("a (h c) p -> a h (c p)", h=4)).then_inc(fb_moved, 16)
                    with act.Else():
                        act.sem_inc(fb_moved, FB_MOVED)

                def body(b, first, last):
                    act.wait_ge(flag_ready, b + 1)
                    flag = act.value_load(flags[0:1, ds(b, 1)], min_val=0, max_val=1)
                    for k in range(BLOCKS):
                        if k % (BLOCKS // 2) == 0:
                            fallback(b, k // (BLOCKS // 2), flag)
                        exp_block(b, k)
                        if k == ROUTER_EXP_BLOCK and not first:
                            router_exp(aux_base(b) + aux_order(not last, True).index("router") + 1)

                all_batches(act, lambda: None, body)
                router_exp(aux_base(NB - 1) + len(POST) + POST.index("router") + 1)

            @block.vector
            def _(v):
                def chain(sem, base, total):
                    count = [0]

                    def link(ins):
                        count[0] += 1
                        ins.then_inc(sem, 1)
                        v.wait_ge(sem, base + count[0])

                    def close():
                        assert count[0] == total, (count[0], total)
                    return link, close

                v.memset(w_o[:, :], 0.0).then_inc(const_ready, 1)
                v.memset(VA[:, :, :, :], 0.0)
                v.memset(oT_norm[:, :, :, :], 0.0)
                v.memset(coef[:, :], 0.0)
                v.memset(sel_sq[:, :, :], 0.0)
                v.memset(scale_qk[0:D, :], HD ** -0.5)
                v.memset(scale_qk[D:P, :], 1.0)
                v.memset(ones8[:, :], 1.0)
                v.memset(half[:, :], 0.5)
                v.memset(neg_half[:, :], -0.5).then_inc(const_ready, 1)
                v.wait_ge(const_ready, 2)
                v.memset(VA[:, :, :, HD:HD + 1], 1.0).then_inc(const_ready, 1)
                v.wait_ge(w_loaded, 16 * WEIGHTS)
                v.tensor_reduce(lower[:, 0, :], ident[:, 0:D].rearrange("p (h d) -> p h d", d=HD), AX.X, ALU.add)
                v.tensor_reduce(lower[:, 1, :], ident[:, D:P].rearrange("p (h d) -> p h d", d=HD), AX.X,
                                ALU.add).then_inc(const_ready, 1)
                v.wait_ge(const_ready, 4)
                v.tensor_copy(sel_sq[:, :, 0:H], lower[:, 0:2, :])
                v.tensor_tensor(posb[:, :, :], posb[:, :, :], tok_b[:, :].unsqueeze(1).broadcast_to([P, NCH, D]),
                                ALU.add).then_inc(const_ready, 1)
                v.wait_ge(const_ready, 5)
                v.memset(lower[:, :, :], 0.0).then_inc(const_ready, 1)
                v.wait_ge(const_ready, 6)
                for e in range(1, NX):
                    last = v.memset(lower[:, e, 0:e], 1.0)
                last.then_inc(const_ready, 1)
                v.wait_ge(const_ready, 7)

                def layernorm(src, stats_, mv_, ve_, centred_, rstd_, dst, link, ready, rstd_done, count, out_sem):
                    for c in range(NCH):
                        last = v.bn_stats(stats_[:, c, :], src(c))
                    link(last)
                    alone(v)
                    for c in range(NCH):
                        last = v.bn_aggr(mv_[:, c, :], stats_[:, c, :])
                    link(last)
                    v.tensor_scalar(ve_[:, :], mv_[:, :, 1], EPS, None, ALU.add).then_inc(ready, 1)
                    link(v.tensor_tensor(centred_[:, :, :], src(None),
                                         mv_[:, :, 0:1].broadcast_to([P, NCH, D]), ALU.subtract))
                    v.wait_ge(rstd_done, count)
                    return v.tensor_tensor(dst[:, :, :], centred_[:, :, :],
                                           rstd_[:, :].unsqueeze(2).broadcast_to([P, NCH, D]),
                                           ALU.mult).then_inc(out_sem, 1)

                def prep_step(step, bp, filled, st):
                    if step == "embed":
                        st["link"], st["close"] = chain(prep_chain, PREP_CHAIN * bp, PREP_CHAIN)
                    link, close = st["link"], st["close"]
                    v.wait_ge(aux_filled, filled)
                    if step == "embed":
                        v.tensor_tensor(H_all[:, ds(bp * NCH, NCH), :], aux.rearrange("p (c e) -> p c e", e=D),
                                        posb[:, :, :], ALU.add).then_inc(aux_drained, 1)
                        v.wait_ge(aux_drained, filled)
                        alone(v)
                        layernorm(lambda c: H_all[:, ds(bp * NCH + c, 1), :] if c is not None
                                  else H_all[:, ds(bp * NCH, NCH), :], stats, mv, ve, centred, rstd, xn, link, var_ready, rstd_ready, bp + 1, xn_ready)
                    elif step in ("norm_t0", "norm_t1"):
                        n = int(step[-1])
                        v.tensor_copy(xnT[:, n * BANK:(n + 1) * BANK], aux[0:D, :]).then_inc(aux_drained, 1)
                    elif step in ("qk0", "qk1"):
                        n = int(step[-1])
                        v.tensor_scalar(qk[:, n * BANK:(n + 1) * BANK], aux, b_qk[:, 0:1], scale_qk[:, 0:1],
                                        ALU.add, ALU.mult).then_inc(aux_drained, 1)
                    elif step == "v":
                        if later(bp):
                            v.wait_ge(va_ready, 2 * bp)
                        v.tensor_tensor(v_new[:, :, :], aux.rearrange("p (c e) -> p c e", e=D),
                                        b_v[:, :].unsqueeze(1).broadcast_to([P, NCH, D]),
                                        ALU.add).then_inc(aux_drained, 1)
                        v.wait_ge(aux_drained, filled)
                        if later(bp):
                            v.wait_ge(parts_stored, 16 * bp)
                        link(v.tensor_copy(qk_parts[:, 0, :], qk[:, :]))
                        link(v.tensor_tensor(qk_rest[:, :], qk[:, :], qk_parts[:, 0, :], ALU.subtract))
                        v.tensor_tensor(squares[:, :], qk_parts[:, 0, :], qk_parts[:, 0, :],
                                        ALU.mult).then_inc(squares_ready, 1)
                        link(v.tensor_copy(qk_parts[:, 1, :], qk_rest[:, :]))
                        v.tensor_tensor(qk_parts[:, 2, :], qk_rest[:, :], qk_parts[:, 1, :],
                                        ALU.subtract).then_inc(parts_ready, 1)
                    elif step == "sq":
                        v.tensor_copy(sq[:, :], aux)
                        v.reduce_max(sq_max[:, :], aux, AX.X).then_inc(aux_drained, 1)
                        v.wait_ge(aux_drained, filled)
                        alone(v)
                        v.tensor_copy(sq_moved[:, 0:1], sq_max[SECOND:SECOND + H, :])
                        v.tensor_copy(sq_moved[:, 1:2], sq_max[32:32 + H, :])
                        link(v.tensor_copy(sq_moved[:, 2:3], sq_max[32 + SECOND:32 + SECOND + H, :]))
                        v.tensor_tensor(q_sq_max[:, :], sq_max[0:H, :], sq_moved[:, 0:1], ALU.max)
                        link(v.tensor_tensor(k_sq_max[:, :], sq_moved[:, 1:2], sq_moved[:, 2:3], ALU.max))
                        v.tensor_tensor(rq2[:, :], q_sq_max[:, :], k_sq_max[:, :], ALU.mult).then_inc(rq2_ready, 1)
                        link(v.tensor_scalar(coef[0:H, 0:1], q_sq_max[:, :], TINY, None, ALU.max))
                        link(v.reciprocal(coef[0:H, 1:2], coef[0:H, 0:1]))
                        v.wait_ge(rq_ready, bp + 1)
                        v.tensor_scalar(excess[:, :], rq[:, :], RQ_LIMIT, None, ALU.is_gt
                                        ).then_inc(excess_ready, 1)
                        v.tensor_scalar(coef[0:H, 2:3], rq[:, :], 0.5, bmax[:, 0:1], ALU.mult, ALU.add)
                        link(v.scalar_tensor_tensor(coef[0:H, 3:4], coef[0:H, 1:2], -0.5, rq[:, :],
                                                    ALU.mult, ALU.mult))
                        link(v.tensor_copy(coef[SECOND:SECOND + H, 2:4], coef[0:H, 2:4]))
                        link(v.tensor_scalar(shift[:, :], sq[0:Q_ROWS, :], coef[0:Q_ROWS, 3:4],
                                             coef[0:Q_ROWS, 2:3], ALU.mult, ALU.subtract))
                        if later(bp):
                            v.wait_ge(shift_stored, 32 * bp)
                        link(v.tensor_copy(shift_parts[:, 0, :], shift[:, :]))
                        link(v.tensor_tensor(shift_rest[:, :], shift[:, :], shift_parts[:, 0, :], ALU.subtract))
                        link(v.tensor_copy(shift_parts[:, 1, :], shift_rest[:, :]))
                        close()
                        v.tensor_tensor(shift_parts[:, 2, :], shift_rest[:, :], shift_parts[:, 1, :],
                                        ALU.subtract).then_inc(shift_ready, 1)
                    else:
                        v.tensor_scalar(flags[0:1, ds(bp, 1)], aux[0:1, 0:1], 1.0, None,
                                        ALU.min).then_inc(aux_drained, 1)
                        v.wait_ge(aux_drained, filled)
                        v.sem_inc(flag_ready, 1)

                def post_step(step, bq, filled, st):
                    if step == "out_proj":
                        st["plink"], st["pclose"] = chain(post_chain, POST_CHAIN * bq, POST_CHAIN)
                    link, close = st["plink"], st["pclose"]
                    v.wait_ge(aux_filled, filled)
                    hq = H_all[:, ds(bq * NCH, NCH), :]
                    if step == "out_proj":
                        v.tensor_tensor(h1[:, :, :], aux.rearrange("p (c e) -> p c e", e=D), hq,
                                        ALU.add).then_inc(aux_drained, 1)
                        v.wait_ge(aux_drained, filled)
                        link(v.tensor_tensor(h1[:, :, :], h1[:, :, :], b_o[:, :].unsqueeze(1).broadcast_to([P, NCH, D]),
                                             ALU.add))
                        layernorm(lambda c: h1[:, c, :] if c is not None else h1[:, :, :], p_stats, p_mv, p_ve,
                                  p_centred, p_rstd, x2, link, p_var_ready, p_rstd_ready, bq + 1, x2_ready)
                        v.wait_ge(x2_ready, bq + 1)
                        v.tensor_tensor(hq, h1[:, :, :], x2[:, :, :], ALU.add)
                    elif step in ("post_t0", "post_t1"):
                        n = int(step[-1])
                        if n == 0 and later(bq):
                            v.wait_ge(x2T_stored, 16 * bq)
                        v.tensor_copy(x2T[:, n * BANK:(n + 1) * BANK], aux[0:D, :]).then_inc(aux_drained, 1)
                    elif step == "router":
                        raw = aux[:, 0:NCH * NX].rearrange("p (c e) -> p c e", e=NX)
                        link(v.tensor_reduce(logit_max[:, :], raw, AX.X, ALU.max))
                        v.tensor_tensor(logits[:, :, :], raw, logit_max[:, :].unsqueeze(2).broadcast_to([P, NCH, NX]),
                                        ALU.subtract).then_inc(aux_drained, 1)
                    else:
                        if later(bq):
                            v.wait_ge(cT_stored, 16 * bq)
                        v.tensor_copy(cT[:, :], aux[0:PARTS * NX, :].bitcast(BF16)).then_inc(aux_drained, 1)

                def combine(bq, st):
                    link, close = st["plink"], st["pclose"]
                    v.wait_ge(router_exped, bq + 1)
                    link(v.tensor_reduce(r_sum[:, :], router_e[:, :, :], AX.X, ALU.add))
                    link(v.reciprocal(r_inv[:, :], r_sum[:, :]))
                    link(v.tensor_tensor(rprob[:, :, :], router_e[:, :, :],
                                         r_inv[:, :].unsqueeze(2).broadcast_to([P, NCH, NX]), ALU.mult))
                    other = rprob[:, :, :].unsqueeze(2).broadcast_to([P, NCH, NX, NX])
                    own = rprob[:, :, :].unsqueeze(3).broadcast_to([P, NCH, NX, NX])
                    v.tensor_tensor(above[:, :, :].rearrange("p c (e f) -> p c e f", f=NX), other, own, ALU.is_gt)
                    last = v.tensor_tensor(equal[:, :, :].rearrange("p c (e f) -> p c e f", f=NX), other, own,
                                           ALU.is_equal)
                    link(last)
                    link(v.tensor_tensor(equal[:, :, :], equal[:, :, :],
                                         lower[:, :, :].rearrange("p e f -> p (e f)").unsqueeze(1).broadcast_to(
                                             [P, NCH, NX * NX]), ALU.mult))
                    link(v.tensor_tensor(above[:, :, :], above[:, :, :], equal[:, :, :], ALU.add))
                    link(v.tensor_reduce(rank[:, :, :], above[:, :, :].rearrange("p c (e f) -> p c e f", f=NX),
                                         AX.X, ALU.add))
                    link(v.scalar_tensor_tensor(chosen[:, :, :], rank[:, :, :], 2.0, rprob[:, :, :],
                                                ALU.is_lt, ALU.mult))
                    link(v.tensor_reduce(c_sum[:, :], chosen[:, :, :], AX.X, ALU.add))
                    link(v.tensor_scalar(c_inv[:, :], c_sum[:, :], 1e-12, None, ALU.max))
                    link(v.reciprocal(c_sum[:, :], c_inv[:, :]))
                    link(v.tensor_tensor(comb[:, :, :], chosen[:, :, :],
                                         c_sum[:, :].unsqueeze(2).broadcast_to([P, NCH, NX]), ALU.mult))
                    link(v.tensor_copy(comb_parts[:, :, 0, :], comb[:, :, :]))
                    link(v.tensor_tensor(comb_rest[:, :, :], comb[:, :, :], comb_parts[:, :, 0, :], ALU.subtract))
                    link(v.tensor_copy(comb_parts[:, :, 1, :], comb_rest[:, :, :]))
                    close()
                    v.tensor_tensor(comb_parts[:, :, 2, :], comb_rest[:, :, :], comb_parts[:, :, 1, :],
                                    ALU.subtract).then_inc(comb_ready, 1)

                def evacuate(b, g):
                    hg, ih = g // 2, g % 2
                    link, close = chain(evac_chain, EVAC_CHAIN * b + EVAC_BASE[g], EVAC_BASE[g + 1] - EVAC_BASE[g])
                    if later(b) or g:
                        v.wait_ge(on_ready, GROUPS * b + g)
                    v.wait_ge(pv_done, QUADS * b + 8 * g + 8)
                    v.transpose(oT[:, :, :].rearrange("p j r -> p (j r)"), o_acc).then_inc(o_evacuated, 1)
                    v.wait_ge(o_evacuated, GROUPS * b + g + 1)
                    alone(v)
                    link(v.reciprocal(o_inv[:, :], oT[:, :, HD]))
                    last = v.tensor_tensor(oT_norm[:, ih, :, HD * hg:HD * hg + HD], oT[:, :, 0:HD],
                                           o_inv[:, :].unsqueeze(2).broadcast_to([P, BANK // 32, HD]), ALU.mult)
                    if hg:
                        link(last)
                        v.transpose(ON[:, ih * BANK:(ih + 1) * BANK],
                                    oT_norm[:, ih, :, :].rearrange("p j r -> p (j r)")).then_inc(on_ready, 1)
                    else:
                        last.then_inc(on_ready, 1)
                    close()

                def fallback(b, hg, flag):
                    base = 2 * b + hg
                    with v.If(flag != 0):
                        for u in range(FB_UNITS):
                            v.wait_ge(fb_scored, FB_SCORED * base + u + 1)
                            v.tensor_reduce(fb_max[:, u:u + 1], score_buf(u % 2), AX.X, ALU.max,
                                            negate=True).then_inc(fb_maxed, 1)
                        v.wait_ge(fb_scored, FB_SCORED * base + FB_UNITS + 1)
                        v.tensor_copy(fb_rows[:, :], psum[0:FB_UNITS, 4 * BANK:4 * BANK + P]).then_inc(fb_chain, 1)
                        v.wait_ge(fb_chain, FB_CHAIN * base + 1)
                        v.tensor_copy(fb_parts[:, 0, :], fb_rows[:, :]).then_inc(fb_chain, 1)
                        v.wait_ge(fb_chain, FB_CHAIN * base + 2)
                        v.tensor_tensor(fb_rest[:, :], fb_rows[:, :], fb_parts[:, 0, :],
                                        ALU.subtract).then_inc(fb_chain, 1)
                        v.wait_ge(fb_chain, FB_CHAIN * base + 3)
                        v.tensor_copy(fb_parts[:, 1, :], fb_rest[:, :]).then_inc(fb_chain, 1)
                        v.wait_ge(fb_chain, FB_CHAIN * base + 4)
                        v.tensor_tensor(fb_parts[:, 2, :], fb_rest[:, :], fb_parts[:, 1, :],
                                        ALU.subtract).then_inc(fb_maxed, 1)
                    with v.Else():
                        v.sem_inc(fb_maxed, FB_MAXED)
                        v.sem_inc(fb_chain, FB_CHAIN)

                def prologue():
                    st = {}
                    for i, step in enumerate(PREP):
                        prep_step(step, 0, i + 1, st)

                def body(b, first, last):
                    v.wait_ge(flag_ready, b + 1)
                    flag = v.value_load(flags[0:1, ds(b, 1)], min_val=0, max_val=1)
                    order = aux_order(not last, not first)
                    st = {}
                    for slot in range(QUADS):
                        if slot == 0:
                            fallback(b, 0, flag)
                        if slot == 16:
                            fallback(b, 1, flag)
                        for step in steps_of(slot, not last, not first):
                            filled = aux_base(b) + order.index(step) + 1
                            if step in PREP:
                                prep_step(step, b + 1, filled, st)
                            else:
                                post_step(step, b - 1, filled, st)
                        if slot == LAST_EVAC_SLOT and not first:
                            evacuate(b - 1, 3)
                        if slot in EVAC_SLOTS:
                            evacuate(b, EVAC_SLOTS[slot])
                        if slot == COMBINE_SLOT and not first:
                            combine(b - 1, st)

                all_batches(v, prologue, body)
                evacuate(NB - 1, 3)
                st = {}
                for i, step in enumerate(POST):
                    if step == "combine_t":
                        combine(NB - 1, st)
                    post_step(step, NB - 1, aux_base(NB) - len(PREP) + i + 1, st)

            @block.tensor
            def _(pe):
                def aux_step(step, n, done, drained):
                    pe.wait_ge(aux_drained, drained) if not (isinstance(drained, int) and drained == 0) else None
                    if step == "embed":
                        pe.wait_ge(x_loaded, 16 * (n + 1))
                        for c in range(NCH):
                            last = pe.matmul(aux[:, c * D:(c + 1) * D], xT[:, c * P:(c + 1) * P], w_tok[:, :],
                                             start=True, stop=True)
                    elif step in ("norm_t0", "norm_t1", "post_t0", "post_t1"):
                        src, ready = (xn, xn_ready) if step[0] == "n" else (x2, x2_ready)
                        pe.wait_ge(ready, n + 1)
                        alone(pe)
                        for c in range(4):
                            last = pe.transpose(aux[0:D, c * P:(c + 1) * P], src[:, 4 * int(step[-1]) + c, :],
                                                ident[:, :])
                    elif step in ("qk0", "qk1"):
                        i = int(step[-1])
                        last = pe.matmul(aux, w_qk[:, :], xnT[:, i * BANK:(i + 1) * BANK], start=True, stop=True)
                    elif step == "v":
                        for c in range(NCH):
                            last = pe.matmul(aux[:, c * D:(c + 1) * D], xnT[:, c * P:(c + 1) * P], w_v[:, :],
                                             start=True, stop=True)
                    elif step == "sq":
                        pe.wait_ge(squares_ready, n + 1)
                        alone(pe)
                        for i in range(2):
                            for w in range(2):
                                r = i * SECOND + 32 * w
                                last = pe.matmul(aux[r:r + 32, :], sel_sq[:, w, :],
                                                 squares[:, i * BANK:(i + 1) * BANK], start=True, stop=True)
                    elif step == "flag":
                        pe.wait_ge(excess_ready, n + 1)
                        alone(pe)
                        last = pe.matmul(aux[0:1, 0:1], excess[:, :], ones8[:, :], start=True, stop=True)
                    elif step == "out_proj":
                        pe.wait_ge(on_ready, GROUPS * (n + 1))
                        for c in range(NCH):
                            last = pe.matmul(aux[:, c * D:(c + 1) * D], ON[:, c * P:(c + 1) * P], w_o[:, :],
                                             start=True, stop=True)
                    elif step == "router":
                        for c in range(NCH):
                            last = pe.matmul(aux[:, c * NX:(c + 1) * NX], x2T[:, c * P:(c + 1) * P], w_r[:, :],
                                             start=True, stop=True)
                    else:
                        pe.wait_ge(comb_ready, n + 1)
                        for c in range(NCH):
                            last = pe.transpose(aux[0:PARTS * NX, :].bitcast(BF16)[:, c * P:(c + 1) * P],
                                                comb_parts[:, c, :, :].rearrange("p a e -> p (a e)"), ident_bf[:, :])
                    last.then_inc(aux_filled, 1)

                def head_of(q, g):
                    return 4 * (q // 16) + g, (q // 8) % 2, q % 8

                def scores(b, q):
                    for g in range(4):
                        k = 2 * q + g // 2
                        if g % 2 == 0:
                            if last_use(k) >= 0 or later(b):
                                pe.wait_ge(exped, BLOCKS * b + last_use(k) + 1)
                        h, ih, jt = head_of(q, g)
                        last = pe.matmul(score_buf(buf_of(k))[:, (g % 2) * BANK:(g % 2 + 1) * BANK],
                                         KA[0:SCORE_ROWS, h, jt * P:(jt + 1) * P],
                                         QA[0:SCORE_ROWS, h, ih * BANK:(ih + 1) * BANK], start=True, stop=True)
                        if g % 2:
                            last.then_inc(scored, 1)

                def values(b, q):
                    pe.wait_ge(exped, BLOCKS * b + 2 * q + 2)
                    if q % 8 == 0 and (later(b) or q):
                        pe.wait_ge(o_evacuated, GROUPS * b + q // 8)
                    if q % 16 == 0:
                        pe.wait_ge(va_ready, 2 * b + q // 16 + 1)
                    for g in range(4):
                        k = 2 * q + g // 2
                        h, ih, jt = head_of(q, g)
                        last = pe.matmul(o_acc[32 * g:32 * g + 32, :], VA[:, jt, h, :],
                                         probs[:, k % PROB_BUFS, (g % 2) * BANK:(g % 2 + 1) * BANK],
                                         start=(jt == 0), stop=(jt == NCH - 1))
                    last.then_inc(pv_done, 1)

                def fallback(b, hg, flag):
                    base = 2 * b + hg
                    with pe.If(flag != 0):
                        if later(b) or hg:
                            pe.wait_ge(exped, BLOCKS * b + BLOCKS // 2 * hg)
                        for u in range(FB_UNITS):
                            if u >= 2:
                                pe.wait_ge(fb_maxed, FB_MAXED * base + u - 1)
                            h, c = 4 * hg + u // NCH, u % NCH
                            for n in range(2):
                                last = pe.matmul(score_buf(u % 2)[:, n * BANK:(n + 1) * BANK],
                                                 QA[0:SHIFT_ROW, h, c * P:(c + 1) * P],
                                                 KA[0:SHIFT_ROW, h, n * BANK:(n + 1) * BANK], start=True, stop=True)
                            last.then_inc(fb_scored, 1)
                        pe.wait_ge(fb_maxed, FB_MAXED * base + FB_UNITS)
                        pe.transpose(psum[0:FB_UNITS, 4 * BANK:4 * BANK + P], fb_max[:, :],
                                     ident[:, :]).then_inc(fb_scored, 1)
                    with pe.Else():
                        pe.sem_inc(fb_scored, FB_SCORED)
                    pe.wait_ge(fb_moved, FB_MOVED * (base + 1))

                def prologue():
                    pe.wait_ge(w_loaded, 16 * WEIGHTS)
                    pe.wait_ge(w_out_loaded, 16 * H)
                    pe.wait_ge(const_ready, 7)
                    for i, step in enumerate(PREP):
                        aux_step(step, 0, i + 1, i)

                def body(b, first, last):
                    pe.wait_ge(flag_ready, b + 1)
                    flag = pe.value_load(flags[0:1, ds(b, 1)], min_val=0, max_val=1)
                    order = aux_order(not last, not first)
                    for q in range(QUADS):
                        if q % 16 == 0:
                            pe.wait_ge(aug_loaded[q // 16], 16 * AUG_DMAS * (b + 1))
                            fallback(b, q // 16, flag)
                        scores(b, q)
                        for step in steps_of(q, not last, not first):
                            i = order.index(step)
                            aux_step(step, b + 1 if step in PREP else b - 1, aux_base(b) + i + 1, aux_base(b) + i)
                        if q >= LAG:
                            values(b, q - LAG)
                        elif not first:
                            values(b - 1, QUADS + q - LAG)

                all_batches(pe, prologue, body)
                for q in range(QUADS - LAG, QUADS):
                    values(NB - 1, q)
                for i, step in enumerate(POST):
                    n = aux_base(NB) - len(PREP) + i
                    aux_step(step, NB - 1, n + 1, n)


def experts(nc, pool, io, psum, scratch, out):
    H_all, ident = pool["H_all"], pool["ident"]
    ctx = ExitStack()
    with ctx:
        def sb(name, shape, dt):
            return ctx.enter_context(nc.sbuf_tensor(name, shape, dt))

        def sem(name):
            return ctx.enter_context(nc.semaphore(name))

        PAIRS = NX // 2
        UNITS = 2 * PAIRS
        KC = PARTS * NX
        w1 = sb("w1", [P, NX * D], F32)
        w2 = sb("w2", [P, PAIRS, D], F32)
        b1 = sb("b1", [P, PAIRS], F32)
        b2 = sb("b2", [KC, D], F32)
        b2_rest = sb("b2_rest", [KC, D], F32)
        b2_parts = sb("b2_parts", [KC, PARTS, D], BF16)
        spread = sb("spread", [KC, PAIRS, P], BF16)
        fold = sb("fold", [P, D], F32)
        x2T = sb("m_x2T", [P, 2, T], F32)
        cT = sb("m_cT", [KC, 2, T], BF16)
        act_h = sb("act_h", [P, 2, BANK], F32)
        gated = sb("gated", [P, PAIRS, BANK], F32)
        yT = sb("yT", [P, 2, BANK], F32)
        result = sb("result", [P, 2, NCH, D], F32)
        hid = [psum[:, i * BANK:(i + 1) * BANK] for i in range(2)]
        wgt = [psum[:, (2 + i) * BANK:(3 + i) * BANK] for i in range(2)]
        ysum = [psum[:, (4 + i) * BANK:(5 + i) * BANK] for i in range(2)]
        ybank = [psum[:, (6 + i) * BANK:(6 + i) * BANK + 4 * D] for i in range(2)]

        loaded = sem("m_loaded")
        zeroed = sem("m_zeroed")
        consts = sem("m_consts")
        tokens = [sem(f"m_tokens_{i}") for i in range(2)]
        hidden = sem("m_hidden")
        weights = sem("m_weights")
        gelued = sem("m_gelued")
        gated_ready = sem("m_gated")
        summed = sem("m_summed")
        yT_moved = sem("m_yT_moved")
        y_ready = sem("m_y")
        y_taken = sem("m_y_taken")
        stored = [sem(f"m_stored_{i}") for i in range(2)]

        b2_ready = sem("m_b2_ready")
        LOADS = 3 + PARTS
        BODY = 2 * UNITS

        with nc.Block() as block:
            @block.sync
            def _(sp):
                def load_tokens(b, s):
                    sp.dma_start(x2T[0:D, s, :], scratch["x2T"][ds(b, 1), :, :].rearrange("o d t -> (o d) t")
                                 ).then_inc(tokens[s], 16)
                    sp.dma_start(cT[:, s, :], scratch["cT"][ds(b, 1), :, :].rearrange("o d t -> (o d) t")
                                 ).then_inc(tokens[s], 16)

                def store(pair, s):
                    sp.wait_ge(y_taken, 4 * pair + 2 * s + 2)
                    sp.dma_start(out[ds(pair * 2 + s, 1), :, :].rearrange("o (c p) e -> p (o c) e", p=P),
                                 result[:, s, :, :]).then_inc(stored[s], 16)

                def body_sp(pair, first, last):
                    for s in range(2):
                        if not last:
                            sp.wait_ge(y_ready, 4 * pair + 2 * s + 2)
                            load_tokens(pair * 2 + 2 + s, s)
                        store(pair, s)

                sp.dma_start(w1[0:D, :], io["w1"]).then_inc(loaded, 16)
                sp.dma_start(w2[:, :, :], io["w2"]).then_inc(loaded, 16)
                sp.dma_start(b1[:, :], io["b1"]).then_inc(loaded, 16)
                for a in range(PARTS):
                    sp.dma_start(b2[a * NX:(a + 1) * NX, :], io["b2"]).then_inc(loaded, 16)
                for s in range(2):
                    load_tokens(s, s)
                body_sp(0, True, False)
                with sp.Fori(1, NB // 2 - 1) as pair:
                    body_sp(pair, False, False)
                body_sp(NB // 2 - 1, False, True)
                for s in range(2):
                    sp.wait_ge(stored[s], 8 * NB)

            @block.gpsimd
            def _(g):
                g.memset(spread[:, :, :], 0.0).then_inc(consts, 1)
                for a in range(PARTS):
                    g.wait_ge(consts, a + 1)
                    view = spread[:, :, :].rearrange("k m (e n) -> k m e n", e=2)
                    g.affine_select(out=view, in_=view, compare_op=ALU.not_equal, fill=1.0, base=-NX * a,
                                    pattern=[[-2, PAIRS], [-1, 2], [0, D]], channel_multiplier=1).then_inc(consts, 1)

            @block.scalar
            def _(act):
                act.wait_ge(loaded, 16 * LOADS)

                def body(pair, first):
                    for i in range(BODY):
                        act.wait_ge(hidden, BODY * pair + i + 1)
                        if i >= 2 or not first:
                            act.wait_ge(gated_ready, BODY * pair + i - 1)
                        nc.scalar.activation(act_h[:, i % 2, :], hid[i % 2], ACT.Gelu,
                                             bias=b1[:, i % PAIRS:i % PAIRS + 1]).then_inc(gelued, 1)

                body(0, True)
                with act.Fori(1, NB // 2) as pair:
                    body(pair, False)

            @block.vector
            def _(v):
                v.memset(w1[D:P, :], 0.0)
                v.memset(x2T[D:P, :, :], 0.0)
                v.tensor_tensor(fold[:, :], ident[:, 0:D], ident[:, D:P], ALU.add).then_inc(zeroed, 1)
                v.wait_ge(loaded, 16 * LOADS)
                for n, ins in enumerate((
                        lambda: v.tensor_copy(b2_parts[:, 0, :], b2[:, :]),
                        lambda: v.tensor_tensor(b2_rest[:, :], b2[:, :], b2_parts[:, 0, :], ALU.subtract),
                        lambda: v.tensor_copy(b2_parts[:, 1, :], b2_rest[:, :]),
                        lambda: v.tensor_tensor(b2_parts[:, 2, :], b2_rest[:, :], b2_parts[:, 1, :], ALU.subtract))):
                    ins().then_inc(b2_ready, 1)
                    v.wait_ge(b2_ready, n + 1)

                def move(pair, half, first):
                    v.wait_ge(summed, 2 * (4 * pair + half) + 2)
                    if not first or half >= 2:
                        v.wait_ge(y_ready, 4 * pair + half - 1)
                    v.tensor_copy(yT[:, half % 2, :], ysum[half % 2]).then_inc(yT_moved, 1)

                def take(pair, half, first):
                    s, hh = (half % 4) // 2, half % 2
                    v.wait_ge(y_ready, 4 * pair + half + 1)
                    if hh == 0 and not first:
                        v.wait_ge(stored[s], 16 * pair)
                    rows = H_all[:, ds((pair * 2) * NCH + 4 * half, 4), :]
                    v.tensor_tensor(result[:, s, 4 * hh:4 * hh + 4, :], ybank[half % 2].rearrange(
                        "p (c e) -> p c e", e=D), rows, ALU.add).then_inc(y_taken, 1)

                def body(pair, first):
                    for i in range(BODY):
                        half = i // PAIRS - 1
                        if i % PAIRS == 2 and (half >= 0 or not first):
                            move(pair, half, first)
                        v.wait_ge(gelued, BODY * pair + i + 1)
                        v.wait_ge(weights, BODY * pair + i + 1)
                        if i >= PAIRS or not first:
                            v.wait_ge(summed, BODY // 2 * pair + (i - PAIRS) // 2 + 1)
                        v.tensor_tensor(gated[:, i % PAIRS, :], act_h[:, i % 2, :], wgt[i % 2],
                                        ALU.mult).then_inc(gated_ready, 1)
                        if i % PAIRS == 3 and (half >= 0 or not first):
                            take(pair, half, first)

                body(0, True)
                with v.Fori(1, NB // 2) as pair:
                    body(pair, False)
                move(NB // 2 - 1, 3, False)
                take(NB // 2 - 1, 3, False)

            @block.tensor
            def _(pe):
                pe.wait_ge(loaded, 16 * LOADS)
                pe.wait_ge(consts, PARTS + 1)
                pe.wait_ge(b2_ready, 4)
                pe.wait_ge(zeroed, 1)

                def sum_two(pair, i, first):
                    half = i // PAIRS
                    pe.wait_ge(gated_ready, BODY * pair + i + 2)
                    if i % PAIRS == 0 and (half >= 2 or not first):
                        pe.wait_ge(yT_moved, 4 * pair + half - 1)
                    for n in range(2):
                        m = i % PAIRS + n
                        last = pe.matmul(ysum[half % 2][n * D:(n + 1) * D, :], w2[:, m, :], gated[:, m, :],
                                         start=(m < 2), stop=(m >= 2))
                    last.then_inc(summed, 1)

                def by_token(pair, half, first):
                    s, hh = (half % 4) // 2, half % 2
                    pe.wait_ge(yT_moved, 4 * pair + half + 1)
                    if half >= 2 or not first:
                        pe.wait_ge(y_taken, 4 * pair + half - 1)
                    for c in range(4):
                        y = ybank[half % 2][:, c * D:(c + 1) * D]
                        pe.matmul(y, yT[:, half % 2, c * P:(c + 1) * P], fold[:, :], start=True, stop=False)
                        for a in range(PARTS):
                            last = pe.matmul(y, cT[:, s, (4 * hh + c) * P:(4 * hh + c + 1) * P], b2_parts[:, a, :],
                                             start=False, stop=(a == PARTS - 1))
                    last.then_inc(y_ready, 1)

                def body(pair, first):
                    for i in range(BODY):
                        half, m = i // PAIRS, i % PAIRS
                        s, cols = half // 2, slice((half % 2) * BANK, (half % 2 + 1) * BANK)
                        if i % UNITS == 0:
                            pe.wait_ge(tokens[s], 32 * pair + 32)
                        if i >= 2 or not first:
                            pe.wait_ge(gelued, BODY * pair + i - 1)
                        pe.matmul(hid[i % 2], w1[:, m * P:(m + 1) * P], x2T[:, s, cols],
                                  start=True, stop=True).then_inc(hidden, 1)
                        if i >= 2 or not first:
                            pe.wait_ge(gated_ready, BODY * pair + i - 1)
                        pe.matmul(wgt[i % 2], spread[:, m, :], cT[:, s, cols],
                                  start=True, stop=True).then_inc(weights, 1)
                        if i % 2 and (i >= 3 or not first):
                            sum_two(pair, i - 3, first)
                        if m == 2 and (half >= 1 or not first):
                            by_token(pair, half - 1, first)

                body(0, True)
                with pe.Fori(1, NB // 2) as pair:
                    body(pair, False)
                sum_two(NB // 2 - 1, BODY - 2, False)
                by_token(NB // 2 - 1, 3, False)


def vit_tower(nc, xT, tok_WT, tok_b, pos, tgt, edge_attr, Wq, bq, Wk, bk, Wv, bv, Wo, bo, We, be, router_wT,
              w1, b1, w2, b2, out):
    io = dict(xT=xT, tok_WT=tok_WT, tok_b=tok_b, pos=pos, tgt=tgt, edge_attr=edge_attr, Wq=Wq, bq=bq, Wk=Wk, bk=bk,
              Wv=Wv, bv=bv, Wo=Wo, bo=bo, We=We, be=be, router_wT=router_wT, w1=w1, b1=b1, w2=w2, b2=b2)

    def dram(name, shape, dt):
        return nc.dram_tensor(name, shape, dt, kind="Internal").ap()

    scratch = dict(win=dram("win_d", [T], F32), bias=dram("bias_d", [H, T], F32),
                   bparts=dram("bparts_d", [PARTS, H, T], BF16), parts=dram("parts_d", [PARTS, P, T], BF16),
                   shift=dram("shift_d", [PARTS, H, T], BF16), fb=dram("fb_d", [PARTS, FB_UNITS, P], BF16),
                   x2T=dram("x2T_d", [NB, D, T], F32), cT=dram("cT_d", [NB, PARTS * NX, T], BF16))
    with ExitStack() as ctx:
        def sb(name, shape, dt):
            return ctx.enter_context(nc.sbuf_tensor(name, shape, dt))

        psum = ctx.enter_context(nc.psum_tensor("psum", [P, 8 * BANK], F32))
        pool = dict(H_all=sb("H_all", [P, NB * NCH, D], F32), ident=sb("ident", [P, P], F32),
                    ident_bf=sb("ident_bf", [P, P], BF16), bmax=sb("bmax", [H, 1], F32))
        with ExitStack() as ctx2:
            pool["KA"] = ctx2.enter_context(nc.sbuf_tensor("KA", [P, H, T], BF16))
            pool["QA"] = ctx2.enter_context(nc.sbuf_tensor("QA", [P, H, T], BF16))
            edge_bias(nc, pool, io, psum, scratch)
            attention(nc, pool, io, psum, scratch)
        experts(nc, pool, io, psum, scratch, out)


def kernel(x, L0_tok_W, L0_tok_b, L0_tok_pos_embed, L0_attn_edge_index, L0_attn_edge_attr, L0_attn_Wq, L0_attn_bq,
           L0_attn_Wk, L0_attn_bk, L0_attn_Wv, L0_attn_bv, L0_attn_Wo, L0_attn_bo, L0_attn_We, L0_attn_be,
           L0_ffn_router_w, L0_ffn_w1, L0_ffn_b1, L0_ffn_w2, L0_ffn_b2):
    import numpy as np
    import concourse.bacc as bacc
    from concourse.bass_utils import run_bass_kernel_spmd

    def laid(a):
        return np.ascontiguousarray(a)

    x = np.asarray(x)
    side = HD
    mp, fp = x.shape[2] // side, x.shape[3] // side
    patches = x[:, 0].reshape(NB, mp, side, fp, side).transpose(0, 2, 4, 1, 3).reshape(NB, D, T)
    w1 = np.asarray(L0_ffn_w1)
    arrays = dict(
        xT=laid(patches), tok_WT=laid(np.asarray(L0_tok_W).T), tok_b=laid(L0_tok_b),
        pos=laid(np.asarray(L0_tok_pos_embed).reshape(NCH, P, D).transpose(1, 0, 2)),
        tgt=laid(np.asarray(L0_attn_edge_index)[1].reshape(EC, P).T), edge_attr=laid(L0_attn_edge_attr),
        Wq=laid(L0_attn_Wq), bq=laid(L0_attn_bq), Wk=laid(L0_attn_Wk), bk=laid(L0_attn_bk),
        Wv=laid(L0_attn_Wv), bv=laid(L0_attn_bv), Wo=laid(L0_attn_Wo), bo=laid(L0_attn_bo),
        We=laid(L0_attn_We), be=laid(L0_attn_be), router_wT=laid(np.asarray(L0_ffn_router_w).T),
        w1=laid(w1.transpose(1, 0, 2).reshape(D, NX * D)),
        b1=laid(np.asarray(L0_ffn_b1).reshape(NX // 2, P).T),
        w2=laid(np.asarray(L0_ffn_w2).reshape(NX // 2, P, D).transpose(1, 0, 2)), b2=laid(L0_ffn_b2))
    nc = bacc.Bacc("TRN2", target_bir_lowering=False, num_devices=1)
    args = {n: nc.dram_tensor(f"in_{n}", a.shape, mybir.dt.from_np(a.dtype), kind="ExternalInput").ap()
            for n, a in arrays.items()}
    out = nc.dram_tensor("out_h", (NB, T, D), F32, kind="ExternalOutput").ap()
    vit_tower(nc, **args, out=out)
    r = run_bass_kernel_spmd(nc, [{f"in_{n}": a for n, a in arrays.items()}], core_ids=[0])
    return r.results[0]["out_h"]
```

```python
import concourse.bass as bass
from concourse import mybir
from contextlib import ExitStack

F32 = mybir.dt.float32
BF16 = mybir.dt.bfloat16
I32 = mybir.dt.int32
ALU = mybir.AluOpType
ACT = mybir.ActivationFunctionType
AX = mybir.AxisListType

P = 128
NB = 16
T = 1024
D = 64
H = 8
HD = D // H
NCH = T // P
E = 16384
EC = E // P
NX = 8

EPS = 1e-5
BANK = 512

PARTS = 3
PART_ROWS = PARTS * PARTS * HD
BIAS_ROW = PART_ROWS
SHIFT_ROW = PART_ROWS + PARTS
SCORE_ROWS = SHIFT_ROW + PARTS

QUADS = 2 * 2 * NCH
BLOCKS = 2 * QUADS
GROUPS = 4
LAG = 2
SCORE_BUFS = 3
PROB_BUFS = 8
EVAC_SLOTS = {8 * g + 7 + LAG: g for g in range(3)}
LAST_EVAC_SLOT = LAG - 1
AUX_SLOTS = {2: ["embed"], 7: ["norm_t0"], 8: ["norm_t1"], 9: ["qk0"], 10: ["qk1"], 11: ["v"], 14: ["sq"],
             18: ["out_proj"], 19: ["flag"], 23: ["post_t0"], 24: ["post_t1"], 25: ["router"], 31: ["combine_t"]}
PREP = ["embed", "norm_t0", "norm_t1", "qk0", "qk1", "v", "sq", "flag"]
POST = ["out_proj", "post_t0", "post_t1", "router", "combine_t"]
ROUTER_EXP_BLOCK = 52
BUF_TURN = 38
PAIRS = NX // 2
UNITS = 2 * PAIRS
KC = PARTS * NX
POST_UNITS = {0: "out_proj", 5: "post_t0", 6: "post_t1", 7: "router", 15: "combine_t"}
ROUTER_UNIT = 7
RANK_UNIT, WEIGH_UNIT = 11, 13
COMBINE_SLOT = 26
RQ_LIMIT = 31.0
TINY = 1e-30
QK_COLS, V_COLS, ROUTER_COLS = slice(0, 2 * D), slice(2 * D, 3 * D), slice(3 * D, 3 * D + NX)
W1_COL = 3 * D + NX
W_COLS = W1_COL + NX * D
TURNS = ((0, 0), (1, 0), (2, 1))
SECOND = 64
Q_ROWS = SECOND + H
ONE_ROW = 31


ds = bass.ds

FB_UNITS = 4 * NCH


def steps_of(slot, prep, post):
    return [s for s in AUX_SLOTS.get(slot, []) if (prep and s in PREP) or (post and s in POST)]


def aux_order(prep, post):
    return [s for slot in range(QUADS) for s in steps_of(slot, prep, post)]


def aux_base(b):
    if isinstance(b, int) and b == 0:
        return len(PREP)
    return (len(PREP) + len(POST)) * b + (2 * len(PREP) - len(PREP) - len(POST))


def attention(nc, pool, io, psum, scratch, out):
    H_all, bmax, ident, ident_bf = (pool[k] for k in ("H_all", "bmax", "ident", "ident_bf"))
    q_parts_d, k_parts_d, shift_d, fb_d = (scratch[k] for k in ("q_parts", "k_parts", "shift", "fb"))
    x2_d, x2_low_d, cT_d = scratch["x2"], scratch["x2_low"], scratch["cT"]
    ctx = ExitStack()
    with ctx:
        def sb(name, shape, dt):
            return ctx.enter_context(nc.sbuf_tensor(name, shape, dt))

        def sem(name):
            return ctx.enter_context(nc.semaphore(name))

        w_o = sb("w_o", [P, D], F32)
        w_parts = sb("w_parts", [P, PARTS, W_COLS], BF16)
        lower = sb("lower", [P, NX, NX], F32)
        neg_half = sb("neg_half", [P, NCH], F32)
        ON = sb("ON", [P, T], F32)
        h1 = sb("h1", [P, NCH, D], F32)
        p_stats = sb("p_stats", [P, NCH, 6], F32)
        p_mv = sb("p_mv", [P, NCH, 2], F32)
        p_ve = sb("p_ve", [P, NCH], F32)
        p_rstd = sb("p_rstd", [P, NCH], F32)
        p_centred = sb("p_centred", [P, NCH, D], F32)
        x2 = sb("x2", [P, NCH, D], F32)
        x2_parts = sb("x2_parts", [P, NCH, 4, D], BF16)
        x2_stacks = sb("x2_stacks", [P, 2, T], BF16)
        logit_max = sb("logit_max", [P, NCH], F32)
        logits = sb("logits", [P, NCH, NX], F32)
        router_e = sb("router_e", [P, NCH, NX], F32)
        r_sum = sb("r_sum", [P, NCH], F32)
        r_inv = sb("r_inv", [P, NCH], F32)
        rprob = sb("rprob", [P, NCH, NX], F32)
        above = sb("above", [P, NCH, NX * NX], F32)
        equal = sb("equal", [P, NCH, NX * NX], F32)
        rank = sb("rank", [P, NCH, NX], F32)
        chosen = sb("chosen", [P, NCH, NX], F32)
        c_sum = sb("c_sum", [P, NCH], F32)
        c_inv = sb("c_inv", [P, NCH], F32)
        comb = sb("comb", [P, NCH, NX], F32)
        comb_rest = sb("comb_rest", [P, NCH, NX], F32)
        comb_parts = sb("comb_parts", [P, NCH, PARTS, NX], BF16)
        cT = sb("cT", [PARTS * NX, T], BF16)
        w2 = sb("w2", [P, PAIRS, D], F32)
        b1 = sb("b1", [P, PAIRS], F32)
        b2 = sb("b2", [KC, D], F32)
        b2_rest = sb("b2_rest", [KC, D], F32)
        b2_parts = sb("b2_parts", [KC, PARTS, D], BF16)
        b2_rows = sb("b2_rows", [PARTS * KC, D], BF16)
        spread = sb("spread", [KC, PAIRS, P], BF16)
        inner = ctx.enter_context(ExitStack())

        def sb(name, shape, dt):
            return inner.enter_context(nc.sbuf_tensor(name, shape, dt))

        QA, KA = sb("QA", [P, H, T], BF16), sb("KA", [P, H, T], BF16)
        w_tok = sb("w_tok", [D, D], F32)
        posb = sb("posb", [P, NCH, D], F32)
        tok_b = sb("tok_b", [P, D], F32)
        b_v = sb("b_v", [P, D], F32)
        b_qk = sb("b_qk", [P, 1], F32)
        scale_qk = sb("scale_qk", [P, 1], F32)
        sel_sq = sb("sel_sq", [P, 2, 32], BF16)
        ones8 = sb("ones8", [H, 1], F32)
        half = sb("half", [H, 1], F32)
        xT = sb("xT", [D, T], F32)
        stats = sb("stats", [P, NCH, 6], F32)
        mv = sb("mv", [P, NCH, 2], F32)
        ve = sb("ve", [P, NCH], F32)
        rstd = sb("rstd", [P, NCH], F32)
        centred = sb("centred", [P, NCH, D], F32)
        xn = sb("xn", [P, NCH, D], F32)
        xn_parts = sb("xn_parts", [P, NCH, 4, D], BF16)
        xn_stacks = sb("xn_stacks", [P, 2, T], BF16)
        qk = sb("qk", [P, T], F32)
        qk_rest = sb("qk_rest", [P, T], F32)
        qk_parts = sb("qk_parts", [P, PARTS, T], BF16)
        squares = sb("squares", [P, T], BF16)
        v_new = sb("v_new", [P, NCH, D], F32)
        sq = sb("sq", [P, BANK], F32)
        sq_max = sb("sq_max", [P, 1], F32)
        sq_moved = sb("sq_moved", [H, 3], F32)
        q_sq_max = sb("q_sq_max", [H, 1], F32)
        k_sq_max = sb("k_sq_max", [H, 1], F32)
        rq2 = sb("rq2", [H, 1], F32)
        rq = sb("rq", [H, 1], F32)
        coef = sb("coef", [P, 4], F32)
        excess = sb("excess", [H, 1], F32)
        shift = sb("shift", [Q_ROWS, BANK], F32)
        shift_rest = sb("shift_rest", [Q_ROWS, BANK], F32)
        shift_parts = sb("shift_parts", [Q_ROWS, PARTS, BANK], BF16)
        flags = sb("flags", [1, NB], I32)
        VA = sb("VA", [P, NCH, H, 32], F32)
        oT = sb("oT", [P, BANK // 32, 32], F32)
        o_inv = sb("o_inv", [P, BANK // 32], F32)
        oT_norm = sb("oT_norm", [P, 2, BANK // 32, 32], F32)

        def score_buf(i):
            return psum[:, 2 * BANK * i:2 * BANK * (i + 1)]

        def buf_of(k):
            return k % SCORE_BUFS if k < BUF_TURN else (k - 2 if k == BUF_TURN else k - 1) % SCORE_BUFS

        def last_use(k):
            return max(j for j in range(k - BLOCKS, k) if buf_of(j % BLOCKS) == buf_of(k))

        o_acc = psum[:, 6 * BANK:7 * BANK]
        aux = psum[:, 7 * BANK:8 * BANK]

        w_loaded = sem("w_loaded")
        stood_alone = sem("stood_alone")
        w_tok_loaded = sem("w_tok_loaded")
        w_out_loaded = sem("w_out_loaded")
        room_set = sem("room_set")
        const_ready = sem("const_ready")
        b2_loaded = sem("b2_loaded")
        spread_ready = sem("spread_ready")
        experts_loaded = sem("experts_loaded")
        x_loaded = sem("x_loaded")
        aux_filled = sem("aux_filled")
        aux_drained = sem("aux_drained")
        var_ready = sem("var_ready")
        rstd_ready = sem("rstd_ready")
        xn_made = sem("xn_made")
        xn_ready = sem("xn_ready")
        parts_ready = sem("parts_ready")
        squares_ready = sem("squares_ready")
        rq2_ready = sem("rq2_ready")
        rq_ready = sem("rq_ready")
        excess_ready = sem("excess_ready")
        shift_ready = sem("shift_ready")
        flag_ready = sem("flag_ready")
        parts_stored = sem("parts_stored")
        shift_stored = sem("shift_stored")
        aug_loaded = [sem("aug_loaded_0"), sem("aug_loaded_1")]
        va_ready = sem("va_ready")
        scored = sem("scored")
        exped = sem("exped")
        pv_done = sem("pv_done")
        o_evacuated = sem("o_evacuated")
        on_ready = sem("on_ready")
        p_var_ready = sem("p_var_ready")
        p_rstd_ready = sem("p_rstd_ready")
        x2_made = sem("x2_made")
        x2_ready = sem("x2_ready")
        x2_stored = sem("x2_stored")
        router_exped = sem("router_exped")
        comb_ready = sem("comb_ready")
        cT_stored = sem("cT_stored")
        prep_chain = sem("prep_chain")
        post_chain = sem("post_chain")
        evac_chain = sem("evac_chain")
        fb_scored = sem("fb_scored")
        fb_maxed = sem("fb_maxed")
        fb_chain = sem("fb_chain")
        fb_moved = sem("fb_moved")

        WEIGHTS, EXPERT_LOADS = 13, 2
        EDGE_CHAIN = 31
        AUG_DMAS = 2 * PARTS + 1
        PARTS_STORES = 16 * 6
        FB_SCORED, FB_MAXED, FB_MOVED, FB_CHAIN = FB_UNITS + 1, FB_UNITS + 1, 32, 4
        PREP_CHAIN, POST_CHAIN, EVAC_CHAIN = 18, 21, 6
        EVAC_BASE = (0, 1, 2, 4, EVAC_CHAIN)

        def later(b):
            return not (isinstance(b, int) and b == 0)

        def alone(eng):
            eng.sem_inc(stood_alone, 1)

        def all_batches(eng, body):
            body(0, True, False)
            with eng.Fori(1, NB - 1) as b:
                body(b, False, False)
            body(NB - 1, False, True)

        def sync_steps(sp):
            def load_x(bp):
                sp.dma_start(xT[:, :], io["xT"][bp, :, :]).then_inc(x_loaded, 16)

            def store_parts(bp):
                sp.wait_ge(parts_ready, bp + 1)
                for hg in range(2):
                    for w, dst in enumerate((q_parts_d, k_parts_d)):
                        rows = slice(w * D + hg * 32, w * D + hg * 32 + 32)
                        sp.dma_start(dst[hg, 0:PARTS].rearrange("a r i -> r a i"), qk_parts[rows, :, :]
                                     ).then_inc(parts_stored, 16)
                    sp.dma_start(k_parts_d[hg, PARTS:2 * PARTS - 1].rearrange("a r i -> r a i"),
                                 qk_parts[rows, 0:PARTS - 1, :]).then_inc(parts_stored, 16)
                sp.wait_ge(parts_stored, PARTS_STORES * (bp + 1))
                alone(sp)

            def store_x2(bq):
                sp.dma_start(x2_d[bq, :, :], x2_stacks[:, 0, :]).then_inc(x2_stored, 16)
                sp.dma_start(x2_low_d[bq, :, :], x2_stacks[0:D, 1, :]).then_inc(x2_stored, 16)

            def store_shift(bp):
                sp.wait_ge(shift_ready, bp + 1)
                for n in range(2):
                    sp.dma_start(shift_d[:, :, n * BANK:(n + 1) * BANK].rearrange("a h i -> h a i"),
                                 shift_parts[n * SECOND:n * SECOND + H, :, :]).then_inc(shift_stored, 16)
                sp.wait_ge(shift_stored, 32 * (bp + 1))
                alone(sp)

            def load_rows(hg):
                hs = slice(4 * hg, 4 * hg + 4)
                for turn in range(PARTS):
                    r = slice(PARTS * HD * turn, PARTS * HD * (turn + 1))
                    for dst, src in ((QA, q_parts_d[hg, 0:PARTS]), (KA, k_parts_d[hg, turn:turn + PARTS])):
                        sp.dma_start(dst[r, hs, :], src.rearrange("a (d h) i -> (a d) h i", h=4)
                                     ).then_inc(aug_loaded[hg], 16)

            def load_shift(hg):
                hs = slice(4 * hg, 4 * hg + 4)
                sp.dma_start(QA[SHIFT_ROW:SHIFT_ROW + PARTS, hs, :], shift_d[:, hs, :]).then_inc(aug_loaded[hg], 16)

            return load_x, store_parts, store_x2, store_shift, load_rows, load_shift

        def pool_steps(g):
            def prep_rstd(bp):
                g.wait_ge(var_ready, bp + 1)
                g.tensor_tensor(rstd[:, :], ve[:, :], neg_half[:, :], ALU.pow).then_inc(rstd_ready, 1)

            def prep_rq(bp):
                g.wait_ge(rq2_ready, bp + 1)
                g.tensor_tensor(rq[:, :], rq2[:, :], half[:, :], ALU.pow).then_inc(rq_ready, 1)

            def copy_v(hg):
                hs = slice(4 * hg, 4 * hg + 4)
                src = v_new[:, :, 32 * hg:32 * hg + 32].rearrange("p c (h d) -> p c h d", d=HD)
                g.tensor_copy(VA[:, :, hs, 0:HD], src).then_inc(va_ready, 1)

            return prep_rstd, prep_rq, copy_v

        def vector_steps(v):
            def chain(sem, base, total):
                count = [0]

                def link(ins):
                    count[0] += 1
                    ins.then_inc(sem, 1)
                    v.wait_ge(sem, base + count[0])

                def close():
                    assert count[0] == total, (count[0], total)
                return link, close

            def layernorm(src, stats_, mv_, ve_, centred_, rstd_, dst, link, ready, rstd_done, count, out_sem):
                for c in range(NCH):
                    last = v.bn_stats(stats_[:, c, :], src(c))
                link(last)
                alone(v)
                for c in range(NCH):
                    last = v.bn_aggr(mv_[:, c, :], stats_[:, c, :])
                link(last)
                v.tensor_scalar(ve_[:, :], mv_[:, :, 1], EPS, None, ALU.add).then_inc(ready, 1)
                link(v.tensor_tensor(centred_[:, :, :], src(None),
                                     mv_[:, :, 0:1].broadcast_to([P, NCH, D]), ALU.subtract))
                v.wait_ge(rstd_done, count)
                return v.tensor_tensor(dst[:, :, :], centred_[:, :, :],
                                       rstd_[:, :].unsqueeze(2).broadcast_to([P, NCH, D]),
                                       ALU.mult).then_inc(out_sem, 1)

            def split_tokens(src, rest, parts, link, ready, before):
                link(v.tensor_copy(parts[:, :, 0, :], src[:, :, :]))
                link(v.tensor_tensor(rest[:, :, :], src[:, :, :], parts[:, :, 0, :], ALU.subtract))
                v.tensor_copy(parts[:, :, 1, :], rest[:, :, :]).then_inc(ready, 1)
                v.tensor_copy(parts[:, :, 3, :], parts[:, :, 0, :])
                v.wait_ge(ready, before + 1)
                alone(v)
                v.tensor_tensor(parts[:, :, 2, :], rest[:, :, :], parts[:, :, 1, :],
                                ALU.subtract).then_inc(ready, 1)

            def prep_step(step, bp, filled, st):
                if step == "embed":
                    st["link"], st["close"] = chain(prep_chain, PREP_CHAIN * bp, PREP_CHAIN)
                link, close = st["link"], st["close"]
                v.wait_ge(aux_filled, filled)
                if step == "embed":
                    v.tensor_tensor(H_all[:, ds(bp * NCH, NCH), :], aux.rearrange("p (c e) -> p c e", e=D),
                                    posb[:, :, :], ALU.add).then_inc(aux_drained, 1)
                    v.wait_ge(aux_drained, filled)
                    alone(v)
                    layernorm(lambda c: H_all[:, ds(bp * NCH + c, 1), :] if c is not None
                              else H_all[:, ds(bp * NCH, NCH), :], stats, mv, ve, centred, rstd, xn, link,
                              var_ready, rstd_ready, bp + 1, xn_made)
                    v.wait_ge(xn_made, bp + 1)
                    split_tokens(xn, centred, xn_parts, link, xn_ready, 2 * bp)
                elif step in ("norm_t0", "norm_t1"):
                    n = int(step[-1])
                    v.tensor_copy(xn_stacks[:, n, :], aux.bitcast(BF16)).then_inc(aux_drained, 1)
                elif step in ("qk0", "qk1"):
                    n = int(step[-1])
                    v.tensor_scalar(qk[:, n * BANK:(n + 1) * BANK], aux, b_qk[:, 0:1], scale_qk[:, 0:1],
                                    ALU.add, ALU.mult).then_inc(aux_drained, 1)
                elif step == "v":
                    if later(bp):
                        v.wait_ge(va_ready, 2 * bp)
                    v.tensor_tensor(v_new[:, :, :], aux.rearrange("p (c e) -> p c e", e=D),
                                    b_v[:, :].unsqueeze(1).broadcast_to([P, NCH, D]),
                                    ALU.add).then_inc(aux_drained, 1)
                    v.wait_ge(aux_drained, filled)
                    if later(bp):
                        v.wait_ge(parts_stored, PARTS_STORES * bp)
                    link(v.tensor_copy(qk_parts[:, 0, :], qk[:, :]))
                    link(v.tensor_tensor(qk_rest[:, :], qk[:, :], qk_parts[:, 0, :], ALU.subtract))
                    v.tensor_tensor(squares[:, :], qk_parts[:, 0, :], qk_parts[:, 0, :],
                                    ALU.mult).then_inc(squares_ready, 1)
                    link(v.tensor_copy(qk_parts[:, 1, :], qk_rest[:, :]))
                    v.tensor_tensor(qk_parts[:, 2, :], qk_rest[:, :], qk_parts[:, 1, :],
                                    ALU.subtract).then_inc(parts_ready, 1)
                elif step == "sq":
                    v.tensor_copy(sq[:, :], aux)
                    v.reduce_max(sq_max[:, :], aux, AX.X).then_inc(aux_drained, 1)
                    v.wait_ge(aux_drained, filled)
                    alone(v)
                    v.tensor_copy(sq_moved[:, 0:1], sq_max[SECOND:SECOND + H, :])
                    v.tensor_copy(sq_moved[:, 1:2], sq_max[32:32 + H, :])
                    link(v.tensor_copy(sq_moved[:, 2:3], sq_max[32 + SECOND:32 + SECOND + H, :]))
                    v.tensor_tensor(q_sq_max[:, :], sq_max[0:H, :], sq_moved[:, 0:1], ALU.max)
                    link(v.tensor_tensor(k_sq_max[:, :], sq_moved[:, 1:2], sq_moved[:, 2:3], ALU.max))
                    v.tensor_tensor(rq2[:, :], q_sq_max[:, :], k_sq_max[:, :], ALU.mult).then_inc(rq2_ready, 1)
                    link(v.tensor_scalar(coef[0:H, 0:1], q_sq_max[:, :], TINY, None, ALU.max))
                    link(v.reciprocal(coef[0:H, 1:2], coef[0:H, 0:1]))
                    v.wait_ge(rq_ready, bp + 1)
                    v.tensor_scalar(excess[:, :], rq[:, :], RQ_LIMIT, None, ALU.is_gt
                                    ).then_inc(excess_ready, 1)
                    v.tensor_scalar(coef[0:H, 2:3], rq[:, :], 0.5, bmax[:, 0:1], ALU.mult, ALU.add)
                    link(v.scalar_tensor_tensor(coef[0:H, 3:4], coef[0:H, 1:2], -0.5, rq[:, :],
                                                ALU.mult, ALU.mult))
                    link(v.tensor_copy(coef[SECOND:SECOND + H, 2:4], coef[0:H, 2:4]))
                    link(v.tensor_scalar(shift[:, :], sq[0:Q_ROWS, :], coef[0:Q_ROWS, 3:4],
                                         coef[0:Q_ROWS, 2:3], ALU.mult, ALU.subtract))
                    if later(bp):
                        v.wait_ge(shift_stored, 32 * bp)
                    link(v.tensor_copy(shift_parts[:, 0, :], shift[:, :]))
                    link(v.tensor_tensor(shift_rest[:, :], shift[:, :], shift_parts[:, 0, :], ALU.subtract))
                    link(v.tensor_copy(shift_parts[:, 1, :], shift_rest[:, :]))
                    close()
                    v.tensor_tensor(shift_parts[:, 2, :], shift_rest[:, :], shift_parts[:, 1, :],
                                    ALU.subtract).then_inc(shift_ready, 1)
                else:
                    v.tensor_scalar(flags[0:1, ds(bp, 1)], aux[0:1, 0:1], 1.0, None,
                                    ALU.min).then_inc(aux_drained, 1)
                    v.wait_ge(aux_drained, filled)
                    v.sem_inc(flag_ready, 1)

            return chain, layernorm, split_tokens, prep_step

        def vector_post(v):
            chain, layernorm, split_tokens, _ = vector_steps(v)

            def post_step(step, bq, filled, st):
                if step == "out_proj":
                    st["plink"], st["pclose"] = chain(post_chain, POST_CHAIN * bq, POST_CHAIN)
                link, close = st["plink"], st["pclose"]
                v.wait_ge(aux_filled, filled)
                hq = H_all[:, ds(bq * NCH, NCH), :]
                if step == "out_proj":
                    v.tensor_tensor(h1[:, :, :], aux.rearrange("p (c e) -> p c e", e=D), hq,
                                    ALU.add).then_inc(aux_drained, 1)
                    v.wait_ge(aux_drained, filled)
                    layernorm(lambda c: h1[:, c, :] if c is not None else h1[:, :, :], p_stats, p_mv, p_ve,
                              p_centred, p_rstd, x2, link, p_var_ready, p_rstd_ready, bq + 1, x2_made)
                    v.wait_ge(x2_made, bq + 1)
                    split_tokens(x2, p_centred, x2_parts, link, x2_ready, 2 * bq)
                    v.tensor_tensor(hq, h1[:, :, :], x2[:, :, :], ALU.add)
                elif step in ("post_t0", "post_t1"):
                    n = int(step[-1])
                    if n == 0 and later(bq):
                        v.wait_ge(x2_stored, 32 * bq)
                    v.tensor_copy(x2_stacks[:, n, :], aux.bitcast(BF16)).then_inc(aux_drained, 1)
                elif step == "router":
                    raw = aux[:, 0:NCH * NX].rearrange("p (c e) -> p c e", e=NX)
                    link(v.tensor_reduce(logit_max[:, :], raw, AX.X, ALU.max))
                    v.tensor_tensor(logits[:, :, :], raw, logit_max[:, :].unsqueeze(2).broadcast_to([P, NCH, NX]),
                                    ALU.subtract).then_inc(aux_drained, 1)
                else:
                    if later(bq):
                        v.wait_ge(cT_stored, 16 * bq)
                    v.tensor_copy(cT[:, :], aux[0:PARTS * NX, :].bitcast(BF16)).then_inc(aux_drained, 1)

            def rank_experts(bq, st):
                link, close = st["plink"], st["pclose"]
                v.wait_ge(router_exped, bq + 1)
                link(v.tensor_reduce(r_sum[:, :], router_e[:, :, :], AX.X, ALU.add))
                link(v.reciprocal(r_inv[:, :], r_sum[:, :]))
                link(v.tensor_tensor(rprob[:, :, :], router_e[:, :, :],
                                     r_inv[:, :].unsqueeze(2).broadcast_to([P, NCH, NX]), ALU.mult))
                other = rprob[:, :, :].unsqueeze(2).broadcast_to([P, NCH, NX, NX])
                own = rprob[:, :, :].unsqueeze(3).broadcast_to([P, NCH, NX, NX])
                v.tensor_tensor(above[:, :, :].rearrange("p c (e f) -> p c e f", f=NX), other, own, ALU.is_gt)
                last = v.tensor_tensor(equal[:, :, :].rearrange("p c (e f) -> p c e f", f=NX), other, own,
                                       ALU.is_equal)
                link(last)
                link(v.tensor_tensor(equal[:, :, :], equal[:, :, :],
                                     lower[:, :, :].rearrange("p e f -> p (e f)").unsqueeze(1).broadcast_to(
                                         [P, NCH, NX * NX]), ALU.mult))
                link(v.tensor_tensor(above[:, :, :], above[:, :, :], equal[:, :, :], ALU.add))
                link(v.tensor_reduce(rank[:, :, :], above[:, :, :].rearrange("p c (e f) -> p c e f", f=NX),
                                     AX.X, ALU.add))

            def weigh_experts(bq, st):
                link, close = st["plink"], st["pclose"]
                link(v.scalar_tensor_tensor(chosen[:, :, :], rank[:, :, :], 2.0, rprob[:, :, :],
                                            ALU.is_lt, ALU.mult))
                link(v.tensor_reduce(c_sum[:, :], chosen[:, :, :], AX.X, ALU.add))
                link(v.tensor_scalar(c_inv[:, :], c_sum[:, :], 1e-12, None, ALU.max))
                link(v.reciprocal(c_sum[:, :], c_inv[:, :]))
                link(v.tensor_tensor(comb[:, :, :], chosen[:, :, :],
                                     c_sum[:, :].unsqueeze(2).broadcast_to([P, NCH, NX]), ALU.mult))
                link(v.tensor_copy(comb_parts[:, :, 0, :], comb[:, :, :]))
                link(v.tensor_tensor(comb_rest[:, :, :], comb[:, :, :], comb_parts[:, :, 0, :], ALU.subtract))
                link(v.tensor_copy(comb_parts[:, :, 1, :], comb_rest[:, :, :]))
                close()
                v.tensor_tensor(comb_parts[:, :, 2, :], comb_rest[:, :, :], comb_parts[:, :, 1, :],
                                ALU.subtract).then_inc(comb_ready, 1)

            return post_step, rank_experts, weigh_experts

        def tensor_steps(pe):
            def aux_step(step, n, done, drained):
                pe.wait_ge(aux_drained, drained) if not (isinstance(drained, int) and drained == 0) else None
                if step == "embed":
                    pe.wait_ge(x_loaded, 16 * (n + 1))
                    for c in range(NCH):
                        last = pe.matmul(aux[:, c * D:(c + 1) * D], xT[:, c * P:(c + 1) * P], w_tok[:, :],
                                         start=True, stop=True)
                elif step in ("norm_t0", "norm_t1", "post_t0", "post_t1"):
                    src, ready = (xn_parts, xn_ready) if step[0] == "n" else (x2_parts, x2_ready)
                    stack = int(step[-1])
                    pe.wait_ge(ready, 2 * n + stack + 1)
                    alone(pe)
                    for c in range(NCH):
                        last = pe.transpose(aux.bitcast(BF16)[:, c * P:(c + 1) * P],
                                            src[:, c, 2 * stack:2 * stack + 2, :].rearrange("p a d -> p (a d)"),
                                            ident_bf[:, :])
                elif step in ("qk0", "qk1"):
                    i = int(step[-1])
                    for turn, stack in TURNS:
                        last = pe.matmul(aux, w_parts[:, turn, QK_COLS], xn_stacks[:, stack, i * BANK:(i + 1) * BANK],
                                         start=(turn == 0), stop=(turn == 2))
                elif step == "v":
                    for c in range(NCH):
                        for turn, stack in TURNS:
                            last = pe.matmul(aux[:, c * D:(c + 1) * D], xn_stacks[:, stack, c * P:(c + 1) * P],
                                             w_parts[:, turn, V_COLS], start=(turn == 0), stop=(turn == 2))
                elif step == "sq":
                    pe.wait_ge(squares_ready, n + 1)
                    alone(pe)
                    for i in range(2):
                        for w in range(2):
                            r = i * SECOND + 32 * w
                            last = pe.matmul(aux[r:r + 32, :], sel_sq[:, w, :],
                                             squares[:, i * BANK:(i + 1) * BANK], start=True, stop=True)
                elif step == "flag":
                    pe.wait_ge(excess_ready, n + 1)
                    alone(pe)
                    last = pe.matmul(aux[0:1, 0:1], excess[:, :], ones8[:, :], start=True, stop=True)
                elif step == "out_proj":
                    pe.wait_ge(on_ready, GROUPS * (n + 1))
                    for c in range(NCH):
                        last = pe.matmul(aux[:, c * D:(c + 1) * D], ON[:, c * P:(c + 1) * P], w_o[:, :],
                                         start=True, stop=True)
                elif step == "router":
                    for c in range(NCH):
                        for turn, stack in TURNS:
                            last = pe.matmul(aux[:, c * NX:(c + 1) * NX], x2_stacks[:, stack, c * P:(c + 1) * P],
                                             w_parts[:, turn, ROUTER_COLS], start=(turn == 0), stop=(turn == 2))
                else:
                    pe.wait_ge(comb_ready, n + 1)
                    for c in range(NCH):
                        last = pe.transpose(aux[0:PARTS * NX, :].bitcast(BF16)[:, c * P:(c + 1) * P],
                                            comb_parts[:, c, :, :].rearrange("p a e -> p (a e)"), ident_bf[:, :])
                last.then_inc(aux_filled, 1)

            return aux_step

        with ExitStack() as edge_ctx:
            def esb(name, shape, dt):
                return edge_ctx.enter_context(nc.sbuf_tensor(name, shape, dt))

            tgt = esb("tgt", [P, EC], I32)
            node_a = esb("node_a", [P, EC], I32)
            node_b = esb("node_b", [P, EC], I32)
            node_af = esb("node_af", [P, EC], F32)
            node_bf = esb("node_bf", [P, EC], F32)
            iota32 = esb("iota32", [P, 32], F32)
            exp_bits = esb("exp_bits", [P, 1], I32)
            offset = esb("offset", [P, 1], F32)
            hot_a = esb("hot_a", [P, EC, 32], BF16)
            hot_b = esb("hot_b", [P, EC, 32], BF16)
            base = esb("base", [P, EC // 2 * 32], F32)
            key = esb("key", [P, EC // 2 * 32], F32)
            win4 = esb("win4", [P, 32], F32)
            win4T = esb("win4T", [P, 32], F32)
            win_by = esb("win_by", [32, 32, 4], F32)
            winT = esb("winT", [32, 32], F32)
            winp = esb("winp", [P, NCH], F32)
            valid = esb("valid", [P, NCH], F32)
            first_at = esb("first_at", [P, NCH], F32)
            idx = esb("idx", [P, NCH], I32)
            attr = esb("attr", [P, NCH, 3], F32)
            we = esb("we", [P, 3, H], F32)
            be = esb("be", [P, H], F32)
            term = esb("term", [P, NCH, H], F32)
            bias = esb("bias", [P, NCH, H], F32)
            bias_hj = esb("bias_hj", [P, H, NCH], F32)
            bias_top = esb("bias_top", [P, H], F32)
            biasT = esb("biasT", [D, P], F32)
            b_rest = esb("b_rest", [D, P], F32)
            bparts = esb("bparts", [D, PARTS, P], BF16)
            ones3 = esb("ones3", [PARTS, T], BF16)
            weights = esb("weights", [P, W_COLS], F32)
            weights_rest = esb("weights_rest", [P, W_COLS], F32)

            exps = hot_a[:, :, :].rearrange("p m a -> p (m a)").bitcast(I32)

            sums = psum[:, 0:EC // 2 * 32]
            biasT_bank = psum[0:D, 5 * BANK:5 * BANK + P]
            top_bank = psum[0:H, 6 * BANK:6 * BANK + P]
            bparts_d = scratch["bparts"]

            tgt_loaded = sem("tgt_loaded")
            edge_w_loaded = sem("edge_w_loaded")
            iotas = sem("iotas")
            ident_ready = sem("ident_ready")
            base_ready = sem("base_ready")
            ones_ready = sem("ones_ready")
            turns_ready = sem("turns_ready")
            b2_split = sem("b2_split")
            b2_placed = sem("b2_placed")
            ones_placed = sem("ones_placed")
            hot_ready = sem("hot_ready")
            edges_summed = sem("edges_summed")
            idx_ready = sem("idx_ready")
            gathered = sem("gathered")
            bias_ready = sem("bias_ready")
            bias_turned = sem("bias_turned")
            bparts_ready = sem("bparts_ready")
            bparts_moved = sem("bparts_moved")
            e_chain = sem("e_chain")

            with nc.Block() as block:
                @block.sync
                def _(sp):
                    load_x, store_parts, store_x2, store_shift, load_rows, load_shift = sync_steps(sp)
                    sp.dma_start(tgt[:, :], io["tgt"]).then_inc(tgt_loaded, 16)
                    load_x(0)
                    sp.dma_start(w_tok[:, :], io["tok_WT"]).then_inc(w_tok_loaded, 16)
                    sp.dma_start(posb[:, :, :], io["pos"]).then_inc(w_tok_loaded, 16)
                    sp.dma_start(tok_b[:, :], io["tok_b"].partition_broadcast(P)).then_inc(w_tok_loaded, 16)
                    sp.wait_ge(ones_ready, 1)
                    for dst in (QA[BIAS_ROW:BIAS_ROW + PARTS, :, :], KA[SHIFT_ROW:SHIFT_ROW + PARTS, :, :]):
                        sp.dma_start(dst, ones3[:, :].unsqueeze(1).broadcast_to([PARTS, H, T])
                                     ).then_inc(ones_placed, 16)
                    sp.wait_ge(aux_filled, 1)
                    load_x(1)
                    store_parts(0)
                    load_rows(0)
                    store_shift(0)
                    load_shift(0)
                    sp.wait_ge(ones_placed, 32)

                @block.scalar
                def _(act):
                    for rows in (slice(0, D), slice(D, P)):
                        for cols, src in ((slice(0, D), io["Wq"]), (slice(D, 2 * D), io["Wk"]), (V_COLS, io["Wv"]),
                                          (ROUTER_COLS, io["router_wT"]), (slice(W1_COL, W_COLS), io["w1"])):
                            act.dma_start(weights[rows, cols], src).then_inc(w_loaded, 16)
                    for dst, src in ((b_qk[0:D, :], io["bq"].unsqueeze(1)), (b_qk[D:P, :], io["bk"].unsqueeze(1)),
                                     (b_v[:, :], io["bv"].partition_broadcast(P))):
                        act.dma_start(dst, src).then_inc(w_loaded, 16)
                    act.dma_start(we[:, :, :], io["We"].rearrange("c h -> (c h)").partition_broadcast(P)
                                  ).then_inc(edge_w_loaded, 16)
                    act.dma_start(be[:, :], io["be"].partition_broadcast(P)).then_inc(edge_w_loaded, 16)
                    act.wait_ge(const_ready, 1)
                    for h in range(H):
                        r = 32 * (h % 4) + HD * (h // 4)
                        act.dma_start(w_o[r:r + HD, :], io["Wo"][h * HD:(h + 1) * HD, :]).then_inc(w_out_loaded, 16)
                    act.dma_start(w_o[ONE_ROW:ONE_ROW + 1, :], io["bo"].unsqueeze(0)).then_inc(w_out_loaded, 16)
                    for a in range(PARTS):
                        act.dma_start(b2[a * NX:(a + 1) * NX, :], io["b2"]).then_inc(b2_loaded, 16)
                    act.wait_ge(b2_split, 1)
                    for a in range(PARTS):
                        act.dma_start(b2_rows[a * KC:(a + 1) * KC, :], b2_parts[:, a, :]).then_inc(b2_placed, 16)
                    act.wait_ge(bparts_ready, 1)
                    act.dma_start(bparts_d.rearrange("a h (c p) -> (h c) a p", p=P), bparts[:, :, :]
                                  ).then_inc(bparts_moved, 16)
                    act.wait_ge(bparts_moved, 16)
                    act.dma_start(KA[BIAS_ROW:BIAS_ROW + PARTS, :, :], bparts_d).then_inc(bparts_moved, 16)
                    act.wait_ge(bparts_moved, 32)
                    act.wait_ge(b2_placed, 16 * PARTS)

                @block.gpsimd
                def _(g):
                    prep_rstd, prep_rq, copy_v = pool_steps(g)
                    g.iota(iota32[:, :], pattern=[[1, 32]], base=0, channel_multiplier=0,
                           allow_small_or_imprecise_dtypes=True).then_inc(iotas, 1)
                    for half_ in range(2):
                        g.wait_ge(iotas, 1 + half_)
                        g.iota(exp_bits[64 * half_:64 * half_ + 64, :], pattern=[[0, 1]], base=127,
                               channel_multiplier=2).then_inc(iotas, 1)
                    g.wait_ge(iotas, 3)
                    g.memset(ident[:, :], 0.0).then_inc(ident_ready, 1)
                    g.wait_ge(ident_ready, 1)
                    g.affine_select(out=ident[:, :], in_=ident[:, :], compare_op=ALU.not_equal, fill=1.0, base=0,
                                    pattern=[[-1, P]], channel_multiplier=1).then_inc(ident_ready, 1)
                    g.wait_ge(ident_ready, 2)
                    g.tensor_copy(ident_bf[:, :], ident[:, :]).then_inc(ident_ready, 1)
                    g.wait_ge(ident_ready, 3)
                    g.iota(base[:, :], pattern=[[2 * P, EC // 2], [0, 32]], base=0, channel_multiplier=0,
                           allow_small_or_imprecise_dtypes=True).then_inc(base_ready, 1)
                    g.wait_ge(base_ready, 1)
                    g.memset(ones3[:, :], 1.0).then_inc(ones_ready, 1)
                    g.wait_ge(ones_ready, 1)
                    g.memset(VA[:, :, :, :], 0.0).then_inc(room_set, 1)
                    g.wait_ge(room_set, 1)
                    g.memset(VA[:, :, :, HD:HD + 1], 1.0).then_inc(room_set, 1)
                    g.wait_ge(room_set, 2)
                    g.memset(oT_norm[:, :, :, :], 0.0).then_inc(room_set, 1)
                    g.wait_ge(room_set, 3)
                    g.memset(oT_norm[:, :, :, ONE_ROW:ONE_ROW + 1], 1.0).then_inc(room_set, 1)
                    g.wait_ge(room_set, 4)
                    g.wait_ge(const_ready, 2)
                    prep_rstd(0)
                    g.wait_ge(rstd_ready, 1)
                    g.wait_ge(w_loaded, 16 * WEIGHTS)
                    g.tensor_copy(w_parts[:, 0, :], weights[:, :]).then_inc(turns_ready, 1)
                    g.wait_ge(turns_ready, 1)
                    g.tensor_tensor(weights_rest[:, :], weights[:, :], w_parts[:, 0, :],
                                    ALU.subtract).then_inc(turns_ready, 1)
                    g.wait_ge(turns_ready, 2)
                    g.tensor_copy(w_parts[:, 1, :], weights_rest[:, :]).then_inc(turns_ready, 1)
                    g.wait_ge(turns_ready, 3)
                    g.tensor_copy(w_parts[0:D, 2, :], w_parts[0:D, 0, :]).then_inc(turns_ready, 1)
                    g.wait_ge(turns_ready, 4)
                    g.tensor_tensor(w_parts[D:P, 2, :], weights_rest[D:P, :], w_parts[D:P, 1, :],
                                    ALU.subtract).then_inc(turns_ready, 1)
                    g.wait_ge(turns_ready, 5)
                    g.wait_ge(idx_ready, 1)
                    for c in range(NCH):
                        g.indirect_dma_start(out=attr[:, c, :], out_offset=None, in_=io["edge_attr"],
                                             in_offset=bass.IndirectOffsetOnAxis(ap=idx[:, c:c + 1], axis=0)
                                             ).then_inc(gathered, 16)
                    g.memset(spread[:, :, :], 0.0).then_inc(spread_ready, 1)
                    for a in range(PARTS):
                        g.wait_ge(spread_ready, a + 1)
                        view = spread[:, :, :].rearrange("k m (e n) -> k m e n", e=2)
                        g.affine_select(out=view, in_=view, compare_op=ALU.not_equal, fill=1.0, base=-NX * a,
                                        pattern=[[-2, PAIRS], [-1, 2], [0, D]], channel_multiplier=1
                                        ).then_inc(spread_ready, 1)
                    g.wait_ge(spread_ready, PARTS + 1)
                    g.wait_ge(aux_drained, PREP.index("v") + 1)
                    for hg in range(2):
                        copy_v(hg)
                    prep_rq(0)

                @block.vector
                def _(v):
                    chain, _, _, prep_step = vector_steps(v)
                    link, close = chain(e_chain, 0, EDGE_CHAIN)
                    st = {}

                    v.memset(w_o[:, :], 0.0).then_inc(const_ready, 1)
                    v.memset(coef[:, :], 0.0)
                    v.memset(sel_sq[:, :, :], 0.0)
                    v.memset(scale_qk[0:D, :], HD ** -0.5)
                    v.memset(scale_qk[D:P, :], 1.0)
                    v.memset(ones8[:, :], 1.0)
                    for n in range(4):
                        v.memset(offset[32 * n:32 * n + 32, :], 64.0 * n - 62.5)
                    v.memset(half[:, :], 0.5)
                    v.memset(neg_half[:, :], -0.5).then_inc(const_ready, 1)

                    v.wait_ge(tgt_loaded, 16)
                    v.wait_ge(iotas, 3)
                    v.tensor_scalar(node_a[:, :], tgt[:, :], 5, None, ALU.logical_shift_right)
                    link(v.tensor_scalar(node_b[:, :], tgt[:, :], 31, None, ALU.bitwise_and))
                    v.tensor_copy(node_af[:, :], node_a[:, :])
                    v.tensor_copy(node_bf[:, :], node_b[:, :])
                    link(v.tensor_scalar(exp_bits[:, :], exp_bits[:, :], 23, None, ALU.logical_shift_left))
                    link(v.tensor_tensor(hot_b[:, :, :], node_bf[:, :].unsqueeze(2).broadcast_to([P, EC, 32]),
                                         iota32[:, :].unsqueeze(1).broadcast_to([P, EC, 32]), ALU.is_equal))
                    v.tensor_scalar(hot_b[:, :, :], hot_b[:, :, :], exp_bits[:, 0:1].bitcast(F32), None, ALU.mult)
                    v.tensor_tensor(hot_a[:, :, :], node_af[:, :].unsqueeze(2).broadcast_to([P, EC, 32]),
                                    iota32[:, :].unsqueeze(1).broadcast_to([P, EC, 32]),
                                    ALU.is_equal).then_inc(hot_ready, 1)

                    v.wait_ge(base_ready, 1)
                    link(v.tensor_scalar(base[:, :], base[:, :], offset[:, 0:1], None, ALU.add))
                    v.wait_ge(w_tok_loaded, 48)
                    v.tensor_tensor(posb[:, :, :], posb[:, :, :], tok_b[:, :].unsqueeze(1).broadcast_to([P, NCH, D]),
                                    ALU.add).then_inc(const_ready, 1)
                    v.wait_ge(const_ready, 3)
                    prep_step("embed", 0, 1, st)

                    v.wait_ge(edges_summed, 4)
                    link(v.tensor_scalar(exps, sums.bitcast(I32), 23, None, ALU.logical_shift_right))
                    link(v.scalar_tensor_tensor(key[:, :], exps, 0.5, base[:, :], ALU.mult, ALU.add))
                    link(v.scalar_tensor_tensor(base[:, :], exps, 0.0, key[:, :], ALU.is_gt, ALU.mult))
                    link(v.tensor_reduce(win4[:, :], base[:, :].rearrange("p (m b) -> p b m", b=32), AX.X, ALU.max))
                    link(v.transpose(win4T[:, :], win4[:, :]))
                    for n in range(4):
                        last = v.tensor_copy(win_by[:, :, n], win4T[32 * n:32 * n + 32, :])
                    link(last)
                    link(v.tensor_reduce(winT[:, :], win_by[:, :, :], AX.X, ALU.max))
                    for r in range(4):
                        last = v.tensor_copy(winp[32 * r:32 * r + 32, :],
                                             winT[:, :].rearrange("b (c r) -> b r c", r=4)[:, r, :])
                    link(last)
                    v.tensor_scalar(valid[:, :], winp[:, :], 0.0, None, ALU.is_gt)
                    link(v.tensor_scalar(first_at[:, :], winp[:, :], -1.0, 0.0, ALU.add, ALU.max))
                    v.tensor_copy(idx[:, :], first_at[:, :]).then_inc(idx_ready, 1)

                    for n, step in enumerate(PREP[1:]):
                        if step == "sq":
                            break
                        prep_step(step, 0, n + 2, st)
                        if step == "norm_t1":
                            v.wait_ge(ident_ready, 3)
                            v.tensor_reduce(lower[:, 0, :].rearrange("p (g h) -> p g h", g=2),
                                            ident[:, 0:D].rearrange("p (g d h) -> p g h d", g=2, h=4),
                                            AX.X, ALU.add)
                            link(v.tensor_reduce(lower[:, 1, :].rearrange("p (g h) -> p g h", g=2),
                                            ident[:, D:P].rearrange("p (g d h) -> p g h d", g=2, h=4),
                                                 AX.X, ALU.add))
                            link(v.tensor_copy(sel_sq[:, :, 0:H], lower[:, 0:2, :]))
                            link(v.memset(lower[:, :, :], 0.0))
                            for e in range(1, NX):
                                last = v.memset(lower[:, e, 0:e], 1.0)
                            last.then_inc(const_ready, 1)

                    v.wait_ge(b2_loaded, 16 * PARTS)
                    link(v.tensor_copy(b2_parts[:, 0, :], b2[:, :]))
                    link(v.tensor_tensor(b2_rest[:, :], b2[:, :], b2_parts[:, 0, :], ALU.subtract))
                    link(v.tensor_copy(b2_parts[:, 1, :], b2_rest[:, :]))
                    v.tensor_tensor(b2_parts[:, 2, :], b2_rest[:, :], b2_parts[:, 1, :],
                                    ALU.subtract).then_inc(b2_split, 1)

                    v.wait_ge(edge_w_loaded, 32)
                    v.wait_ge(gathered, 16 * NCH)
                    for c in range(3):
                        dst = bias if c == 0 else term
                        link(v.tensor_tensor(dst[:, :, :], attr[:, :, c:c + 1].broadcast_to([P, NCH, H]),
                                             we[:, c, :].unsqueeze(1).broadcast_to([P, NCH, H]), ALU.mult))
                        if c:
                            link(v.tensor_tensor(bias[:, :, :], bias[:, :, :], term[:, :, :], ALU.add))
                    link(v.tensor_tensor(bias[:, :, :], bias[:, :, :],
                                         be[:, :].unsqueeze(1).broadcast_to([P, NCH, H]), ALU.add))
                    link(v.tensor_tensor(bias_hj[:, :, :].rearrange("p h c -> p c h"), bias[:, :, :],
                                         valid[:, :].unsqueeze(2).broadcast_to([P, NCH, H]), ALU.mult))
                    v.tensor_reduce(bias_top[:, :], bias_hj[:, :, :], AX.X, ALU.max).then_inc(bias_ready, 1)
                    v.wait_ge(bias_turned, 1)
                    link(v.tensor_copy(biasT[:, :], biasT_bank))
                    link(v.tensor_copy(bparts[:, 0, :], biasT[:, :]))
                    link(v.tensor_tensor(b_rest[:, :], biasT[:, :], bparts[:, 0, :], ALU.subtract))
                    link(v.tensor_copy(bparts[:, 1, :], b_rest[:, :]))
                    v.tensor_tensor(bparts[:, 2, :], b_rest[:, :], bparts[:, 1, :],
                                    ALU.subtract).then_inc(bparts_ready, 1)
                    link(v.reduce_max(bmax[:, :], top_bank, AX.X))
                    close()
                    prep_step("sq", 0, PREP.index("sq") + 1, st)
                    prep_step("flag", 0, PREP.index("flag") + 1, st)

                @block.tensor
                def _(pe):
                    aux_step = tensor_steps(pe)
                    pe.wait_ge(w_tok_loaded, 48)
                    aux_step("embed", 0, 1, 0)
                    pe.wait_ge(hot_ready, 1)
                    for m in range(EC):
                        for g in range(2):
                            tile = 32 * (2 * (m % 2) + g)
                            rows = slice(64 * g, 64 * g + 64)
                            last = pe.matmul(sums[tile:tile + 32, 32 * (m // 2):32 * (m // 2) + 32],
                                             hot_a[rows, m, :], hot_b[rows, m, :], start=True, stop=True)
                        if m % 32 == 31:
                            last.then_inc(edges_summed, 1)
                    pe.wait_ge(ident_ready, 3)
                    for i, step in enumerate(PREP):
                        if step == "qk0":
                            pe.wait_ge(turns_ready, 5)
                        if step == "sq":
                            pe.wait_ge(const_ready, 4)
                            pe.wait_ge(bias_ready, 1)
                            pe.transpose(biasT_bank, bias_hj[:, :, :].rearrange("p h c -> p (h c)"), ident[:, :])
                            pe.transpose(top_bank, bias_top[:, :], ident[:, :]).then_inc(bias_turned, 1)
                        if i:
                            aux_step(step, 0, i + 1, i)
                    pe.wait_ge(w_out_loaded, 16 * (H + 1))

        probs = sb("probs", [P, PROB_BUFS, 2 * BANK], F32)
        fb_max = sb("fb_max", [P, FB_UNITS], F32)
        fb_rows = sb("fb_rows", [FB_UNITS, P], F32)
        fb_rest = sb("fb_rest", [FB_UNITS, P], F32)
        fb_parts = sb("fb_parts", [FB_UNITS, PARTS, P], BF16)

        with nc.Block() as block:
            @block.sync
            def _(sp):
                load_x, store_parts, store_x2, store_shift, load_rows, load_shift = sync_steps(sp)

                def body(b, first, last, next_x=True):
                    order = aux_order(not last, not first)
                    if not last:
                        for hg in range(2):
                            sp.wait_ge(aug_loaded[hg], 16 * AUG_DMAS * (b + 1))
                            alone(sp)
                        if next_x:
                            sp.wait_ge(aux_filled, aux_base(b) + 1)
                            load_x(b + 2)
                        store_parts(b + 1)
                        sp.wait_ge(scored, BLOCKS * b + BLOCKS // 2)
                        load_rows(0)
                        store_shift(b + 1)
                        load_shift(0)
                    if not first:
                        sp.wait_ge(aux_drained, aux_base(b) + order.index("post_t1") + 1)
                        store_x2(b - 1)
                    if not first:
                        sp.wait_ge(aux_drained, aux_base(b) + order.index("combine_t") + 1)
                        sp.dma_start(cT_d[b - 1, :, :], cT[:, :]).then_inc(cT_stored, 16)
                    if not last:
                        sp.wait_ge(scored, BLOCKS * (b + 1))
                        load_rows(1)
                        load_shift(1)

                load_rows(1)
                load_shift(1)
                body(0, True, False)
                with sp.Fori(1, NB - 2) as b:
                    body(b, False, False)
                body(NB - 2, False, False, next_x=False)
                body(NB - 1, False, True)
                for dst, src in ((w2[:, :, :], io["w2"]), (b1[:, :], io["b1"])):
                    sp.dma_start(dst, src).then_inc(experts_loaded, 16)
                sp.wait_ge(x2_stored, 32 * (NB - 1))
                sp.wait_ge(cT_stored, 16 * (NB - 1))

            @block.gpsimd
            def _(g):
                prep_rstd, prep_rq, copy_v = pool_steps(g)

                def post_pow(bq):
                    g.wait_ge(p_var_ready, bq + 1)
                    g.tensor_tensor(p_rstd[:, :], p_ve[:, :], neg_half[:, :], ALU.pow).then_inc(p_rstd_ready, 1)

                def body(b, first, last):
                    if not last:
                        prep_rstd(b + 1)
                        prep_rq(b + 1)
                        g.wait_ge(aux_drained, aux_base(b) + aux_order(True, not first).index("v") + 1)
                    for hg in range(2):
                        if not last:
                            g.wait_ge(pv_done, QUADS * b + 16 * (hg + 1))
                            alone(g)
                            copy_v(hg)
                        if hg == 0 and not first:
                            post_pow(b - 1)

                all_batches(g, body)

            @block.scalar
            def _(act):
                def exp_block(b, k):
                    act.wait_ge(scored, BLOCKS * b + k + 1)
                    if k >= PROB_BUFS:
                        act.wait_ge(pv_done, QUADS * b + (k - PROB_BUFS) // 2 + 1)
                    elif later(b):
                        act.wait_ge(pv_done, QUADS * b + (k - PROB_BUFS) // 2 + 1)
                    nc.scalar.activation(probs[:, k % PROB_BUFS, :], score_buf(buf_of(k)),
                                         ACT.Exp).then_inc(exped, 1)

                def router_exp(drained):
                    act.wait_ge(aux_drained, drained)
                    nc.scalar.activation(router_e[:, :, :], logits[:, :, :], ACT.Exp).then_inc(router_exped, 1)

                def fallback(b, hg, flag):
                    with act.If(flag != 0):
                        act.wait_ge(fb_maxed, FB_MAXED * (2 * b + hg + 1))
                        act.dma_start(fb_d.rearrange("a u p -> u a p"), fb_parts[:, :, :]).then_inc(fb_moved, 16)
                        act.wait_ge(fb_moved, FB_MOVED * (2 * b + hg) + 16)
                        act.dma_start(QA[SHIFT_ROW:SHIFT_ROW + PARTS, 4 * hg:4 * hg + 4, :],
                                      fb_d.rearrange("a (h c) p -> a h (c p)", h=4)).then_inc(fb_moved, 16)
                    with act.Else():
                        act.sem_inc(fb_moved, FB_MOVED)

                def body(b, first, last):
                    act.wait_ge(flag_ready, b + 1)
                    flag = act.value_load(flags[0:1, ds(b, 1)], min_val=0, max_val=1)
                    for k in range(BLOCKS):
                        if k % (BLOCKS // 2) == 0:
                            fallback(b, k // (BLOCKS // 2), flag)
                        exp_block(b, k)
                        if k == ROUTER_EXP_BLOCK and not first:
                            router_exp(aux_base(b) + aux_order(not last, True).index("router") + 1)

                all_batches(act, body)

            @block.vector
            def _(v):
                chain, _, _, prep_step = vector_steps(v)
                post_step, rank_experts, weigh_experts = vector_post(v)

                def evacuate(b, g):
                    hg, ih = g // 2, g % 2
                    link, close = chain(evac_chain, EVAC_CHAIN * b + EVAC_BASE[g], EVAC_BASE[g + 1] - EVAC_BASE[g])
                    if later(b) or g:
                        v.wait_ge(on_ready, GROUPS * b + g)
                    v.wait_ge(pv_done, QUADS * b + 8 * g + 8)
                    v.transpose(oT[:, :, :].rearrange("p j r -> p (j r)"), o_acc).then_inc(o_evacuated, 1)
                    v.wait_ge(o_evacuated, GROUPS * b + g + 1)
                    alone(v)
                    link(v.reciprocal(o_inv[:, :], oT[:, :, HD]))
                    last = v.tensor_tensor(oT_norm[:, ih, :, HD * hg:HD * hg + HD], oT[:, :, 0:HD],
                                           o_inv[:, :].unsqueeze(2).broadcast_to([P, BANK // 32, HD]), ALU.mult)
                    if hg:
                        link(last)
                        v.transpose(ON[:, ih * BANK:(ih + 1) * BANK],
                                    oT_norm[:, ih, :, :].rearrange("p j r -> p (j r)")).then_inc(on_ready, 1)
                    else:
                        last.then_inc(on_ready, 1)
                    close()

                def fallback(b, hg, flag):
                    base = 2 * b + hg
                    with v.If(flag != 0):
                        for u in range(FB_UNITS):
                            v.wait_ge(fb_scored, FB_SCORED * base + u + 1)
                            v.tensor_reduce(fb_max[:, u:u + 1], score_buf(u % 2), AX.X, ALU.max,
                                            negate=True).then_inc(fb_maxed, 1)
                        v.wait_ge(fb_scored, FB_SCORED * base + FB_UNITS + 1)
                        v.tensor_copy(fb_rows[:, :], psum[0:FB_UNITS, 4 * BANK:4 * BANK + P]).then_inc(fb_chain, 1)
                        v.wait_ge(fb_chain, FB_CHAIN * base + 1)
                        v.tensor_copy(fb_parts[:, 0, :], fb_rows[:, :]).then_inc(fb_chain, 1)
                        v.wait_ge(fb_chain, FB_CHAIN * base + 2)
                        v.tensor_tensor(fb_rest[:, :], fb_rows[:, :], fb_parts[:, 0, :],
                                        ALU.subtract).then_inc(fb_chain, 1)
                        v.wait_ge(fb_chain, FB_CHAIN * base + 3)
                        v.tensor_copy(fb_parts[:, 1, :], fb_rest[:, :]).then_inc(fb_chain, 1)
                        v.wait_ge(fb_chain, FB_CHAIN * base + 4)
                        v.tensor_tensor(fb_parts[:, 2, :], fb_rest[:, :], fb_parts[:, 1, :],
                                        ALU.subtract).then_inc(fb_maxed, 1)
                    with v.Else():
                        v.sem_inc(fb_maxed, FB_MAXED)
                        v.sem_inc(fb_chain, FB_CHAIN)

                def body(b, first, last):
                    v.wait_ge(flag_ready, b + 1)
                    flag = v.value_load(flags[0:1, ds(b, 1)], min_val=0, max_val=1)
                    order = aux_order(not last, not first)
                    st = {}
                    for slot in range(QUADS):
                        if slot == 0:
                            fallback(b, 0, flag)
                        if slot == 16:
                            fallback(b, 1, flag)
                        for step in steps_of(slot, not last, not first):
                            filled = aux_base(b) + order.index(step) + 1
                            if step in PREP:
                                prep_step(step, b + 1, filled, st)
                            else:
                                post_step(step, b - 1, filled, st)
                        if slot == LAST_EVAC_SLOT and not first:
                            evacuate(b - 1, 3)
                        if slot in EVAC_SLOTS:
                            evacuate(b, EVAC_SLOTS[slot])
                        if slot == COMBINE_SLOT and not first:
                            rank_experts(b - 1, st)
                            weigh_experts(b - 1, st)

                all_batches(v, body)
                evacuate(NB - 1, 3)

            @block.tensor
            def _(pe):
                aux_step = tensor_steps(pe)

                def head_of(q, g):
                    return 4 * (q // 16) + g, (q // 8) % 2, q % 8

                def scores(b, q):
                    for g in range(4):
                        k = 2 * q + g // 2
                        if g % 2 == 0:
                            if last_use(k) >= 0 or later(b):
                                pe.wait_ge(exped, BLOCKS * b + last_use(k) + 1)
                        h, ih, jt = head_of(q, g)
                        last = pe.matmul(score_buf(buf_of(k))[:, (g % 2) * BANK:(g % 2 + 1) * BANK],
                                         KA[0:SCORE_ROWS, h, jt * P:(jt + 1) * P],
                                         QA[0:SCORE_ROWS, h, ih * BANK:(ih + 1) * BANK], start=True, stop=True)
                        if g % 2:
                            last.then_inc(scored, 1)

                def values(b, q):
                    pe.wait_ge(exped, BLOCKS * b + 2 * q + 2)
                    if q % 8 == 0 and (later(b) or q):
                        pe.wait_ge(o_evacuated, GROUPS * b + q // 8)
                    if q % 16 == 0:
                        pe.wait_ge(va_ready, 2 * b + q // 16 + 1)
                    for g in range(4):
                        k = 2 * q + g // 2
                        h, ih, jt = head_of(q, g)
                        last = pe.matmul(o_acc[32 * g:32 * g + 32, :], VA[:, jt, h, :],
                                         probs[:, k % PROB_BUFS, (g % 2) * BANK:(g % 2 + 1) * BANK],
                                         start=(jt == 0), stop=(jt == NCH - 1))
                    last.then_inc(pv_done, 1)

                def fallback(b, hg, flag):
                    base = 2 * b + hg
                    with pe.If(flag != 0):
                        if later(b) or hg:
                            pe.wait_ge(exped, BLOCKS * b + BLOCKS // 2 * hg)
                        for u in range(FB_UNITS):
                            if u >= 2:
                                pe.wait_ge(fb_maxed, FB_MAXED * base + u - 1)
                            h, c = 4 * hg + u // NCH, u % NCH
                            for n in range(2):
                                last = pe.matmul(score_buf(u % 2)[:, n * BANK:(n + 1) * BANK],
                                                 QA[0:SHIFT_ROW, h, c * P:(c + 1) * P],
                                                 KA[0:SHIFT_ROW, h, n * BANK:(n + 1) * BANK], start=True, stop=True)
                            last.then_inc(fb_scored, 1)
                        pe.wait_ge(fb_maxed, FB_MAXED * base + FB_UNITS)
                        pe.transpose(psum[0:FB_UNITS, 4 * BANK:4 * BANK + P], fb_max[:, :],
                                     ident[:, :]).then_inc(fb_scored, 1)
                    with pe.Else():
                        pe.sem_inc(fb_scored, FB_SCORED)
                    pe.wait_ge(fb_moved, FB_MOVED * (base + 1))

                def body(b, first, last):
                    pe.wait_ge(flag_ready, b + 1)
                    flag = pe.value_load(flags[0:1, ds(b, 1)], min_val=0, max_val=1)
                    order = aux_order(not last, not first)
                    for q in range(QUADS):
                        if q % 16 == 0:
                            pe.wait_ge(aug_loaded[q // 16], 16 * AUG_DMAS * (b + 1))
                            fallback(b, q // 16, flag)
                        scores(b, q)
                        for step in steps_of(q, not last, not first):
                            i = order.index(step)
                            aux_step(step, b + 1 if step in PREP else b - 1, aux_base(b) + i + 1, aux_base(b) + i)
                        if q >= LAG:
                            values(b, q - LAG)
                        elif not first:
                            values(b - 1, QUADS + q - LAG)

                all_batches(pe, body)
                for q in range(QUADS - LAG, QUADS):
                    values(NB - 1, q)

        inner.close()

        def sb(name, shape, dt):
            return ctx.enter_context(nc.sbuf_tensor(name, shape, dt))

        m_x2 = sb("m_x2", [P, 2, 2, T], BF16)
        m_cT = sb("m_cT", [PARTS * KC, 2, T], BF16)
        act_h = sb("act_h", [P, 2, BANK], F32)
        gated = sb("gated", [P, PAIRS, BANK], F32)
        yT = sb("yT", [P, 2, BANK], F32)
        result = sb("result", [P, 2, NCH, D], F32)
        hid = [psum[:, i * BANK:(i + 1) * BANK] for i in range(2)]
        wgt = [psum[:, (2 + i) * BANK:(3 + i) * BANK] for i in range(2)]
        ysum = [psum[:, (4 + i) * BANK:(5 + i) * BANK] for i in range(2)]
        ybank = psum[:, 6 * BANK:7 * BANK].rearrange("p (c t e) -> p c t e", c=4, t=2)

        tokens = [sem(f"m_tokens_{i}") for i in range(2)]
        hidden = sem("m_hidden")
        weights = sem("m_weights")
        gelued = sem("m_gelued")
        gated_ready = sem("m_gated")
        summed = sem("m_summed")
        yT_moved = sem("m_yT_moved")
        y_ready = sem("m_y")
        half_taken = sem("m_half_taken")
        y_taken = sem("m_y_taken")
        stored = [sem(f"m_stored_{i}") for i in range(2)]

        TOKEN_LOADS = 16 * (3 + PARTS)
        BODY = 2 * UNITS

        END = aux_base(NB) - len(PREP)

        with nc.Block() as block:
            @block.sync
            def _(sp):
                _, _, store_x2, _, _, _ = sync_steps(sp)

                def load_tokens(b, s):
                    def of(d):
                        return d[ds(b, 1), :, :].rearrange("o d t -> (o d) t")

                    sp.dma_start(m_x2[:, s, 0, :], of(x2_d)).then_inc(tokens[s], 16)
                    sp.dma_start(m_x2[0:D, s, 1, :], of(x2_low_d)).then_inc(tokens[s], 16)
                    sp.dma_start(m_x2[D:P, s, 1, :], of(x2_d)[0:D, :]).then_inc(tokens[s], 16)
                    for a in range(PARTS):
                        sp.dma_start(m_cT[a * KC:(a + 1) * KC, s, :], of(cT_d)).then_inc(tokens[s], 16)

                def store(pair, s):
                    sp.wait_ge(y_taken, 4 * pair + 2 * s + 2)
                    sp.dma_start(out[ds(pair * 2 + s, 1), :, :].rearrange("o (c p) e -> p (o c) e", p=P),
                                 result[:, s, :, :]).then_inc(stored[s], 16)

                def body_sp(pair, first, last):
                    for s in range(2):
                        if not last:
                            sp.wait_ge(y_ready, 4 * pair + 2 * s + 2)
                            load_tokens(pair * 2 + 2 + s, s)
                        store(pair, s)

                for s in range(2):
                    load_tokens(s, s)
                sp.wait_ge(aux_drained, END + POST.index("post_t1") + 1)
                store_x2(NB - 1)
                body_sp(0, True, False)
                sp.wait_ge(aux_drained, END + POST.index("combine_t") + 1)
                sp.dma_start(cT_d[NB - 1, :, :], cT[:, :]).then_inc(cT_stored, 16)
                sp.wait_ge(x2_stored, 32 * NB)
                sp.wait_ge(cT_stored, 16 * NB)
                with sp.Fori(1, NB // 2 - 1) as pair:
                    body_sp(pair, False, False)
                body_sp(NB // 2 - 1, False, True)
                for s in range(2):
                    sp.wait_ge(stored[s], 8 * NB)

            @block.gpsimd
            def _(g):
                g.wait_ge(p_var_ready, NB)
                g.tensor_tensor(p_rstd[:, :], p_ve[:, :], neg_half[:, :], ALU.pow).then_inc(p_rstd_ready, 1)

            @block.scalar
            def _(act):
                def body(pair, first):
                    for i in range(BODY):
                        act.wait_ge(hidden, BODY * pair + i + 1)
                        if i >= 2 or not first:
                            act.wait_ge(gated_ready, BODY * pair + i - 1)
                        nc.scalar.activation(act_h[:, i % 2, :], hid[i % 2], ACT.Gelu,
                                             bias=b1[:, i % PAIRS:i % PAIRS + 1]).then_inc(gelued, 1)
                        if first and i == ROUTER_UNIT:
                            act.wait_ge(aux_drained, END + POST.index("router") + 1)
                            nc.scalar.activation(router_e[:, :, :], logits[:, :, :], ACT.Exp).then_inc(router_exped, 1)

                act.wait_ge(experts_loaded, 16 * EXPERT_LOADS)
                body(0, True)
                with act.Fori(1, NB // 2) as pair:
                    body(pair, False)

            @block.vector
            def _(v):
                post_step, rank_experts, weigh_experts = vector_post(v)
                st = {}

                def move(pair, half, first):
                    v.wait_ge(summed, 2 * (4 * pair + half) + 2)
                    if not first or half >= 2:
                        v.wait_ge(y_ready, 4 * pair + half - 1)
                    v.tensor_copy(yT[:, half % 2, :], ysum[half % 2]).then_inc(yT_moved, 1)

                def take(pair, half, first):
                    s, hh = (half % 4) // 2, half % 2
                    v.wait_ge(y_ready, 4 * pair + half + 1)
                    if hh == 0 and not first:
                        v.wait_ge(stored[s], 16 * pair)
                    rows = H_all[:, ds((pair * 2) * NCH + 4 * half, 4), :]
                    mine = result[:, s, 4 * hh:4 * hh + 4, :]
                    v.tensor_tensor(mine, ybank[:, :, 0, :], rows, ALU.add).then_inc(half_taken, 1)
                    v.wait_ge(half_taken, 4 * pair + half + 1)
                    v.tensor_tensor(mine, ybank[:, :, 1, :], mine, ALU.add).then_inc(y_taken, 1)

                def body(pair, first):
                    for i in range(BODY):
                        half = i // PAIRS - 1
                        if first and i == RANK_UNIT:
                            rank_experts(NB - 1, st)
                        if first and i == WEIGH_UNIT:
                            weigh_experts(NB - 1, st)
                        if first and i in POST_UNITS:
                            step = POST_UNITS[i]
                            post_step(step, NB - 1, END + POST.index(step) + 1, st)
                        if i % PAIRS == 2 and (half >= 0 or not first):
                            move(pair, half, first)
                        v.wait_ge(gelued, BODY * pair + i + 1)
                        v.wait_ge(weights, BODY * pair + i + 1)
                        if i >= PAIRS or not first:
                            v.wait_ge(summed, BODY // 2 * pair + (i - PAIRS) // 2 + 1)
                        v.tensor_tensor(gated[:, i % PAIRS, :], act_h[:, i % 2, :], wgt[i % 2],
                                        ALU.mult).then_inc(gated_ready, 1)
                        if i % PAIRS == 3 and (half >= 0 or not first):
                            take(pair, half, first)

                body(0, True)
                with v.Fori(1, NB // 2) as pair:
                    body(pair, False)
                move(NB // 2 - 1, 3, False)
                take(NB // 2 - 1, 3, False)

            @block.tensor
            def _(pe):
                aux_step = tensor_steps(pe)
                pe.wait_ge(experts_loaded, 16 * EXPERT_LOADS)

                def sum_two(pair, i, first):
                    half = i // PAIRS
                    pe.wait_ge(gated_ready, BODY * pair + i + 2)
                    if i % PAIRS == 0 and (half >= 2 or not first):
                        pe.wait_ge(yT_moved, 4 * pair + half - 1)
                    for n in range(2):
                        m = i % PAIRS + n
                        last = pe.matmul(ysum[half % 2][n * D:(n + 1) * D, :], w2[:, m, :], gated[:, m, :],
                                         start=(m < 2), stop=(m >= 2))
                    if i % PAIRS == 0:
                        s, cols = (half % 4) // 2, slice((half % 2) * BANK, (half % 2 + 1) * BANK)
                        last = pe.matmul(ysum[half % 2][0:D, :], b2_rows[:, :], m_cT[:, s, cols],
                                         start=False, stop=False)
                    last.then_inc(summed, 1)

                def by_token(pair, half):
                    pe.wait_ge(yT_moved, 4 * pair + half + 1)
                    for c in range(4):
                        last = pe.transpose(ybank[:, c, :, :].rearrange("p t e -> p (t e)"),
                                            yT[:, half % 2, c * P:(c + 1) * P], ident[:, :])
                    last.then_inc(y_ready, 1)

                def body(pair, first):
                    for i in range(BODY):
                        half, m = i // PAIRS, i % PAIRS
                        s, cols = half // 2, slice((half % 2) * BANK, (half % 2 + 1) * BANK)
                        if first and i in POST_UNITS:
                            n = END + POST.index(POST_UNITS[i])
                            aux_step(POST_UNITS[i], NB - 1, n + 1, n)
                        if i % UNITS == 0:
                            pe.wait_ge(tokens[s], TOKEN_LOADS * pair + TOKEN_LOADS)
                        if i >= 2 or not first:
                            pe.wait_ge(gelued, BODY * pair + i - 1)
                        for turn, stack in TURNS:
                            last = pe.matmul(hid[i % 2], w_parts[:, turn, W1_COL + m * P:W1_COL + (m + 1) * P],
                                             m_x2[:, s, stack, cols], start=(turn == 0), stop=(turn == 2))
                        last.then_inc(hidden, 1)
                        if i >= 2 or not first:
                            pe.wait_ge(gated_ready, BODY * pair + i - 1)
                        pe.matmul(wgt[i % 2], spread[:, m, :], m_cT[0:KC, s, cols],
                                  start=True, stop=True).then_inc(weights, 1)
                        if m == 3 and (half >= 1 or not first):
                            if half >= 2 or not first:
                                pe.wait_ge(y_taken, 4 * pair + half - 1)
                            by_token(pair, half - 1)
                        if i % 2 and (i >= 3 or not first):
                            sum_two(pair, i - 3, first)

                body(0, True)
                with pe.Fori(1, NB // 2) as pair:
                    body(pair, False)
                sum_two(NB // 2 - 1, BODY - 2, False)
                pe.wait_ge(y_taken, 2 * NB - 1)
                by_token(NB // 2 - 1, 3)


def vit_tower(nc, xT, tok_WT, tok_b, pos, tgt, edge_attr, Wq, bq, Wk, bk, Wv, bv, Wo, bo, We, be, router_wT,
              w1, b1, w2, b2, out):
    io = dict(xT=xT, tok_WT=tok_WT, tok_b=tok_b, pos=pos, tgt=tgt, edge_attr=edge_attr, Wq=Wq, bq=bq, Wk=Wk, bk=bk,
              Wv=Wv, bv=bv, Wo=Wo, bo=bo, We=We, be=be, router_wT=router_wT, w1=w1, b1=b1, w2=w2, b2=b2)

    def dram(name, shape, dt):
        return nc.dram_tensor(name, shape, dt, kind="Internal").ap()

    scratch = dict(bparts=dram("bparts_d", [PARTS, H, T], BF16), q_parts=dram("q_parts_d", [2, PARTS, 32, T], BF16),
                   k_parts=dram("k_parts_d", [2, 2 * PARTS - 1, 32, T], BF16),
                   shift=dram("shift_d", [PARTS, H, T], BF16), fb=dram("fb_d", [PARTS, FB_UNITS, P], BF16),
                   x2=dram("x2_d", [NB, P, T], BF16), x2_low=dram("x2_low_d", [NB, D, T], BF16),
                   cT=dram("cT_d", [NB, PARTS * NX, T], BF16))
    with ExitStack() as ctx:
        def sb(name, shape, dt):
            return ctx.enter_context(nc.sbuf_tensor(name, shape, dt))

        psum = ctx.enter_context(nc.psum_tensor("psum", [P, 8 * BANK], F32))
        pool = dict(H_all=sb("H_all", [P, NB * NCH, D], F32), ident=sb("ident", [P, P], F32),
                    ident_bf=sb("ident_bf", [P, P], BF16), bmax=sb("bmax", [H, 1], F32))
        attention(nc, pool, io, psum, scratch, out)


def kernel(x, L0_tok_W, L0_tok_b, L0_tok_pos_embed, L0_attn_edge_index, L0_attn_edge_attr, L0_attn_Wq, L0_attn_bq,
           L0_attn_Wk, L0_attn_bk, L0_attn_Wv, L0_attn_bv, L0_attn_Wo, L0_attn_bo, L0_attn_We, L0_attn_be,
           L0_ffn_router_w, L0_ffn_w1, L0_ffn_b1, L0_ffn_w2, L0_ffn_b2):
    import numpy as np
    import concourse.bacc as bacc
    from concourse.bass_utils import run_bass_kernel_spmd

    def laid(a):
        return np.ascontiguousarray(a)

    def by_dim(w):
        w = np.asarray(w)
        return laid(w.reshape(w.shape[:-1] + (2, 4, HD)).swapaxes(-1, -2).reshape(w.shape))

    x = np.asarray(x)
    side = HD
    mp, fp = x.shape[2] // side, x.shape[3] // side
    patches = x[:, 0].reshape(NB, mp, side, fp, side).transpose(0, 2, 4, 1, 3).reshape(NB, D, T)
    w1 = np.asarray(L0_ffn_w1)
    arrays = dict(
        xT=laid(patches), tok_WT=laid(np.asarray(L0_tok_W).T), tok_b=laid(L0_tok_b),
        pos=laid(np.asarray(L0_tok_pos_embed).reshape(NCH, P, D).transpose(1, 0, 2)),
        tgt=laid(np.asarray(L0_attn_edge_index)[1].reshape(EC, P).T), edge_attr=laid(L0_attn_edge_attr),
        Wq=by_dim(L0_attn_Wq), bq=by_dim(L0_attn_bq), Wk=by_dim(L0_attn_Wk), bk=by_dim(L0_attn_bk),
        Wv=laid(L0_attn_Wv), bv=laid(L0_attn_bv), Wo=laid(L0_attn_Wo), bo=laid(L0_attn_bo),
        We=laid(L0_attn_We), be=laid(L0_attn_be), router_wT=laid(np.asarray(L0_ffn_router_w).T),
        w1=laid(w1.transpose(1, 0, 2).reshape(D, NX * D)),
        b1=laid(np.asarray(L0_ffn_b1).reshape(NX // 2, P).T),
        w2=laid(np.asarray(L0_ffn_w2).reshape(NX // 2, P, D).transpose(1, 0, 2)), b2=laid(L0_ffn_b2))
    nc = bacc.Bacc("TRN2", target_bir_lowering=False, num_devices=1)
    args = {n: nc.dram_tensor(f"in_{n}", a.shape, mybir.dt.from_np(a.dtype), kind="ExternalInput").ap()
            for n, a in arrays.items()}
    out = nc.dram_tensor("out_h", (NB, T, D), F32, kind="ExternalOutput").ap()
    vit_tower(nc, **args, out=out)
    r = run_bass_kernel_spmd(nc, [{f"in_{n}": a for n, a in arrays.items()}], core_ids=[0])
    return r.results[0]["out_h"]
```
